# Optimizing a Trainium2 kernel written in Bass

```python
import numpy as np
import jax
import jax.numpy as jnp

def _softmax(x, axis=-1):
    return jax.nn.softmax(x, axis=axis)

def _gelu(x):
    return jax.nn.gelu(x, approximate=True)

def _silu(x):
    return jax.nn.silu(x)

def _sigmoid(x):
    return jax.nn.sigmoid(x)

def _layernorm(x, axis=-1, eps=1e-05):
    m = jnp.mean(x, axis=axis, keepdims=True)
    v = jnp.var(x, axis=axis, keepdims=True)
    return (x - m) / jnp.sqrt(v + eps)

def _scatter_add(tgt, idx, src, axis=0):
    return tgt.at[idx].add(src)

def _segment_sum(src, seg, n):
    return jax.ops.segment_sum(src, seg, n)
kernel_name = 'mk_decoder_postln_d2_seqx_r8_708a22'

def setup_inputs(seed: int=0):
    np.random.seed(seed)
    _w = jnp.asarray

    def _rec_inputs():
        import jax
        import jax.numpy as jnp
        _rk = jax.random.key(seed)
        x = 7.22e-05 + 1 * jax.random.normal(jax.random.fold_in(_rk, 1), (32, 128, 128), jnp.float32)
        _lenS = 128 - jax.random.randint(jax.random.fold_in(_rk, 7), (32,), 0, max(1, 128 // 4) + 1, jnp.int32)
        _lenS2 = 128 - jax.random.randint(jax.random.fold_in(_rk, 8), (32,), 0, max(1, 128 // 4) + 1, jnp.int32)
        _ctx_1024P = jax.random.normal(jax.random.fold_in(_rk, 11), (32, 16, 128), jnp.float32)
        _ctx_1024c = jax.random.dirichlet(jax.random.fold_in(_rk, 511), 0.3 * jnp.ones((16,), jnp.float32), (32, 128))
        _ctx_1024t = jnp.einsum('bsk,bkd->bsd', _ctx_1024c, _ctx_1024P)
        _ctx_1024t = _ctx_1024t * jax.lax.rsqrt(jnp.mean(jnp.square(_ctx_1024t)) + 1e-12) * 0.953939
        ctx_1024 = -1.52775e-05 + 0.999936 * (_ctx_1024t + 0.3 * jax.random.normal(jax.random.fold_in(_rk, 611), (32, 128, 128), jnp.float32))
        _validS = jnp.arange(128)[None, :] < _lenS[:, None]
        _validS2 = jnp.arange(128)[None, :] < _lenS2[:, None]
        _causal = jnp.tril(jnp.ones((128, 128), dtype=bool))
        mask_BxS2_bk0 = jnp.logical_not(jnp.broadcast_to(_validS2[:, :], (32, 128)))
        return (x, ctx_1024, mask_BxS2_bk0)
    x, ctx_1024, mask_BxS2_bk0 = _rec_inputs()

    def _L0_attn_setup():
        import jax, jax.numpy as jnp
        import numpy as np
        D_MODEL = 128
        D_STATE = 128
        HEAD_DIM = 64
        EXPAND = 2
        K = 4
        N_GROUPS = 1
        D_INNER = EXPAND * D_MODEL
        N_HEADS = D_INNER // HEAD_DIM
        D_PROJ = 2 * D_INNER + 2 * N_GROUPS * D_STATE + N_HEADS
        EPS = 1e-06

        def _rmsnorm(x, w):
            return x * jax.lax.rsqrt(jnp.mean(x * x, axis=-1, keepdims=True) + EPS) * w
        key = jax.random.key(seed)
        ks = jax.random.split(key, 8)
        B, L = (2, 256)
        x = jax.random.normal(ks[0], (B, L, D_MODEL), jnp.float32)
        norm_w = jnp.ones((D_MODEL,), jnp.float32)
        in_proj_w = jax.random.normal(ks[1], (D_PROJ, D_MODEL), jnp.float32) / np.sqrt(D_MODEL).astype(np.float32)
        conv_w = jax.random.normal(ks[2], (D_INNER, K), jnp.float32) / np.sqrt(K).astype(np.float32)
        conv_b = jnp.zeros((D_INNER,), jnp.float32)
        A_log = jnp.log(jax.random.uniform(ks[3], (N_HEADS,), jnp.float32) * 15.0 + 1.0)
        D = jnp.ones((N_HEADS,), jnp.float32)
        dt_bias = jnp.log(jax.random.uniform(ks[4], (N_HEADS,), jnp.float32) * 0.099 + 0.001)
        out_proj_w = jax.random.normal(ks[5], (D_MODEL, D_INNER), jnp.float32) / np.sqrt(D_INNER).astype(np.float32)
        return dict(x=x, norm_w=norm_w, in_proj_w=in_proj_w, conv_w=conv_w, conv_b=conv_b, A_log=A_log, D=D, dt_bias=dt_bias, out_proj_w=out_proj_w)
    _L0_attn_all = _L0_attn_setup()
    _L0_attn_in = {k: v for k, v in _L0_attn_all.items() if k in ('norm_w', 'in_proj_w', 'conv_w', 'conv_b', 'A_log', 'D', 'dt_bias', 'out_proj_w')}
    del _L0_attn_all

    def _L0_xattn_setup():
        import jax, jax.numpy as jnp
        import numpy as np
        D_MODEL = 128
        N_HEADS = 1
        HEAD_DIM = D_MODEL // N_HEADS
        N, LEN_Q, LEN_IN = (8, 128, 512)
        key = jax.random.key(seed)
        ks = jax.random.split(key, 7)
        s = 1.0 / np.sqrt(D_MODEL)
        return {'query': jax.random.normal(ks[0], (N, LEN_Q, D_MODEL), dtype=jnp.float32), 'input_flatten': jax.random.normal(ks[1], (N, LEN_IN, D_MODEL), dtype=jnp.float32), 'input_padding_mask': jax.random.randint(ks[2], (N, LEN_IN), 0, 2).astype(bool), 'Wq': jax.random.normal(ks[3], (D_MODEL, D_MODEL), dtype=jnp.float32) * s, 'bq': jnp.zeros((D_MODEL,), dtype=jnp.float32), 'Wk': jax.random.normal(ks[4], (D_MODEL, D_MODEL), dtype=jnp.float32) * s, 'bk': jnp.zeros((D_MODEL,), dtype=jnp.float32), 'Wo': jax.random.normal(ks[5], (D_MODEL, D_MODEL), dtype=jnp.float32) * s, 'bo': jnp.zeros((D_MODEL,), dtype=jnp.float32)}
    _L0_xattn_all = _L0_xattn_setup()
    _L0_xattn_in = {k: v for k, v in _L0_xattn_all.items() if k in ('Wq', 'bq', 'Wk', 'bk', 'Wo', 'bo')}
    del _L0_xattn_all

    def _L0_ffn_setup():
        import jax, jax.numpy as jnp
        import numpy as np
        N, T, D = (4, 512, 128)
        NUM_EXPERTS = 8
        EXPERT_CAP = 2.0
        MLP_RATIO = 4
        HIDDEN = MLP_RATIO * D
        key = jax.random.key(seed)
        k1, k2, k3, k4 = jax.random.split(key, 4)
        x = jax.random.normal(k1, (N, T, D), dtype=jnp.float32)
        gate_w = jax.random.truncated_normal(k2, -2.0, 2.0, (D, NUM_EXPERTS), dtype=jnp.float32) * 0.02
        w1 = jax.random.normal(k3, (NUM_EXPERTS, D, HIDDEN), dtype=jnp.float32) * 0.02
        w2 = jax.random.normal(k4, (NUM_EXPERTS, HIDDEN, D), dtype=jnp.float32) * 0.02
        return {'x': x, 'gate_w': gate_w, 'w1': w1, 'w2': w2}
    _L0_ffn_all = _L0_ffn_setup()
    _L0_ffn_in = {k: v for k, v in _L0_ffn_all.items() if k in ('gate_w', 'w1', 'w2')}
    del _L0_ffn_all

    def _L1_attn_setup():
        import jax, jax.numpy as jnp
        import numpy as np
        DIM = 128
        HEADS = 16
        DHEAD = DIM // HEADS
        key = jax.random.key(seed)
        k1, k2, k3, k4 = jax.random.split(key, 4)
        B, N = (4, 512)
        x = jax.random.normal(k1, (B, N, DIM), dtype=jnp.float32)
        s = 1.0 / np.sqrt(DIM)
        W_qkv = jax.random.uniform(k2, (DIM, 3 * DIM), jnp.float32, -s, s)
        W_out = jax.random.uniform(k3, (DIM, DIM), jnp.float32, -s, s)
        b_out = jax.random.uniform(k4, (DIM,), jnp.float32, -s, s)
        return {'x': x, 'W_qkv': W_qkv, 'W_out': W_out, 'b_out': b_out}
    _L1_attn_all = _L1_attn_setup()
    _L1_attn_in = {k: v for k, v in _L1_attn_all.items() if k in ('W_qkv', 'W_out', 'b_out')}
    del _L1_attn_all

    def _L1_xattn_setup():
        import jax, jax.numpy as jnp
        import numpy as np
        EMBED_DIM = 128
        NUM_HEADS = 16
        HEAD_DIM = EMBED_DIM // NUM_HEADS
        B, T_Q, T_K = (2, 256, 256)
        key = jax.random.key(seed)
        ks = jax.random.split(key, 11)
        s = 1.0 / np.sqrt(EMBED_DIM)
        return {'query': jax.random.normal(ks[0], (B, T_Q, EMBED_DIM), jnp.float32), 'key': jax.random.normal(ks[1], (B, T_K, EMBED_DIM), jnp.float32), 'value': jax.random.normal(ks[2], (B, T_K, EMBED_DIM), jnp.float32), 'Wq': jax.random.normal(ks[3], (EMBED_DIM, EMBED_DIM), jnp.float32) * s, 'bq': jnp.zeros((EMBED_DIM,), jnp.float32), 'Wk': jax.random.normal(ks[4], (EMBED_DIM, EMBED_DIM), jnp.float32) * s, 'bk': jnp.zeros((EMBED_DIM,), jnp.float32), 'Wv': jax.random.normal(ks[5], (EMBED_DIM, EMBED_DIM), jnp.float32) * s, 'bv': jnp.zeros((EMBED_DIM,), jnp.float32), 'Wo': jax.random.normal(ks[6], (EMBED_DIM, EMBED_DIM), jnp.float32) * s, 'bo': jnp.zeros((EMBED_DIM,), jnp.float32)}
    _L1_xattn_all = _L1_xattn_setup()
    _L1_xattn_in = {k: v for k, v in _L1_xattn_all.items() if k in ('Wq', 'bq', 'Wk', 'bk', 'Wv', 'bv', 'Wo', 'bo')}
    del _L1_xattn_all

    def _L1_ffn_setup():
        import jax, jax.numpy as jnp
        import numpy as np
        DIM = 128
        NUM_EXPERTS = 6
        TOP_K = 2
        HIDDEN = DIM * 2
        key = jax.random.key(seed)
        ks = jax.random.split(key, 7)
        s_in = 1.0 / np.sqrt(DIM)
        s_h = 1.0 / np.sqrt(HIDDEN)
        x = jax.random.normal(ks[0], (4, 256, DIM), dtype=jnp.float32)
        Wg = jax.random.uniform(ks[1], (DIM, NUM_EXPERTS), jnp.float32, -s_in, s_in)
        bg = jax.random.uniform(ks[2], (NUM_EXPERTS,), jnp.float32, -s_in, s_in)
        W1 = jax.random.uniform(ks[3], (NUM_EXPERTS, DIM, HIDDEN), jnp.float32, -s_in, s_in)
        b1 = jax.random.uniform(ks[4], (NUM_EXPERTS, HIDDEN), jnp.float32, -s_in, s_in)
        W2 = jax.random.uniform(ks[5], (NUM_EXPERTS, HIDDEN, DIM), jnp.float32, -s_h, s_h)
        b2 = jax.random.uniform(ks[6], (NUM_EXPERTS, DIM), jnp.float32, -s_h, s_h)
        return {'x': x, 'Wg': Wg, 'bg': bg, 'W1': W1, 'b1': b1, 'W2': W2, 'b2': b2}
    _L1_ffn_all = _L1_ffn_setup()
    _L1_ffn_in = {k: v for k, v in _L1_ffn_all.items() if k in ('Wg', 'bg', 'W1', 'b1', 'W2', 'b2')}
    del _L1_ffn_all
    return {'x': x, 'ctx_1024': ctx_1024, 'mask_BxS2_bk0': mask_BxS2_bk0, 'L0_attn_norm_w': _L0_attn_in['norm_w'], 'L0_attn_in_proj_w': _L0_attn_in['in_proj_w'], 'L0_attn_conv_w': _L0_attn_in['conv_w'], 'L0_attn_conv_b': _L0_attn_in['conv_b'], 'L0_attn_A_log': _L0_attn_in['A_log'], 'L0_attn_D': _L0_attn_in['D'], 'L0_attn_dt_bias': _L0_attn_in['dt_bias'], 'L0_attn_out_proj_w': _L0_attn_in['out_proj_w'], 'L0_xattn_Wq': _L0_xattn_in['Wq'], 'L0_xattn_bq': _L0_xattn_in['bq'], 'L0_xattn_Wk': _L0_xattn_in['Wk'], 'L0_xattn_bk': _L0_xattn_in['bk'], 'L0_xattn_Wo': _L0_xattn_in['Wo'], 'L0_xattn_bo': _L0_xattn_in['bo'], 'L0_ffn_gate_w': _L0_ffn_in['gate_w'], 'L0_ffn_w1': _L0_ffn_in['w1'], 'L0_ffn_w2': _L0_ffn_in['w2'], 'L1_attn_W_qkv': _L1_attn_in['W_qkv'], 'L1_attn_W_out': _L1_attn_in['W_out'], 'L1_attn_b_out': _L1_attn_in['b_out'], 'L1_xattn_Wq': _L1_xattn_in['Wq'], 'L1_xattn_bq': _L1_xattn_in['bq'], 'L1_xattn_Wk': _L1_xattn_in['Wk'], 'L1_xattn_bk': _L1_xattn_in['bk'], 'L1_xattn_Wv': _L1_xattn_in['Wv'], 'L1_xattn_bv': _L1_xattn_in['bv'], 'L1_xattn_Wo': _L1_xattn_in['Wo'], 'L1_xattn_bo': _L1_xattn_in['bo'], 'L1_ffn_Wg': _L1_ffn_in['Wg'], 'L1_ffn_bg': _L1_ffn_in['bg'], 'L1_ffn_W1': _L1_ffn_in['W1'], 'L1_ffn_b1': _L1_ffn_in['b1'], 'L1_ffn_W2': _L1_ffn_in['W2'], 'L1_ffn_b2': _L1_ffn_in['b2']}

def reference(x, ctx_1024, mask_BxS2_bk0, L0_attn_norm_w, L0_attn_in_proj_w, L0_attn_conv_w, L0_attn_conv_b, L0_attn_A_log, L0_attn_D, L0_attn_dt_bias, L0_attn_out_proj_w, L0_xattn_Wq, L0_xattn_bq, L0_xattn_Wk, L0_xattn_bk, L0_xattn_Wo, L0_xattn_bo, L0_ffn_gate_w, L0_ffn_w1, L0_ffn_w2, L1_attn_W_qkv, L1_attn_W_out, L1_attn_b_out, L1_xattn_Wq, L1_xattn_bq, L1_xattn_Wk, L1_xattn_bk, L1_xattn_Wv, L1_xattn_bv, L1_xattn_Wo, L1_xattn_bo, L1_ffn_Wg, L1_ffn_bg, L1_ffn_W1, L1_ffn_b1, L1_ffn_W2, L1_ffn_b2):
    import jax
    import jax.numpy as jnp

    def _L0_attn_ref(x, norm_w, in_proj_w, conv_w, conv_b, A_log, D, dt_bias, out_proj_w):
        import jax, jax.numpy as jnp
        import numpy as np
        D_MODEL = 128
        D_STATE = 128
        HEAD_DIM = 64
        EXPAND = 2
        K = 4
        N_GROUPS = 1
        D_INNER = EXPAND * D_MODEL
        N_HEADS = D_INNER // HEAD_DIM
        D_PROJ = 2 * D_INNER + 2 * N_GROUPS * D_STATE + N_HEADS
        EPS = 1e-06

        def _rmsnorm(x, w):
            return x * jax.lax.rsqrt(jnp.mean(x * x, axis=-1, keepdims=True) + EPS) * w
        batch, L, _ = x.shape
        residual = x
        xn = _rmsnorm(x, norm_w)
        proj = jnp.einsum('bld,pd->blp', xn, in_proj_w)
        i = 0
        z = proj[:, :, i:i + D_INNER]
        i += D_INNER
        x_ssm = proj[:, :, i:i + D_INNER]
        i += D_INNER
        bc = N_GROUPS * D_STATE
        Bm = proj[:, :, i:i + bc].reshape(batch, L, N_GROUPS, D_STATE)
        i += bc
        Cm = proj[:, :, i:i + bc].reshape(batch, L, N_GROUPS, D_STATE)
        i += bc
        dt_raw = proj[:, :, i:i + N_HEADS]
        xp = jnp.pad(x_ssm, ((0, 0), (K - 1, 0), (0, 0)))
        x_conv = conv_b
        for k in range(K):
            x_conv = x_conv + xp[:, k:k + L, :] * conv_w[:, k]
        x_conv = jax.nn.silu(x_conv)
        xh = x_conv.reshape(batch, L, N_HEADS, HEAD_DIM)
        dt = jax.nn.softplus(dt_raw + dt_bias)
        dA = jnp.exp(-jnp.exp(A_log) * dt)
        dtx = dt[..., None] * xh
        gidx = jnp.arange(N_HEADS) // (N_HEADS // N_GROUPS)
        Bg = Bm[:, :, gidx, :]
        Cg = Cm[:, :, gidx, :]

        def step(h, inp):
            dA_t, dtx_t, B_t, C_t = inp
            h = h * dA_t[:, :, None, None] + dtx_t[..., None] * B_t[:, :, None, :]
            y_t = jnp.einsum('bhpn,bhn->bhp', h, C_t)
            return (h, y_t)
        h0 = jnp.zeros((batch, N_HEADS, HEAD_DIM, D_STATE), jnp.float32)
        xs = (jnp.swapaxes(dA, 0, 1), jnp.swapaxes(dtx, 0, 1), jnp.swapaxes(Bg, 0, 1), jnp.swapaxes(Cg, 0, 1))
        _, ys = jax.lax.scan(step, h0, xs)
        y = jnp.swapaxes(ys, 0, 1) + D[None, None, :, None] * xh
        y = y.reshape(batch, L, D_INNER) * jax.nn.silu(z)
        return residual + jnp.einsum('bli,di->bld', y, out_proj_w)

    def _L0_xattn_ref(query, input_flatten, input_padding_mask, Wq, bq, Wk, bk, Wo, bo):
        import jax, jax.numpy as jnp
        import numpy as np
        D_MODEL = 128
        N_HEADS = 1
        HEAD_DIM = D_MODEL // N_HEADS
        N, LEN_Q, LEN_IN = (8, 128, 512)
        n, len_q, _ = query.shape
        len_in = input_flatten.shape[1]
        Q = (query @ Wq.T + bq).reshape(n, len_q, N_HEADS, HEAD_DIM).transpose(0, 2, 1, 3)
        K = (input_flatten @ Wk.T + bk).reshape(n, len_in, N_HEADS, HEAD_DIM).transpose(0, 2, 1, 3)
        scores = jnp.einsum('nhqd,nhkd->nhqk', Q, K)
        scores = jnp.where(input_padding_mask[:, None, None, :], -jnp.inf, scores)
        attn = jax.nn.softmax(scores, axis=-1)
        V = jnp.broadcast_to(input_flatten[:, None], (n, N_HEADS, len_in, D_MODEL))
        out = jnp.einsum('nhql,nhld->nhqd', attn, V)
        out = out.transpose(0, 2, 1, 3).reshape(n, len_q, D_MODEL)
        return out @ Wo.T + bo

    def _L0_ffn_ref(x, gate_w, w1, w2):
        import jax, jax.numpy as jnp
        import numpy as np
        N, T, D = (4, 512, 128)
        NUM_EXPERTS = 8
        EXPERT_CAP = 2.0
        MLP_RATIO = 4
        HIDDEN = MLP_RATIO * D
        x = x.astype(jnp.float32)
        n, t, d = x.shape
        k = int(EXPERT_CAP * t / NUM_EXPERTS)
        scores = jnp.einsum('ntd,de->nte', x, gate_w)
        probs = jax.nn.softmax(scores, axis=-1)
        probs = jnp.transpose(probs, (0, 2, 1))
        g, m = jax.lax.top_k(probs, k)
        xin = jax.vmap(lambda xb, mb: xb[mb])(x, m)
        h = jax.nn.gelu(jnp.einsum('nekd,edf->nekf', xin, w1))
        h = jnp.einsum('nekf,efd->nekd', h, w2)
        weighted = g[..., None] * h
        flat_idx = (m + jnp.arange(n, dtype=m.dtype)[:, None, None] * t).reshape(-1)
        out = jnp.zeros((n * t, d), dtype=jnp.float32).at[flat_idx].add(weighted.reshape(-1, d))
        out = out.reshape(n, t, d)
        return out.astype(jnp.bfloat16)

    def _L1_attn_ref(x, W_qkv, W_out, b_out):
        import jax, jax.numpy as jnp
        import numpy as np
        DIM = 128
        HEADS = 16
        DHEAD = DIM // HEADS
        B, N, C = x.shape
        qkv = x @ W_qkv
        q, k, v = jnp.split(qkv, 3, axis=-1)
        resh = lambda t: t.reshape(B, N, HEADS, DHEAD).transpose(0, 2, 1, 3)
        q, k, v = (resh(q), resh(k), resh(v))
        q = jax.nn.elu(q) + 1.0
        k = jax.nn.elu(k) + 1.0
        kv = jnp.einsum('bhnd,bhne->bhde', k, v)
        z = k.sum(axis=2)
        numerator = jnp.einsum('bhnd,bhde->bhne', q, kv)
        denominator = jnp.einsum('bhnd,bhd->bhn', q, z)[..., None] + 1e-06
        out = numerator / denominator
        out = out.transpose(0, 2, 1, 3).reshape(B, N, C)
        return out @ W_out + b_out

    def _L1_xattn_ref(query, key, value, Wq, bq, Wk, bk, Wv, bv, Wo, bo):
        import jax, jax.numpy as jnp
        import numpy as np
        EMBED_DIM = 128
        NUM_HEADS = 16
        HEAD_DIM = EMBED_DIM // NUM_HEADS
        B, T_Q, T_K = (2, 256, 256)
        b, tq, _ = query.shape
        tk = key.shape[1]
        q = (query @ Wq.T + bq).reshape(b, tq, NUM_HEADS, HEAD_DIM).transpose(0, 2, 1, 3)
        k = (key @ Wk.T + bk).reshape(b, tk, NUM_HEADS, HEAD_DIM).transpose(0, 2, 1, 3)
        v = (value @ Wv.T + bv).reshape(b, tk, NUM_HEADS, HEAD_DIM).transpose(0, 2, 1, 3)
        scores = jnp.einsum('bhqd,bhkd->bhqk', q, k) / np.sqrt(HEAD_DIM)
        attn = jax.nn.softmax(scores, axis=-1)
        attn = jnp.nan_to_num(attn, nan=0.0)
        out = jnp.einsum('bhqk,bhkd->bhqd', attn, v)
        out = out.transpose(0, 2, 1, 3).reshape(b, tq, EMBED_DIM)
        return out @ Wo.T + bo

    def _L1_ffn_ref(x, Wg, bg, W1, b1, W2, b2):
        import jax, jax.numpy as jnp
        import numpy as np
        DIM = 128
        NUM_EXPERTS = 6
        TOP_K = 2
        HIDDEN = DIM * 2
        gate_logits = jnp.einsum('bsd,de->bse', x, Wg) + bg
        topk_w, topk_idx = jax.lax.top_k(gate_logits, TOP_K)
        topk_w = jax.nn.softmax(topk_w, axis=-1)
        combine = jnp.sum(jax.nn.one_hot(topk_idx, NUM_EXPERTS, dtype=x.dtype) * topk_w[..., None], axis=-2)
        h = jnp.einsum('bsd,edh->ebsh', x, W1) + b1[:, None, None, :]
        h = jax.nn.gelu(h, approximate=False)
        y = jnp.einsum('ebsh,ehd->ebsd', h, W2) + b2[:, None, None, :]
        out = jnp.einsum('ebsd,bse->bsd', y, combine)
        return out
    x = _layernorm(x + _L0_attn_ref(x, L0_attn_norm_w, L0_attn_in_proj_w, L0_attn_conv_w, L0_attn_conv_b, L0_attn_A_log, L0_attn_D, L0_attn_dt_bias, L0_attn_out_proj_w), axis=-1)
    x = _layernorm(x + _L0_xattn_ref(x, ctx_1024, mask_BxS2_bk0, L0_xattn_Wq, L0_xattn_bq, L0_xattn_Wk, L0_xattn_bk, L0_xattn_Wo, L0_xattn_bo), axis=-1)
    x = _layernorm(x + _L0_ffn_ref(x, L0_ffn_gate_w, L0_ffn_w1, L0_ffn_w2), axis=-1)
    x = _layernorm(x + _L1_attn_ref(x, L1_attn_W_qkv, L1_attn_W_out, L1_attn_b_out), axis=-1)
    x = _layernorm(x + _L1_xattn_ref(x, ctx_1024, ctx_1024, L1_xattn_Wq, L1_xattn_bq, L1_xattn_Wk, L1_xattn_bk, L1_xattn_Wv, L1_xattn_bv, L1_xattn_Wo, L1_xattn_bo), axis=-1)
    x = _layernorm(x + _L1_ffn_ref(x, L1_ffn_Wg, L1_ffn_bg, L1_ffn_W1, L1_ffn_b1, L1_ffn_W2, L1_ffn_b2), axis=-1)
    return x

_drawn_inputs = setup_inputs


def setup_inputs(seed=0):
    import zlib

    import numpy as np

    out = dict(_drawn_inputs(seed))
    spreads = {'L0_attn_norm_w': (1.0, 0.2),
     'L0_attn_conv_b': (0.0, 0.1),
     'L0_attn_D': (1.0, 0.2),
     'L0_xattn_bq': (0.0, 0.1),
     'L0_xattn_bk': (0.0, 0.8),
     'L0_xattn_bo': (0.0, 0.1),
     'L1_xattn_bq': (0.0, 0.314),
     'L1_xattn_bk': (0.0, 0.8),
     'L1_xattn_bv': (0.0, 0.1),
     'L1_xattn_bo': (0.0, 0.1)}
    factors = {'L0_ffn_gate_w': 4.373, 'L0_ffn_w1': 4.001, 'L0_ffn_w2': 3.911, 'L1_ffn_b1': 4.421}
    for name, (base, spread) in spreads.items():
        noise = np.random.default_rng([zlib.crc32(name.encode()), seed]).standard_normal(out[name].shape)
        drawn = base * np.exp(spread * noise) if base else spread * noise
        out[name] = jnp.asarray(drawn.astype(out[name].dtype))
    for name, factor in factors.items():
        out[name] = (out[name] * factor).astype(out[name].dtype)
    return out
```

```python
from contextlib import ExitStack

import concourse.bass as bass
from concourse import mybir

ALU = mybir.AluOpType
ACT = mybir.ActivationFunctionType
AX = mybir.AxisListType
F32 = mybir.dt.float32
BF16 = mybir.dt.bfloat16
U8 = mybir.dt.uint8
U32 = mybir.dt.uint32

P = 128
GB = 4
W = GB * P
LANES = 2
HS, PD = 4, 64
NE0, HID0, CAP = 8, 512, 32
FT0 = HID0 // P
NH, HD = 16, 8
NE1, HID1 = 6, 256
FT1 = HID1 // P
SLOTS = 6
KROWS = SLOTS * HD
SHIFT0 = 2 * KROWS
SROWS = SHIFT0 + 4
MASKED = -1e30
LN_EPS, RMS_EPS, DEN_EPS = 1e-5, 1e-6, 1e-6
TINY = 2.0 ** -26
N_CONSTANTS = 10

SEQUENCES = {
    "mamba_pe": "m_xt m_xs0 m_xs1 m_b m_c m_dtt m_gram m_dt m_z0 m_z1 m_xhr0 m_xhr1 m_out",
    "mamba_act": "m_xt_sb m_b_sb m_c_sb m_dtt_sb m_tanh0 m_tanh1 m_dt_exp m_dt_ln m_tz0 m_tz1",
    "mamba_dve": "m_stats m_moments m_sq m_ms m_norm m_tap00 m_tap01 m_tap02 m_tap03 m_tap10 m_tap11 m_tap12 m_tap13"
                 " m_xh0 m_xh1 m_gram_sb m_dt_sb m_dt_abs m_dt_one m_dt_den m_dt_rec m_dt_ratio m_dt_log1p m_dt_done"
                 " m_decay m_half m_sz0 m_sz1 m_dtx0 m_dtx1 m_skip0 m_skip1 m_gate0 m_gate1",
    "norm_dve": " ".join(f"n{n}_res n{n}_stats n{n}_mom n{n}_eps n{n}_done" for n in range(6)),
    "norm_pool": "m_rstd n0_rstd n1_rstd n2_rstd n3_rstd n4_rstd n5_rstd",
    "cross_pe": "c_kt c_xt c_q c_scores c_pt c_ot c_out",
    "cross_act": "c_kt_sb c_xt_sb c_q_sb c_exp c_ot_sb",
    "cross_dve": "c_mask c_max c_rsum c_pt_sb",
    "resid_pool": "m_twice c_resid l_resid x_resid",
    "choice_pe": "f_xt f_gt f_g f_pt f_bc f_rows f_xi f_down0 f_down1 f_add",
    "choice_act": "f_xt_sb f_gt_sb f_gexp f_xi_sb1 f_y_sb0 f_y_sb1 f_add_sb",
    "choice_dve": "f_gmax f_gsub f_gsum f_grec f_prob f_pt_sb"
                  + "".join(f" f_topv{r} f_topi{r} f_topw{r}" for r in range(CAP // 8)) + " f_idx f_idxm f_rowsel f_onehot f_rows_sb f_scat f_xi_sb0",
    "linear_pe": "l_xt l_q l_kv0 l_kv1 l_kv l_num l_at l_out",
    "linear_act": "l_xt_sb l_eq l_ek l_v l_at_sb",
    "linear_dve": "l_qmin l_qf l_kmin l_kf l_kvm l_zm l_den l_rec l_att",
    "heads_pe": "x_k x_v x_xt x_q x_nmt x_out",
    "heads_act": "x_k_sb x_k_h x_xt_sb x_q_sb x_q_h",
    "heads_dve": "x_v_sb x_k_r1 x_k_m x_k_l x_q_r1 x_q_m x_q_l x_nm_h x_nm_l x_rden x_att",
    "heads_pool": "x_zero",
    "mixture_pe": "e_xt e_gt e_g e_ct e_b2",
    "mixture_act": "e_xt_sb e_gt_sb e_exp e_ct_sb",
    "mixture_dve": "e_g_sb e_above e_equal e_tied e_rank1 e_rank e_sel e_max e_sub e_msel e_sum e_rec e_comb e_acc0",
}
COUNTED = {"m_rd": GB, "m_seg": GB, "m_yb": GB, "m_l": GB, "m_mix": GB, "f_up": NE0, "f_act": NE0,
           "x_a": 4 * GB, "x_amax": 4 * GB, "x_b": 4 * GB, "x_p": 4 * GB, "x_pv": 4 * GB,
           "e_up": NE1 * FT1, "e_act": NE1 * FT1, "e_down": NE1, "e_acc": NE1 - 1}


def decoder(nc, x, ctx_r, ctx_t, mask, w, out):
    pairs = x.shape[1] // (W * LANES)
    stack = ExitStack()

    def sb(name, shape, dt=F32):
        return stack.enter_context(nc.sbuf_tensor(name, shape, dt))

    with stack:
        sequence = {q: [stack.enter_context(nc.semaphore(f"{q}{g}")) for g in range(LANES)] for q in SEQUENCES}
        counted = {name: stack.enter_context(nc.semaphore(name)) for name in COUNTED}
        constants = stack.enter_context(nc.semaphore("constants"))
        scaled = stack.enter_context(nc.semaphore("scaled"))
        home = {step: (q, n) for q, steps in SEQUENCES.items() for n, step in enumerate(steps.split())}
        taken = {(q, g): [] for q in SEQUENCES for g in range(LANES)}

        def at(i, g, step):
            q, n = home[step]
            return sequence[q][g], i * len(SEQUENCES[q].split()) + (n + 1)

        def sig(step, g):
            q, _ = home[step]
            taken[q, g].append(step)
            assert taken[q, g] == SEQUENCES[q].split()[:len(taken[q, g])], (step, taken[q, g])
            return sequence[q][g]

        weights_in = stack.enter_context(nc.semaphore("weights_in"))
        inputs_in = [stack.enter_context(nc.semaphore(f"inputs_in{g}")) for g in range(LANES)]
        rows_moved = [stack.enter_context(nc.semaphore(f"rows_moved{g}")) for g in range(LANES)]
        parts_out = [stack.enter_context(nc.semaphore(f"parts_out{g}")) for g in range(LANES)]
        parts_in = [stack.enter_context(nc.semaphore(f"parts_in{g}")) for g in range(LANES)]
        shift_out = [stack.enter_context(nc.semaphore(f"shift_out{g}")) for g in range(LANES)]
        shift_in = [stack.enter_context(nc.semaphore(f"shift_in{g}")) for g in range(LANES)]
        lane_free = [stack.enter_context(nc.semaphore(f"lane_free{g}")) for g in range(LANES)]

        wt = {name: sb("w_" + name, list(ap.shape)) for name, ap in w.items()
              if name not in ("xbo0", "xbo1", "lbo", "xbv", "negA")}
        bcast = {name: sb("w_" + name, [P, ap.shape[0]]) for name, ap in w.items()
                 if name in ("xbo0", "xbo1", "lbo", "xbv", "negA")}
        n_weights = len(w)

        ident = sb("ident", [P, P])
        tri = sb("tri", [P, P])
        strict = sb("strict", [P, P])
        ones_row = sb("ones_row", [32, P], BF16)
        head_mask = sb("head_mask", [P, P])
        head_cols = sb("head_cols", [P, NH])
        ones_of_head = sb("ones_of_head", [P, 4, 32])
        tok_id = sb("tok_id", [P, 1])
        tok_row = sb("tok_row", [P, P])
        own_col = sb("own_col", [32, 32])
        own_quarter = sb("own_quarter", [32, 4])
        own_row = sb("own_row", [32, GB, 2])
        before = sb("before", [P, NE1, NE1])
        neg_half = sb("neg_half", [P, GB])
        a_half = sb("a_half", [P, 2])
        neg_a = sb("neg_a", [P, HS])
        wq_scaled_bias = sb("wq_scaled_bias", [P, 1])
        neg_a_exp = sb("neg_a_exp", [P, HS])
        ones4 = sb("ones4", [P, GB, 1])
        spare = sb("spare", [P, 1 + LANES])
        pool_made = stack.enter_context(nc.semaphore("pool_made"))

        def lane(name, shape, dt=F32):
            return [sb(f"{name}{g}", shape, dt) for g in range(LANES)]

        def seqs(ap):
            return ap.rearrange("p (b n) -> p b n", b=GB)

        def flat(ap):
            return ap[:].rearrange("p b n -> p (b n)")

        def spread(ap, axis, count):
            v = ap.unsqueeze(axis)
            return v.broadcast_to(tuple(v.shape[:axis]) + (count,) + tuple(v.shape[axis + 1:]))

        X = lane("X", [P, GB, P])
        CR = lane("CR", [P, GB, P])
        CT = lane("CT", [P, GB, P])
        MK = lane("MK", [1, W], U8)
        MB = lane("MB", [1, W], BF16)
        R = lane("R", [P, GB, P])
        T = lane("T", [P, GB, P])
        A03 = lane("A03_", [P, 4, W])
        A47 = lane("A47_", [P, 4, W])
        A = [[seqs((A03 if n < 4 else A47)[g][:, n % 4, :]) for g in range(LANES)] for n in range(8)]
        VM = [A47[g][:].rearrange("p b (h m) -> p b h m", m=32) for g in range(LANES)]
        B16 = lane("B16", [P, W], BF16)
        HFW = lane("HF_", [P, 4, W])
        HF = [[HFW[g][:, 2 * n:2 * n + 2, :] for g in range(LANES)] for n in range(2)]
        HTW = lane("HT_", [P, 2, W])
        HT = [[HTW[g][:, n, :].rearrange("p (f n) -> p f n", f=FT0) for g in range(LANES)] for n in range(2)]
        PTW = lane("PT_", [P, 2, W])
        PT = [[PTW[g][:, n, :].rearrange("p (h n) -> p h n", h=4) for g in range(LANES)] for n in range(2)]
        PARTS = [[(HTW if n < 4 else PTW)[g][:, (n % 4) // 2, (n % 2) * (W // 2):(n % 2 + 1) * (W // 2)].bitcast(BF16)
                  for g in range(LANES)] for n in range(6)]
        g8 = [HTW[g][0:8, 0, :] for g in range(LANES)]
        cT = [HTW[g][0:NE1, 1, :] for g in range(LANES)]
        idxm = [HTW[g][0:32, 1, :].bitcast(BF16).rearrange("p (c k) -> p c k", k=CAP) for g in range(LANES)]
        HFF = [HFW[g][:].rearrange("p a n -> p (a n)") for g in range(LANES)]
        vx = [HFF[g][:, 0:GB * (P + 2)].rearrange("p (b n) -> p b n", b=GB) for g in range(LANES)]
        r144 = [HFF[g][:, 2 * W:2 * W + GB * (P + NH)].rearrange("p (b n) -> p b n", b=GB) for g in range(LANES)]
        QS = lane("QS", [SROWS, NH // 2, 2, W], BF16)
        KS = lane("KS", [SROWS, NH // 2, W], BF16)
        st6 = lane("st6", [P, GB, 6])
        mv = lane("mv", [P, GB, 2])
        sm = [lane(f"sm{n}_", [P, 64]) for n in range(8)]
        small = [lane(f"small{n}_", [32, P]) for n in range(5)]
        topv = lane("topv", [32, CAP])
        topi = lane("topi", [32, CAP], U32)
        nmp = [[HTW[g][0:NH, n, 0:W // 2].bitcast(BF16) for g in range(LANES)] for n in range(2)]
        bank = [[stack.enter_context(nc.psum_tensor(f"bank{g}{k}", [P, W], F32)) for k in range(4)]
                for g in range(LANES)]
        q_parts = [nc.dram_tensor(f"q_parts{g}", [SLOTS, P, W], BF16, kind="Internal").ap() for g in range(LANES)]
        k_parts = [nc.dram_tensor(f"k_parts{g}", [SLOTS, P, W], BF16, kind="Internal").ap() for g in range(LANES)]
        s_parts = [nc.dram_tensor(f"s_parts{g}", [2, NH, W], BF16, kind="Internal").ap() for g in range(LANES)]

        def apart(eng):
            eng.nop(nofuse=True)

        def expert_cols(g, n):
            return A47[g][:, 2:4, :].rearrange("p t (e b k) -> p (t e) b k", e=4, b=GB)[:, :, 2 * n:2 * n + 2, :]

        def bank_experts(g, n):
            return bank[g][n][:].rearrange("p (b e k) -> p e b k", b=2, k=CAP)

        def nth(i, g, step, k):
            return i * (LANES * COUNTED[step]) + (g * COUNTED[step] + k + 1)

        block = stack.enter_context(nc.Block())

        @block.sync
        def _(sp):
            for name, ap in w.items():
                dst, src = (bcast[name], ap.partition_broadcast(P)) if name in bcast else (wt[name], ap)
                sp.dma_start(dst[:], src).then_inc(weights_in, 16)
            with sp.Fori(0, pairs, 1) as i:

                def load(g):
                    sp.wait_ge(lane_free[g], i * 16 + 16)
                    cols = bass.ds(i * (LANES * W) + g * W, W)
                    sp.dma_start(X[g][:].rearrange("p b n -> p (b n)"), x[:, cols]).then_inc(inputs_in[g], 16)
                    sp.dma_start(CR[g][:].rearrange("p b n -> p (b n)"), ctx_r[:, cols]).then_inc(inputs_in[g], 16)
                    sp.dma_start(flat(CT[g]), ctx_t[:, cols]).then_inc(inputs_in[g], 16)
                    sp.dma_start(MK[g][:], mask[:, cols]).then_inc(inputs_in[g], 16)

                def move_expert_rows(g):
                    for half in range(2):
                        sp.wait_ge(*at(i, g, f"f_y_sb{half}"))
                        for b in range(GB):
                            for q in range(4):
                                sp.dma_start(A[4 + half][g][32 * q:32 * q + 32, b, :],
                                             A[2 + half][g][32 * b:32 * b + 32, q, :]).then_inc(rows_moved[g], 16)

                def stack_parts(g):
                    for side, names, dram in (("k", "hmhmlh", k_parts[g]), ("q", "hhmmhl", q_parts[g])):
                        sp.wait_ge(*at(i, g, f"x_{side}_l"))
                        for s, part in enumerate(names):
                            src = PARTS["hml".index(part) + (3 if side == "k" else 0)][g]
                            sp.dma_start(dram[s], src[:]).then_inc(parts_out[g], 16)
                    sp.wait_ge(parts_out[g], i * (12 * 16) + 12 * 16)
                    kd = k_parts[g].rearrange("s (d r j) n -> (s d) r j n", d=HD, j=2)
                    qd = q_parts[g].rearrange("s (d r j) n -> (s d) r j n", d=HD, j=2)
                    for j in range(2):
                        rows = slice(KROWS * j, KROWS * j + KROWS)
                        sp.dma_start(KS[g][rows], kd[:, :, j]).then_inc(parts_in[g], 16)
                        sp.dma_start(QS[g][rows, :, j], qd[:, :, j]).then_inc(parts_in[g], 16)

                def stack_shift(g):
                    sp.wait_ge(*at(i, g, "x_nm_l"))
                    for n in range(2):
                        sp.dma_start(s_parts[g][n], nmp[n][g][:]).then_inc(shift_out[g], 16)
                    sp.wait_ge(shift_out[g], i * 32 + 32)
                    sd = s_parts[g].rearrange("n (r j) m -> n r j m", j=2)
                    for j in range(2):
                        rows = slice(SHIFT0 + 2 * j, SHIFT0 + 2 * j + 2)
                        sp.dma_start(QS[g][rows, :, j], sd[:, :, j]).then_inc(shift_in[g], 16)

                def store(g):
                    sp.wait_ge(*at(i, g, "n5_done"))
                    sp.dma_start(out[:, bass.ds(i * (LANES * W) + g * W, W)],
                                 flat(X[g])).then_inc(lane_free[g], 16)

                for step in (load, move_expert_rows, stack_parts, stack_shift, store):
                    for g in range(LANES):
                        step(g)
            for g in range(LANES):
                sp.wait_ge(lane_free[g], 16 * pairs + 16)

        @block.tensor
        def _(pe):
            pe.wait_ge(constants, N_CONSTANTS)
            pe.wait_ge(weights_in, 16 * n_weights)
            with pe.Fori(0, pairs, 1) as i:
                mm, tr = pe.matmul, pe.transpose

                def to_c(g, k, src, step):
                    for b in range(GB):
                        last = tr(bank[g][k][:, b * P:(b + 1) * P], src[:, b, :], ident[:])
                    last.then_inc(sig(step, g), 1)

                def wide(g, k, lhsT, rhs, step):
                    mm(bank[g][k][0:lhsT.shape[1], :], lhsT, rhs, start=True, stop=True).then_inc(sig(step, g), 1)

                def m_xt(g):
                    pe.wait_ge(*at(i, g, "m_norm"))
                    to_c(g, 0, R[g], "m_xt")

                def m_proj(g):
                    pe.wait_ge(*at(i, g, "m_xt_sb"))
                    t = flat(T[g])
                    wide(g, 1, wt["inT"][:, 256:384], t, "m_xs0")
                    wide(g, 2, wt["inT"][:, 384:512], t, "m_xs1")
                    wide(g, 3, wt["inT"][:, 512:640], t, "m_b")
                    wide(g, 0, wt["inT"][:, 640:768], t, "m_c")

                def m_gates(g):
                    t = flat(T[g])
                    pe.wait_ge(*at(i, g, "m_b_sb"))
                    wide(g, 3, wt["inT"][:, 768:772], t, "m_dtt")
                    pe.wait_ge(*at(i, g, "m_c_sb"))
                    for b in range(GB):
                        last = mm(bank[g][0][:, b * P:(b + 1) * P], A[0][g][:, b, :], A[1][g][:, b, :],
                                  start=True, stop=True)
                    last.then_inc(sig("m_gram", g), 1)
                    pe.wait_ge(*at(i, g, "m_dtt_sb"))
                    apart(pe)
                    for b in range(GB):
                        last = tr(bank[g][3][:, b * HS:(b + 1) * HS], g8[g][0:HS, b * P:(b + 1) * P], ident[0:HS, 0:HS])
                    last.then_inc(sig("m_dt", g), 1)

                def m_z(g):
                    t = flat(T[g])
                    pe.wait_ge(*at(i, g, "m_xh0"))
                    wide(g, 1, wt["inT"][:, 0:128], t, "m_z0")
                    pe.wait_ge(*at(i, g, "m_xh1"))
                    wide(g, 2, wt["inT"][:, 128:256], t, "m_z1")

                def m_rows(g):
                    pe.wait_ge(*at(i, g, "m_gram_sb"))
                    to_c(g, 0, A[2][g], "m_xhr0")
                    pe.wait_ge(*at(i, g, "m_dt_sb"))
                    to_c(g, 3, A[3][g], "m_xhr1")

                def m_scan(g):
                    pe.wait_ge(*at(i, g, "m_dtx1"))
                    for b in range(GB):
                        pe.wait_ge(counted["m_rd"], nth(i, g, "m_rd", b))
                        if b >= 2:
                            pe.wait_ge(counted["m_l"], nth(i, g, "m_l", b - 2))
                        mm(bank[g][b % 2][:], strict[:], PTW[g][:, b % 2, :],
                           start=True, stop=True).then_inc(counted["m_seg"], 1)
                        if b >= 1:
                            m_head_rows(g, b - 1)
                    m_head_rows(g, GB - 1)

                def m_head_rows(g, b):
                    pe.wait_ge(counted["m_mix"], nth(i, g, "m_mix", b))
                    for h in range(HS):
                        rows = slice(PD * (h % 2), PD * (h % 2) + PD)
                        last = mm(bank[g][2 + h // 2][rows, b * P:(b + 1) * P],
                                  A[4 + h // 2][g][:, b, PD * (h % 2):PD * (h % 2) + PD],
                                  HT[b % 2][g][:, h, :], start=True, stop=True)
                    last.then_inc(counted["m_yb"], 1)

                def m_out(g):
                    pe.wait_ge(*at(i, g, "m_gate1"))
                    for b in range(GB):
                        for c in range(2):
                            last = mm(bank[g][0][:, b * P:(b + 1) * P], A[6 + c][g][:, b, :],
                                      wt["outT"][:, c, :], start=(c == 0), stop=(c == 1))
                    last.then_inc(sig("m_out", g), 1)

                def c_kt(g):
                    pe.wait_ge(*at(i, g, "m_skip1"))
                    wide(g, 3, wt["wk0"][:], flat(CT[g]), "c_kt")

                def c_q(g):
                    pe.wait_ge(*at(i, g, "n0_done"))
                    to_c(g, 0, X[g], "c_xt")
                    pe.wait_ge(*at(i, g, "c_xt_sb"))
                    wide(g, 1, wt["wq0"][:], flat(T[g]), "c_q")

                def c_scores(g):
                    pe.wait_ge(*at(i, g, "c_mask"))
                    pe.wait_ge(*at(i, g, "c_q_sb"))
                    mm(bank[g][2][:], ones_row[0:1, :], MB[g][:], start=True, stop=False, skip_group_check=True)
                    for b in range(GB):
                        last = mm(bank[g][2][:, b * P:(b + 1) * P], A[1][g][:, b, :], A[0][g][:, b, :],
                                  start=False, stop=True, skip_group_check=True)
                    last.then_inc(sig("c_scores", g), 1)

                def c_pt(g):
                    pe.wait_ge(*at(i, g, "c_exp"))
                    to_c(g, 3, A[2][g], "c_pt")

                def c_ot(g):
                    pe.wait_ge(*at(i, g, "c_pt_sb"))
                    for b in range(GB):
                        last = mm(bank[g][0][:, b * P:(b + 1) * P], CR[g][:, b, :], A[3][g][:, b, :],
                                  start=True, stop=True)
                    last.then_inc(sig("c_ot", g), 1)

                def rows_times(g, k, lhs, rhs, step):
                    for b in range(GB):
                        last = mm(bank[g][k][:, b * P:(b + 1) * P], lhs[:, b, :], rhs, start=True, stop=True)
                    last.then_inc(sig(step, g), 1)

                def c_out(g):
                    pe.wait_ge(*at(i, g, "c_ot_sb"))
                    rows_times(g, 1, A[4][g], wt["wo0"][:], "c_out")

                def f_gate(g):
                    pe.wait_ge(*at(i, g, "n1_done"))
                    to_c(g, 0, X[g], "f_xt")
                    pe.wait_ge(*at(i, g, "f_xt_sb"))
                    wide(g, 1, wt["gate"][:], flat(T[g]), "f_gt")

                def f_gate_rows(g):
                    pe.wait_ge(*at(i, g, "f_gt_sb"))
                    apart(pe)
                    for b in range(GB):
                        last = tr(bank[g][2][:, b * NE0:(b + 1) * NE0], g8[g][0:NE0, b * P:(b + 1) * P],
                                  ident[0:NE0, 0:NE0])
                    last.then_inc(sig("f_g", g), 1)

                def f_prob_t(g):
                    pe.wait_ge(*at(i, g, "f_prob"))
                    tr(bank[g][3][0:32, 0:P], sm[2][g][:, 0:32], ident[:]).then_inc(sig("f_pt", g), 1)

                def f_spread(g):
                    pe.wait_ge(*at(i, g, "f_idxm"))
                    for n in range(2):
                        last = mm(bank[g][n][:], ones_row[:], idxm[g][:, 16 * n:16 * n + 16, :], start=True, stop=True)
                    last.then_inc(sig("f_bc", g), 1)
                    pe.wait_ge(*at(i, g, "f_rowsel"))
                    for n in range(2):
                        last = mm(bank[g][2][:, 8 * n:8 * n + 8], small[3 + n][g][:],
                                  own_row[:].rearrange("p b h -> p (b h)"), start=True, stop=True)
                    last.then_inc(sig("f_rows", g), 1)

                def f_gather(g):
                    pe.wait_ge(*at(i, g, "f_onehot"))
                    for b in range(GB):
                        for n in range(2):
                            last = mm(bank[g][b // 2][:, (b % 2) * 256 + n * P:(b % 2) * 256 + n * P + P], X[g][:, b, :],
                                      A[n][g][:, :, b * CAP:(b + 1) * CAP], start=True, stop=True)
                    last.then_inc(sig("f_xi", g), 1)

                def f_experts(g):
                    pe.wait_ge(*at(i, g, "f_xi_sb0"))
                    pe.wait_ge(*at(i, g, "f_xi_sb1"))
                    for e in range(NE0 + 1):
                        if e < NE0:
                            if e >= 2:
                                pe.wait_ge(counted["f_act"], nth(i, g, "f_act", e - 2))
                            for f in range(FT0):
                                last = mm(bank[g][e % 2][:, f * P:(f + 1) * P], wt["w1"][:, e, f * P:(f + 1) * P],
                                          A[6 + e // 4][g][:, e % 4, :], start=True, stop=True)
                            last.then_inc(counted["f_up"], 1)
                        if e >= 1:
                            f_down(g, e - 1)

                def f_down(g, e):
                    pe.wait_ge(counted["f_act"], nth(i, g, "f_act", e))
                    for f in range(FT0):
                        last = mm(bank[g][2 + e // 4][:, (e % 4) * P:(e % 4 + 1) * P], HT[e % 2][g][:, f, :],
                                  wt["w2"][:, e, f, :], start=(f == 0), stop=(f == FT0 - 1))
                    if e % 4 == 3:
                        last.then_inc(sig(f"f_down{e // 4}", g), 1)

                def f_add(g):
                    pe.wait_ge(*at(i, g, "f_scat"))
                    pe.wait_ge(rows_moved[g], i * (32 * 16) + 32 * 16)
                    for b in range(GB):
                        for h in range(2):
                            last = mm(bank[g][0][:, b * P:(b + 1) * P], HFW[g][:, h, b * P:(b + 1) * P], A[4 + h][g][:, b, :],
                                      start=(h == 0), stop=(h == 1))
                    last.then_inc(sig("f_add", g), 1)

                def l_q(g):
                    pe.wait_ge(*at(i, g, "n2_done"))
                    to_c(g, 0, X[g], "l_xt")
                    pe.wait_ge(*at(i, g, "l_xt_sb"))
                    wide(g, 1, wt["lqkv"][:, 0:P], flat(T[g]), "l_q")
                    for b in range(GB):
                        last = mm(bank[g][2 + b // 2][:, (b % 2) * 256:(b % 2) * 256 + 256], T[g][:, b, :],
                                  wt["lqkv"][:, P:3 * P], start=True, stop=True)
                        if b % 2:
                            last.then_inc(sig(f"l_kv{b // 2}", g), 1)

                def l_kv(g):
                    pe.wait_ge(*at(i, g, "l_kf"))
                    pe.wait_ge(*at(i, g, "l_v"))
                    for b in range(GB):
                        last = mm(bank[g][2 + b // 2][:, (b % 2) * 256:(b % 2) * 256 + P + 1], A[1][g][:, b, :],
                                  vx[g][:, b, 0:P + 1], start=True, stop=True)
                    last.then_inc(sig("l_kv", g), 1)

                def l_num(g):
                    pe.wait_ge(*at(i, g, "l_zm"))
                    for b in range(GB):
                        last = mm(bank[g][b // 2][:, (b % 2) * 256:(b % 2) * 256 + P + NH], A[0][g][:, b, :],
                                  r144[g][:, b, :], start=True, stop=True)
                    last.then_inc(sig("l_num", g), 1)

                def l_at(g):
                    pe.wait_ge(*at(i, g, "l_att"))
                    to_c(g, 2, A[2][g], "l_at")

                def l_out(g):
                    pe.wait_ge(*at(i, g, "l_at_sb"))
                    rows_times(g, 3, A[3][g], wt["lout"][:], "l_out")

                def x_k(g):
                    pe.wait_ge(*at(i, g, "l_att"))
                    wide(g, 0, wt["wk1"][:], flat(CT[g]), "x_k")
                    rows_times(g, 1, CT[g], wt["wv1"][:], "x_v")

                def x_q(g):
                    pe.wait_ge(*at(i, g, "n3_done"))
                    to_c(g, 2, X[g], "x_xt")
                    pe.wait_ge(*at(i, g, "x_xt_sb"))
                    wide(g, 3, wt["wq1"][:], flat(T[g]), "x_q")

                def x_max(g):
                    pe.wait_ge(parts_in[g], i * (4 * 16) + 4 * 16)
                    pe.wait_ge(*at(i, g, "x_v_sb"))
                    pe.wait_ge(*at(i, g, "x_q_sb"))
                    for n in range(4 * GB):
                        b, c = n // 4, n % 4
                        if n >= 4:
                            pe.wait_ge(counted["x_amax"], nth(i, g, "x_amax", n - 4))
                        for m in range(4):
                            pos = 4 * c + m
                            last = mm(bank[g][n % 4][:, m * P:(m + 1) * P],
                                      QS[g][0:SHIFT0, pos // 2, pos % 2, b * P:(b + 1) * P],
                                      KS[g][0:SHIFT0, pos // 2, b * P:(b + 1) * P], start=True, stop=True)
                        last.then_inc(counted["x_a"], 1)

                def x_nmt(g):
                    pe.wait_ge(counted["x_amax"], nth(i, g, "x_amax", 4 * GB - 1))
                    for b in range(GB):
                        last = tr(bank[g][0][0:NH, b * P:(b + 1) * P], sm[0][g][:, b * NH:(b + 1) * NH], ident[:])
                    last.then_inc(sig("x_nmt", g), 1)

                def x_weights(g, n):
                    b, c = n // 4, n % 4
                    if n >= 2:
                        pe.wait_ge(counted["x_p"], nth(i, g, "x_p", n - 2))
                    for r in range(2):
                        last = mm(bank[g][n % 2][:, r * 256:(r + 1) * 256], KS[g][0:SROWS, 2 * c + r, b * P:(b + 1) * P],
                                  QS[g][0:SROWS, 2 * c + r, :, b * P:(b + 1) * P], start=True, stop=True)
                    last.then_inc(counted["x_b"], 1)

                def x_values(g, n):
                    b, c = n // 4, n % 4
                    pe.wait_ge(counted["x_p"], nth(i, g, "x_p", n))
                    for lhs, k in ((VM[g][:, b, c::4], 2), (spread(ones_of_head[:, c, :], 1, 4), 3)):
                        for m in range(4):
                            last = mm(bank[g][k][32 * m:32 * m + 32, b * P:(b + 1) * P],
                                      lhs[:, m],
                                      PT[n % 2][g][:, m, :], start=(c == 0), stop=(c == 3),
                                      skip_group_check=True)
                    last.then_inc(counted["x_pv"], 1)

                def x_heads(g):
                    pe.wait_ge(shift_in[g], i * 32 + 32)
                    pe.wait_ge(*at(i, g, "x_nm_l"))
                    x_weights(g, 0)
                    for n in range(4 * GB):
                        if n + 1 < 4 * GB:
                            x_weights(g, n + 1)
                        x_values(g, n)

                def x_out(g):
                    pe.wait_ge(*at(i, g, "x_att"))
                    rows_times(g, 0, A[3][g], wt["wo1"][:], "x_out")

                def e_gate(g):
                    pe.wait_ge(*at(i, g, "n4_done"))
                    to_c(g, 0, X[g], "e_xt")
                    pe.wait_ge(*at(i, g, "e_xt_sb"))
                    wide(g, 1, wt["wg"][:], flat(T[g]), "e_gt")

                def e_gate_rows(g):
                    pe.wait_ge(*at(i, g, "e_gt_sb"))
                    apart(pe)
                    for b in range(GB):
                        last = tr(bank[g][2][:, b * NE1:(b + 1) * NE1], g8[g][0:NE1, b * P:(b + 1) * P],
                                  ident[0:NE1, 0:NE1])
                    last.then_inc(sig("e_g", g), 1)

                def e_bias(g):
                    pe.wait_ge(*at(i, g, "e_comb"))
                    for b in range(GB):
                        last = tr(bank[g][2][0:NE1, b * P:(b + 1) * P], sm[6][g][:, b * NE1:(b + 1) * NE1], ident[:])
                    last.then_inc(sig("e_ct", g), 1)
                    pe.wait_ge(*at(i, g, "e_ct_sb"))
                    rows_times(g, 3, seqs(cT[g]), wt["b2"][:], "e_b2")

                def e_experts(g):
                    pe.wait_ge(*at(i, g, "e_acc0"))
                    for e in range(NE1 + 1):
                        if e < NE1:
                            for f in range(FT1):
                                n = FT1 * e + f
                                if n >= 2:
                                    pe.wait_ge(counted["e_act"], nth(i, g, "e_act", n - 2))
                                mm(bank[g][n % 2][:], wt["we1"][:, e, f * P:(f + 1) * P],
                                   flat(T[g]), start=True, stop=True).then_inc(counted["e_up"], 1)
                        if e >= 1:
                            e_down(g, e - 1)

                def e_down(g, e):
                    pe.wait_ge(counted["e_act"], nth(i, g, "e_act", FT1 * e + FT1 - 1))
                    if e >= 2:
                        pe.wait_ge(counted["e_acc"], nth(i, g, "e_acc", e - 2))
                    for b in range(GB):
                        for f in range(FT1):
                            last = mm(bank[g][2 + e % 2][:, b * P:(b + 1) * P], HF[e % 2][g][:, f, b * P:(b + 1) * P],
                                      wt["we2"][:, e, f, :], start=(f == 0), stop=(f == FT1 - 1))
                    last.then_inc(counted["e_down"], 1)

                for step in (m_xt, m_proj, m_gates, m_z, m_rows, m_scan, m_out, c_kt, c_q, c_scores, c_pt, c_ot,
                             c_out, f_gate, f_gate_rows, f_prob_t, f_spread, f_gather, f_experts, f_add,
                             l_q, l_kv, l_num, l_at, x_k, l_out, x_q, x_max, x_nmt, x_heads, x_out,
                             e_gate, e_gate_rows, e_bias, e_experts):
                    for g in range(LANES):
                        step(g)

        @block.vector
        def _(dve):
            def const(ins):
                ins.then_inc(constants, 1)

            const(dve.memset(ones_row[:], 1.0))
            const(dve.memset(neg_half[:], -0.5))
            for g in range(LANES):
                const(dve.memset(QS[g][:].rearrange("p r j n -> p (r j n)"), 0.0))
                const(dve.memset(KS[g][:].rearrange("p r n -> p (r n)"), 1.0))
            dve.wait_ge(weights_in, 16 * n_weights)
            const(dve.tensor_scalar(a_half[:], wt["D2"][:], 0.5, None, ALU.mult))
            const(dve.tensor_scalar(wq_scaled_bias[:], wt["xbq1"][:], HD ** -0.5, None, ALU.mult))
            dve.wait_ge(scaled, 1)
            const(dve.tensor_scalar(neg_a[:], neg_a_exp[:], -1.0, None, ALU.mult))
            dve.wait_ge(constants, N_CONSTANTS)

            with dve.Fori(0, pairs, 1) as i:
                def rsum(out_, in_, op=ALU.add, negate=False):
                    return dve.tensor_reduce(out_, in_, AX.X, op, negate=negate)

                def stats_steps(g, src, pre):
                    for b in range(GB):
                        last = dve.bn_stats(st6[g][:, b, :], src[:, b, :])
                    last.then_inc(sig(f"{pre}_stats", g), 1)
                    dve.wait_ge(*at(i, g, f"{pre}_stats"))
                    apart(dve)
                    for b in range(GB):
                        last = dve.bn_aggr(mv[g][:, b, :], st6[g][:, b, :])
                    return last

                def norm_stats(n):
                    def step(g):
                        dve.wait_ge(*at(i, g, f"n{n}_res"))
                        stats_steps(g, R[g], f"n{n}").then_inc(sig(f"n{n}_mom", g), 1)
                        dve.wait_ge(*at(i, g, f"n{n}_mom"))
                        dve.tensor_scalar(sm[7][g][:, 0:GB], mv[g][:, :, 1], LN_EPS, None,
                                          ALU.add).then_inc(sig(f"n{n}_eps", g), 1)
                    return step

                def norm_rows(n):
                    def step(g):
                        dve.wait_ge(*at(i, g, f"n{n}_rstd"))
                        for b in range(GB):
                            last = dve.tensor_scalar(X[g][:, b, :], R[g][:, b, :], mv[g][:, b, 0:1],
                                                     sm[6][g][:, b:b + 1], ALU.subtract, ALU.mult)
                        last.then_inc(sig(f"n{n}_done", g), 1)
                    return step

                def res(n, k, produced, resid=None):
                    def step(g):
                        dve.wait_ge(*at(i, g, produced))
                        if resid:
                            dve.wait_ge(*at(i, g, resid))
                        dve.tensor_tensor(flat(R[g]), bank[g][k][:], flat(R[g]),
                                          ALU.add).then_inc(sig(f"n{n}_res", g), 1)
                    return step

                def m_stats(g):
                    dve.wait_ge(inputs_in[g], i * 64 + 64)
                    stats_steps(g, X[g], "m").then_inc(sig("m_moments", g), 1)
                    dve.wait_ge(*at(i, g, "m_moments"))
                    dve.tensor_tensor(sm[0][g][:, 0:GB], mv[g][:, :, 0], mv[g][:, :, 0], ALU.mult)\
                       .then_inc(sig("m_sq", g), 1)
                    dve.wait_ge(*at(i, g, "m_sq"))
                    dve.scalar_tensor_tensor(sm[7][g][:, 0:GB], mv[g][:, :, 1], RMS_EPS, sm[0][g][:, 0:GB],
                                             ALU.add, ALU.add).then_inc(sig("m_ms", g), 1)

                def m_norm(g):
                    dve.wait_ge(*at(i, g, "m_rstd"))
                    for b in range(GB):
                        last = dve.tensor_scalar(R[g][:, b, :], X[g][:, b, :], sm[6][g][:, b:b + 1], None, ALU.mult)
                    last.then_inc(sig("m_norm", g), 1)

                def m_conv(g):
                    for c in range(2):
                        dve.wait_ge(*at(i, g, f"m_xs{c}"))
                        u, xs = A[6 + c][g], seqs(bank[g][1 + c][:])
                        dve.tensor_scalar(u, xs, wt["convw"][:, c, 3:4], wt["convb"][:, c:c + 1], ALU.mult, ALU.add)\
                           .then_inc(sig(f"m_tap{c}0", g), 1)
                        for k in range(1, 4):
                            dve.wait_ge(*at(i, g, f"m_tap{c}{k - 1}"))
                            dve.scalar_tensor_tensor(u[:, :, k:], xs[:, :, :P - k], wt["convw"][:, c, 3 - k:4 - k],
                                                     u[:, :, k:], ALU.mult, ALU.add).then_inc(sig(f"m_tap{c}{k}", g), 1)

                def m_silu(g):
                    for c in range(2):
                        dve.wait_ge(*at(i, g, f"m_tanh{c}"))
                        dve.scalar_tensor_tensor(A[2 + c][g], seqs(HFW[g][:, 1 + c, :]), 1.0, A[6 + c][g],
                                                 ALU.add, ALU.mult).then_inc(sig(f"m_xh{c}", g), 1)

                def m_gram(g):
                    dve.wait_ge(*at(i, g, "m_gram"))
                    dve.tensor_tensor(seqs(HFW[g][:, 0, :]), seqs(bank[g][0][:]), spread(tri[:], 1, GB), ALU.mult)\
                       .then_inc(sig("m_gram_sb", g), 1)
                    dve.wait_ge(*at(i, g, "m_dt"))
                    dve.tensor_copy(sm[0][g][:, 0:16], bank[g][3][:, 0:16]).then_inc(sig("m_dt_sb", g), 1)
                    dve.wait_ge(*at(i, g, "m_dt_sb"))
                    dve.scalar_tensor_tensor(sm[1][g][:, 0:16], sm[0][g][:, 0:16], -1.0, sm[0][g][:, 0:16],
                                             ALU.mult, ALU.max)\
                       .then_inc(sig("m_dt_abs", g), 1)

                def m_dt_one(g):
                    dve.wait_ge(*at(i, g, "m_dt_exp"))
                    dve.tensor_scalar(sm[3][g][:, 0:16], sm[2][g][:, 0:16], 1.0, None, ALU.add)\
                       .then_inc(sig("m_dt_one", g), 1)
                    dve.wait_ge(*at(i, g, "m_dt_one"))
                    dve.tensor_scalar(sm[4][g][:, 0:16], sm[3][g][:, 0:16], 1.0, TINY, ALU.subtract, ALU.max)\
                       .then_inc(sig("m_dt_den", g), 1)
                    dve.wait_ge(*at(i, g, "m_dt_den"))
                    dve.reciprocal(sm[5][g][:, 0:16], sm[4][g][:, 0:16]).then_inc(sig("m_dt_rec", g), 1)

                def m_dt(g):
                    dve.wait_ge(*at(i, g, "m_dt_ln"))
                    dve.wait_ge(*at(i, g, "m_dt_rec"))
                    dve.scalar_tensor_tensor(sm[4][g][:, 0:16], sm[1][g][:, 0:16], TINY, sm[5][g][:, 0:16],
                                             ALU.max, ALU.mult).then_inc(sig("m_dt_ratio", g), 1)
                    dve.wait_ge(*at(i, g, "m_dt_ratio"))
                    dve.tensor_tensor(sm[5][g][:, 0:16], sm[4][g][:, 0:16], sm[2][g][:, 0:16], ALU.mult)\
                       .then_inc(sig("m_dt_log1p", g), 1)
                    dve.wait_ge(*at(i, g, "m_dt_log1p"))
                    dve.scalar_tensor_tensor(sm[3][g][:, 0:16], sm[0][g][:, 0:16], 0.0, sm[5][g][:, 0:16],
                                             ALU.max, ALU.add).then_inc(sig("m_dt_done", g), 1)
                    dve.wait_ge(*at(i, g, "m_dt_done"))
                    dt = sm[3][g][:, 0:16].rearrange("p (b h) -> p b h", b=GB)
                    dve.tensor_tensor(sm[5][g][:, 0:16].rearrange("p (b h) -> p b h", b=GB), dt,
                                      spread(neg_a[:], 1, GB), ALU.mult).then_inc(sig("m_decay", g), 1)
                    dve.tensor_scalar(sm[4][g][:, 0:16], sm[3][g][:, 0:16], 0.5, None, ALU.mult)\
                       .then_inc(sig("m_half", g), 1)

                def m_gates(g):
                    for c in range(2):
                        dve.wait_ge(*at(i, g, f"m_tz{c}"))
                        dve.scalar_tensor_tensor(A[c][g], seqs(HFW[g][:, 3 if c == 0 else 1, :]), 1.0,
                                                 seqs(bank[g][1 + c][:]), ALU.add, ALU.mult)\
                           .then_inc(sig(f"m_sz{c}", g), 1)
                    dve.wait_ge(*at(i, g, "m_half"))
                    half = sm[4][g][:, 0:16].rearrange("p (b h) -> p b h", b=GB)
                    for c in range(2):
                        dve.wait_ge(*at(i, g, f"m_xhr{c}"))
                        dve.tensor_tensor(A[4 + c][g].rearrange("p b (h q) -> p b h q", h=2),
                                          seqs(bank[g][3 * c][:]).rearrange("p b (h q) -> p b h q", h=2),
                                          spread(half[:, :, 2 * c:2 * c + 2], 3, PD), ALU.mult)\
                           .then_inc(sig(f"m_dtx{c}", g), 1)

                def m_mix(g):
                    gram = seqs(HFW[g][:, 0, :])
                    for b in range(GB):
                        dve.wait_ge(counted["m_l"], nth(i, g, "m_l", b))
                        if b >= 2:
                            dve.wait_ge(counted["m_yb"], nth(i, g, "m_yb", b - 2))
                        dve.tensor_tensor(HT[b % 2][g], HFW[g][:, 2 + b % 2, :].rearrange("p (h n) -> p h n", h=HS),
                                          spread(gram[:, b, :], 1, HS), ALU.mult).then_inc(counted["m_mix"], 1)

                def m_skip(g):
                    dve.wait_ge(counted["m_yb"], nth(i, g, "m_yb", GB - 1))
                    for c in range(2):
                        dve.scalar_tensor_tensor(A[6 + c][g], A[2 + c][g], a_half[:, c:c + 1],
                                                 seqs(bank[g][2 + c][:]), ALU.mult, ALU.add)\
                           .then_inc(sig(f"m_skip{c}", g), 1)
                    for c in range(2):
                        dve.wait_ge(*at(i, g, f"m_skip{c}"))
                        dve.tensor_tensor(A[6 + c][g], A[6 + c][g], A[c][g], ALU.mult)\
                           .then_inc(sig(f"m_gate{c}", g), 1)

                def m_res(g):
                    dve.wait_ge(*at(i, g, "m_out"))
                    dve.wait_ge(*at(i, g, "m_twice"))
                    dve.scalar_tensor_tensor(R[g][:], seqs(bank[g][0][:]), 0.5, R[g][:],
                                             ALU.mult, ALU.add).then_inc(sig("n0_res", g), 1)

                def c_mask(g):
                    dve.tensor_scalar(MB[g][:], MK[g][:], MASKED, None, ALU.mult).then_inc(sig("c_mask", g), 1)

                def c_max(g):
                    dve.wait_ge(*at(i, g, "c_scores"))
                    rsum(sm[0][g][:, 0:GB], seqs(bank[g][2][:]), ALU.max, negate=True).then_inc(sig("c_max", g), 1)

                def c_rsum(g):
                    dve.wait_ge(*at(i, g, "c_exp"))
                    dve.reciprocal(sm[2][g][:, 0:GB], sm[1][g][:, 0:GB]).then_inc(sig("c_rsum", g), 1)

                def c_pt(g):
                    dve.wait_ge(*at(i, g, "c_pt"))
                    dve.tensor_copy(A[3][g], seqs(bank[g][3][:])).then_inc(sig("c_pt_sb", g), 1)

                def c_res(g):
                    dve.wait_ge(*at(i, g, "c_out"))
                    dve.wait_ge(*at(i, g, "c_resid"))
                    dve.wait_ge(*at(i, g, "c_rsum"))
                    for b in range(GB):
                        last = dve.scalar_tensor_tensor(R[g][:, b, :], bank[g][1][:, b * P:(b + 1) * P],
                                                        sm[2][g][:, b:b + 1], R[g][:, b, :], ALU.mult, ALU.add)
                    last.then_inc(sig("n1_res", g), 1)

                def f_max(g):
                    dve.wait_ge(*at(i, g, "f_g"))
                    gate = bank[g][2][:, 0:32].rearrange("p (b e) -> p b e", b=GB)
                    rsum(sm[0][g][:, 0:GB], gate, ALU.max).then_inc(sig("f_gmax", g), 1)
                    dve.wait_ge(*at(i, g, "f_gmax"))
                    dve.tensor_tensor(sm[1][g][:, 0:32].rearrange("p (b e) -> p b e", b=GB), gate,
                                      spread(sm[0][g][:, 0:GB], 2, NE0), ALU.subtract).then_inc(sig("f_gsub", g), 1)

                def f_prob(g):
                    dve.wait_ge(*at(i, g, "f_gexp"))
                    ex = sm[3][g][:, 0:32].rearrange("p (b e) -> p b e", b=GB)
                    rsum(sm[4][g][:, 0:GB], ex).then_inc(sig("f_gsum", g), 1)
                    dve.wait_ge(*at(i, g, "f_gsum"))
                    dve.reciprocal(sm[5][g][:, 0:GB], sm[4][g][:, 0:GB]).then_inc(sig("f_grec", g), 1)
                    dve.wait_ge(*at(i, g, "f_grec"))
                    dve.tensor_tensor(sm[2][g][:, 0:32].rearrange("p (b e) -> p b e", b=GB), ex,
                                      spread(sm[5][g][:, 0:GB], 2, NE0), ALU.mult).then_inc(sig("f_prob", g), 1)

                def f_top(g):
                    dve.wait_ge(*at(i, g, "f_pt"))
                    dve.tensor_copy(small[0][g][:], bank[g][3][0:32, 0:P]).then_inc(sig("f_pt_sb", g), 1)
                    dve.wait_ge(*at(i, g, "f_pt_sb"))
                    for r in range(CAP // 8):
                        src, dst, k = small[r % 2][g], small[1 - r % 2][g], slice(8 * r, 8 * r + 8)
                        if r:
                            dve.wait_ge(*at(i, g, f"f_topw{r - 1}"))
                        apart(dve)
                        dve.max(topv[g][:, k], src[:]).then_inc(sig(f"f_topv{r}", g), 1)
                        dve.wait_ge(*at(i, g, f"f_topv{r}"))
                        apart(dve)
                        dve.max_index(topi[g][:, k], topv[g][:, k], src[:]).then_inc(sig(f"f_topi{r}", g), 1)
                        dve.match_replace(dst[:], topv[g][:, k], src[:], -1.0).then_inc(sig(f"f_topw{r}", g), 1)

                def f_index(g):
                    dve.wait_ge(*at(i, g, f"f_topi{CAP // 8 - 1}"))
                    dve.tensor_copy(small[2][g][:, 0:CAP], topi[g][:]).then_inc(sig("f_idx", g), 1)
                    dve.wait_ge(*at(i, g, "f_idx"))
                    dve.tensor_tensor(idxm[g], spread(small[2][g][:, 0:CAP], 1, 32),
                                      spread(own_col[:], 2, CAP), ALU.mult).then_inc(sig("f_idxm", g), 1)
                    for n, src in ((3, small[2][g][:, 0:CAP]), (4, topv[g][:])):
                        last = dve.tensor_tensor(small[n][g][:].rearrange("p (q k) -> p q k", q=4), spread(src, 1, 4),
                                                 spread(own_quarter[:], 2, CAP), ALU.mult)
                    last.then_inc(sig("f_rowsel", g), 1)

                def f_onehot(g):
                    dve.wait_ge(*at(i, g, "f_bc"))
                    for n in range(2):
                        last = dve.tensor_scalar(A03[g][:, n, :], bank[g][n][:], tok_id[:, 0:1], None, ALU.is_equal)
                    last.then_inc(sig("f_onehot", g), 1)
                    dve.wait_ge(*at(i, g, "f_rows"))
                    dve.tensor_copy(sm[0][g][:, 0:16], bank[g][2][:, 0:16]).then_inc(sig("f_rows_sb", g), 1)
                    dve.wait_ge(*at(i, g, "f_rows_sb"))
                    for b in range(GB):
                        for h in range(2):
                            n = 2 * b + h
                            last = dve.tensor_scalar(HFW[g][:, h, b * P:(b + 1) * P], tok_row[:], sm[0][g][:, n:n + 1],
                                                     sm[0][g][:, 8 + n:9 + n], ALU.is_equal, ALU.mult)
                    last.then_inc(sig("f_scat", g), 1)

                def f_gathered(g):
                    dve.wait_ge(*at(i, g, "f_xi"))
                    dve.tensor_copy(expert_cols(g, 0), bank_experts(g, 0)).then_inc(sig("f_xi_sb0", g), 1)

                def f_res(g):
                    dve.wait_ge(*at(i, g, "f_add_sb"))
                    dve.tensor_tensor(flat(R[g]), flat(X[g]), B16[g][:], ALU.add).then_inc(sig("n2_res", g), 1)

                def l_feat(g):
                    dve.wait_ge(*at(i, g, "l_eq"))
                    dve.tensor_scalar(A[4][g], A[4][g], 1.0, None, ALU.min).then_inc(sig("l_qmin", g), 1)
                    dve.wait_ge(*at(i, g, "l_qmin"))
                    dve.scalar_tensor_tensor(A[0][g], seqs(bank[g][1][:]), 1.0, A[4][g], ALU.add, ALU.max)\
                       .then_inc(sig("l_qf", g), 1)
                    dve.wait_ge(*at(i, g, "l_v"))
                    dve.tensor_scalar(A[5][g], A[5][g], 1.0, None, ALU.min).then_inc(sig("l_kmin", g), 1)
                    dve.wait_ge(*at(i, g, "l_kmin"))
                    for n in range(2):
                        kk = bank[g][2 + n][:].rearrange("p (b n) -> p b n", b=2)[:, :, 0:P]
                        last = dve.scalar_tensor_tensor(A[1][g][:, 2 * n:2 * n + 2, :], kk, 1.0,
                                                        A[5][g][:, 2 * n:2 * n + 2, :], ALU.add, ALU.max)
                    last.then_inc(sig("l_kf", g), 1)

                def l_heads(g):
                    dve.wait_ge(*at(i, g, "l_kv"))
                    for n in range(2):
                        kv = bank[g][2 + n][:].rearrange("p (b n) -> p b n", b=2)
                        last = dve.tensor_tensor(r144[g][:, 2 * n:2 * n + 2, 0:P], kv[:, :, 0:P],
                                                 spread(head_mask[:], 1, 2), ALU.mult)
                    last.then_inc(sig("l_kvm", g), 1)
                    for n in range(2):
                        kv = bank[g][2 + n][:].rearrange("p (b n) -> p b n", b=2)
                        last = dve.tensor_tensor(r144[g][:, 2 * n:2 * n + 2, P:P + NH],
                                                 kv[:, :, P:P + 1].broadcast_to((P, 2, NH)),
                                                 spread(head_cols[:], 1, 2), ALU.mult)
                    last.then_inc(sig("l_zm", g), 1)

                def l_div(g):
                    dve.wait_ge(*at(i, g, "l_num"))
                    den = sm[0][g][:].rearrange("p (b h) -> p b h", b=GB)
                    for n in range(2):
                        kv = bank[g][n][:].rearrange("p (b n) -> p b n", b=2)
                        last = dve.tensor_scalar(den[:, 2 * n:2 * n + 2, :], kv[:, :, P:P + NH], DEN_EPS, None, ALU.add)
                    last.then_inc(sig("l_den", g), 1)
                    dve.wait_ge(*at(i, g, "l_den"))
                    dve.reciprocal(sm[1][g][:], sm[0][g][:]).then_inc(sig("l_rec", g), 1)
                    dve.wait_ge(*at(i, g, "l_rec"))
                    rec = sm[1][g][:].rearrange("p (b h) -> p b h", b=GB)
                    for n in range(2):
                        kv = bank[g][n][:].rearrange("p (b n) -> p b n", b=2)
                        last = dve.tensor_tensor(
                            A[2][g][:, 2 * n:2 * n + 2, :].rearrange("p b (h q) -> p b h q", h=NH),
                            kv[:, :, 0:P].rearrange("p b (h q) -> p b h q", h=NH),
                            spread(rec[:, 2 * n:2 * n + 2, :], 3, HD), ALU.mult)
                    last.then_inc(sig("l_att", g), 1)

                def x_kparts(g):
                    dve.wait_ge(*at(i, g, "x_v"))
                    dve.wait_ge(*at(i, g, "x_zero"))
                    for c in range(4):
                        spot = VM[g][:, :, c::4, HD * c:HD * c + HD]
                        last = dve.tensor_tensor(
                            spot, bank[g][1][:].rearrange("p (b m c q) -> p b m c q", b=GB, m=4, c=4)[:, :, :, c],
                            spread(bcast["xbv"][:].rearrange("p (m c q) -> p m c q", m=4, c=4)[:, :, c], 1, GB), ALU.add)
                    last.then_inc(sig("x_v_sb", g), 1)
                    split(g, "k", 3, A[1], A[2])

                def split(g, side, n, full, rest):
                    dve.wait_ge(*at(i, g, f"x_{side}_h"))
                    dve.tensor_tensor(flat(rest[g]), flat(full[g]), PARTS[n][g], ALU.subtract)\
                       .then_inc(sig(f"x_{side}_r1", g), 1)
                    dve.wait_ge(*at(i, g, f"x_{side}_r1"))
                    dve.tensor_copy(PARTS[n + 1][g], flat(rest[g])).then_inc(sig(f"x_{side}_m", g), 1)
                    dve.wait_ge(*at(i, g, f"x_{side}_m"))
                    dve.tensor_tensor(PARTS[n + 2][g], flat(rest[g]), PARTS[n + 1][g], ALU.subtract)\
                       .then_inc(sig(f"x_{side}_l", g), 1)

                def x_qparts(g):
                    split(g, "q", 0, A[0], A[3])

                def x_max(g):
                    for n in range(4 * GB):
                        b, c = n // 4, n % 4
                        dve.wait_ge(counted["x_a"], nth(i, g, "x_a", n))
                        rsum(sm[0][g][:, b * NH + 4 * c:b * NH + 4 * c + 4], seqs(bank[g][n % 4][:]), ALU.max,
                             negate=True).then_inc(counted["x_amax"], 1)

                def x_shift(g):
                    dve.wait_ge(*at(i, g, "x_nmt"))
                    dve.tensor_copy(nmp[0][g][:], bank[g][0][0:NH, :]).then_inc(sig("x_nm_h", g), 1)
                    dve.wait_ge(*at(i, g, "x_nm_h"))
                    dve.tensor_tensor(nmp[1][g][:], bank[g][0][0:NH, :], nmp[0][g][:], ALU.subtract)\
                       .then_inc(sig("x_nm_l", g), 1)

                def x_div(g):
                    dve.wait_ge(counted["x_pv"], nth(i, g, "x_pv", 4 * GB - 1))
                    dve.reciprocal(A[2][g], seqs(bank[g][3][:])).then_inc(sig("x_rden", g), 1)
                    dve.wait_ge(*at(i, g, "x_rden"))
                    dve.tensor_tensor(A[3][g], seqs(bank[g][2][:]), A[2][g], ALU.mult).then_inc(sig("x_att", g), 1)

                def e_rank(g):
                    dve.wait_ge(*at(i, g, "e_g"))
                    dve.tensor_copy(sm[0][g][:, 0:24], bank[g][2][:, 0:24]).then_inc(sig("e_g_sb", g), 1)
                    dve.wait_ge(*at(i, g, "e_g_sb"))
                    lg = sm[0][g][:, 0:24].rearrange("p (b e) -> p b e", b=GB)
                    above = HFW[g][:, 0, 0:144].rearrange("p (b e j) -> p b e j", b=GB, e=NE1)
                    equal = HFW[g][:, 1, 0:144].rearrange("p (b e j) -> p b e j", b=GB, e=NE1)
                    mine, other = spread(lg, 3, NE1), spread(lg, 2, NE1)
                    dve.tensor_tensor(above, other, mine, ALU.is_gt).then_inc(sig("e_above", g), 1)
                    dve.tensor_tensor(equal, other, mine, ALU.is_equal).then_inc(sig("e_equal", g), 1)
                    dve.wait_ge(*at(i, g, "e_equal"))
                    dve.tensor_tensor(equal, equal, spread(before[:], 1, GB), ALU.mult).then_inc(sig("e_tied", g), 1)
                    dve.wait_ge(*at(i, g, "e_tied"))
                    dve.tensor_tensor(above, above, equal, ALU.add).then_inc(sig("e_rank1", g), 1)
                    dve.wait_ge(*at(i, g, "e_rank1"))
                    rank = sm[1][g][:, 0:24].rearrange("p (b e) -> p b e", b=GB)
                    rsum(rank, above).then_inc(sig("e_rank", g), 1)
                    dve.wait_ge(*at(i, g, "e_rank"))
                    dve.tensor_scalar(sm[2][g][:, 0:24], sm[1][g][:, 0:24], 2.0, None, ALU.is_lt)\
                       .then_inc(sig("e_sel", g), 1)
                    rsum(sm[3][g][:, 0:GB], lg, ALU.max).then_inc(sig("e_max", g), 1)
                    dve.wait_ge(*at(i, g, "e_max"))
                    dve.tensor_tensor(sm[4][g][:, 0:24].rearrange("p (b e) -> p b e", b=GB), lg,
                                      spread(sm[3][g][:, 0:GB], 2, NE1), ALU.subtract).then_inc(sig("e_sub", g), 1)

                def e_comb(g):
                    dve.wait_ge(*at(i, g, "e_exp"))
                    dve.tensor_tensor(sm[1][g][:, 0:24], sm[5][g][:, 0:24], sm[2][g][:, 0:24], ALU.mult)\
                       .then_inc(sig("e_msel", g), 1)
                    dve.wait_ge(*at(i, g, "e_msel"))
                    ex = sm[1][g][:, 0:24].rearrange("p (b e) -> p b e", b=GB)
                    rsum(sm[3][g][:, 0:GB], ex).then_inc(sig("e_sum", g), 1)
                    dve.wait_ge(*at(i, g, "e_sum"))
                    dve.reciprocal(sm[4][g][:, 0:GB], sm[3][g][:, 0:GB]).then_inc(sig("e_rec", g), 1)
                    dve.wait_ge(*at(i, g, "e_rec"))
                    dve.tensor_tensor(sm[6][g][:, 0:24].rearrange("p (b e) -> p b e", b=GB), ex,
                                      spread(sm[4][g][:, 0:GB], 2, NE1), ALU.mult).then_inc(sig("e_comb", g), 1)

                def e_acc0(g):
                    dve.wait_ge(*at(i, g, "e_b2"))
                    dve.tensor_tensor(flat(R[g]), bank[g][3][:], flat(X[g]), ALU.add).then_inc(sig("e_acc0", g), 1)

                def e_acc(g):
                    for e in range(NE1):
                        dve.wait_ge(counted["e_down"], nth(i, g, "e_down", e))
                        if e:
                            dve.wait_ge(counted["e_acc"], nth(i, g, "e_acc", e - 1))
                        else:
                            dve.wait_ge(*at(i, g, "e_acc0"))
                        for b in range(GB):
                            last = dve.scalar_tensor_tensor(
                                R[g][:, b, :], bank[g][2 + e % 2][:, b * P:(b + 1) * P],
                                sm[6][g][:, b * NE1 + e:b * NE1 + e + 1], R[g][:, b, :], ALU.mult, ALU.add)
                        last.then_inc(sig("n5_res", g) if e == NE1 - 1 else counted["e_acc"], 1)

                for step in (m_stats, m_norm, c_mask, m_conv, m_silu, m_gram, m_dt_one, m_dt, m_gates, m_mix, m_skip,
                             m_res, norm_stats(0), norm_rows(0), c_max, c_rsum, c_pt, c_res, norm_stats(1),
                             norm_rows(1), f_max, f_prob, f_top, f_index, f_onehot, f_gathered, f_res, norm_stats(2),
                             norm_rows(2), l_feat, l_heads, l_div, x_kparts, res(3, 3, "l_out", "l_resid"),
                             norm_stats(3), norm_rows(3), x_qparts, x_max, x_shift, x_div,
                             res(4, 0, "x_out", "x_resid"), norm_stats(4), norm_rows(4), e_rank, e_comb, e_acc0,
                             e_acc, norm_stats(5), norm_rows(5)):
                    for g in range(LANES):
                        step(g)

        @block.scalar
        def _(act):
            act.wait_ge(weights_in, 16 * n_weights)
            act.activation(neg_a_exp[:], bcast["negA"][:], ACT.Exp).then_inc(scaled, 1)
            act.wait_ge(constants, N_CONSTANTS)
            with act.Fori(0, pairs, 1) as i:
                def move(dst, k, step, produced, bias=None, scale=1.0, rows=P):
                    def run(g):
                        act.wait_ge(*at(i, g, produced))
                        kw = {} if bias is None else {"bias": bias}
                        act.activation(dst(g), bank[g][k][0:rows, :], ACT.Identity if bias is not None else ACT.Copy,
                                       scale=scale, **kw).then_inc(sig(step, g), 1)
                    return run

                def m_xt(g):
                    act.wait_ge(*at(i, g, "m_xt"))
                    act.activation(flat(T[g]), bank[g][0][:], ACT.Copy, scale=wt["normw"][:, 0:1])\
                       .then_inc(sig("m_xt_sb", g), 1)

                def m_tanh(g):
                    for c in range(2):
                        act.wait_ge(*at(i, g, f"m_tap{c}3"))
                        act.activation(HFW[g][:, 1 + c, :], A47[g][:, 2 + c, :], ACT.Tanh, scale=0.5)\
                           .then_inc(sig(f"m_tanh{c}", g), 1)

                def m_dt_exp(g):
                    act.wait_ge(*at(i, g, "m_dt_abs"))
                    act.activation(sm[2][g][:, 0:16], sm[1][g][:, 0:16], ACT.Exp, scale=-1.0)\
                       .then_inc(sig("m_dt_exp", g), 1)

                def m_dt_ln(g):
                    act.wait_ge(*at(i, g, "m_dt_one"))
                    act.activation(sm[1][g][:, 0:16], sm[3][g][:, 0:16], ACT.Ln).then_inc(sig("m_dt_ln", g), 1)

                def m_tz(g):
                    for c in range(2):
                        act.wait_ge(*at(i, g, f"m_z{c}"))
                        act.activation(HFW[g][:, 3 if c == 0 else 1, :], bank[g][1 + c][:], ACT.Tanh, scale=0.5)\
                           .then_inc(sig(f"m_tz{c}", g), 1)

                def m_l(g):
                    for b in range(GB):
                        act.wait_ge(counted["m_seg"], nth(i, g, "m_seg", b))
                        if b >= 2:
                            act.wait_ge(counted["m_mix"], nth(i, g, "m_mix", b - 2))
                        act.activation(HFW[g][:, 2 + b % 2, :], bank[g][b % 2][:], ACT.Exp).then_inc(counted["m_l"], 1)

                def c_exp(g):
                    act.wait_ge(*at(i, g, "c_max"))
                    for b in range(GB):
                        last = act.activation(A[2][g][:, b, :], bank[g][2][:, b * P:(b + 1) * P], ACT.Exp,
                                              bias=sm[0][g][:, b:b + 1], accum_out=sm[1][g][:, b:b + 1])
                    last.then_inc(sig("c_exp", g), 1)

                def f_gexp(g):
                    act.wait_ge(*at(i, g, "f_gsub"))
                    act.activation(sm[3][g][:, 0:32], sm[1][g][:, 0:32], ACT.Exp).then_inc(sig("f_gexp", g), 1)

                def f_gathered(g):
                    act.wait_ge(*at(i, g, "f_xi"))
                    act.activation(expert_cols(g, 1), bank_experts(g, 1), ACT.Copy).then_inc(sig("f_xi_sb1", g), 1)

                def f_gelu(g):
                    for e in range(NE0):
                        act.wait_ge(counted["f_up"], nth(i, g, "f_up", e))
                        act.activation(HTW[g][:, e % 2, :], bank[g][e % 2][:], ACT.Gelu_apprx_tanh)\
                           .then_inc(counted["f_act"], 1)
                        if e == 4:
                            move(lambda g: A03[g][:, 2, :], 2, "f_y_sb0", "f_down0")(g)
                    move(lambda g: A03[g][:, 3, :], 3, "f_y_sb1", "f_down1")(g)

                def l_exps(g):
                    act.wait_ge(*at(i, g, "l_q"))
                    act.activation(A47[g][:, 0, :], bank[g][1][:], ACT.Exp).then_inc(sig("l_eq", g), 1)
                    for n in range(2):
                        act.wait_ge(*at(i, g, f"l_kv{n}"))
                        kv = bank[g][2 + n][:].rearrange("p (b n) -> p b n", b=2)
                        last = act.activation(A[5][g][:, 2 * n:2 * n + 2, :], kv[:, :, 0:P], ACT.Exp)
                    last.then_inc(sig("l_ek", g), 1)
                    act.wait_ge(*at(i, g, "f_add"))
                    for n in range(2):
                        kv = bank[g][2 + n][:].rearrange("p (b n) -> p b n", b=2)
                        act.activation(vx[g][:, 2 * n:2 * n + 2, 0:P], kv[:, :, P:2 * P], ACT.Copy)
                    act.activation(vx[g][:, :, P:P + 1], ones4[:], ACT.Copy).then_inc(sig("l_v", g), 1)

                def x_k(g):
                    move(lambda g: A03[g][:, 1, :], 0, "x_k_sb", "x_k", wt["xbk1"][:, 0:1])(g)
                    act.wait_ge(*at(i, g, "x_k_sb"))
                    act.activation(PARTS[3][g], A03[g][:, 1, :], ACT.Copy).then_inc(sig("x_k_h", g), 1)

                def x_q(g):
                    move(lambda g: A03[g][:, 0, :], 3, "x_q_sb", "x_q", wq_scaled_bias[:, 0:1], HD ** -0.5)(g)
                    act.wait_ge(*at(i, g, "x_q_sb"))
                    act.activation(PARTS[0][g], A03[g][:, 0, :], ACT.Copy).then_inc(sig("x_q_h", g), 1)

                def x_p(g):
                    for n in range(4 * GB):
                        act.wait_ge(counted["x_b"], nth(i, g, "x_b", n))
                        if n >= 2:
                            act.wait_ge(counted["x_pv"], nth(i, g, "x_pv", n - 2))
                        act.activation(PTW[g][:, n % 2, :], bank[g][n % 2][:], ACT.Exp).then_inc(counted["x_p"], 1)

                def e_exp(g):
                    act.wait_ge(*at(i, g, "e_sub"))
                    act.activation(sm[5][g][:, 0:24], sm[4][g][:, 0:24], ACT.Exp).then_inc(sig("e_exp", g), 1)

                def e_gelu(g):
                    for e in range(NE1):
                        for f in range(FT1):
                            n = FT1 * e + f
                            act.wait_ge(counted["e_up"], nth(i, g, "e_up", n))
                            if e >= 2:
                                act.wait_ge(counted["e_down"], nth(i, g, "e_down", e - 2))
                            act.activation(HFW[g][:, 2 * (e % 2) + f, :], bank[g][n % 2][:], ACT.Gelu,
                                           bias=wt["b1"][:, n:n + 1]).then_inc(counted["e_act"], 1)

                def tile_of(n):
                    return lambda g: A03[g][:, n, :] if n < 4 else A47[g][:, n - 4, :]

                t_of = lambda g: flat(T[g])
                for step in (m_xt, move(tile_of(0), 3, "m_b_sb", "m_b"), move(tile_of(1), 0, "m_c_sb", "m_c"),
                             move(lambda g: g8[g][0:HS, :], 3, "m_dtt_sb", "m_dtt", wt["dtb"][:, 0:1], rows=HS),
                             m_tanh, m_dt_exp, m_dt_ln, m_tz, m_l,
                             move(tile_of(0), 3, "c_kt_sb", "c_kt", wt["xbk0"][:, 0:1]), move(t_of, 0, "c_xt_sb", "c_xt"),
                             move(tile_of(1), 1, "c_q_sb", "c_q", wt["xbq0"][:, 0:1]), c_exp,
                             move(tile_of(4), 0, "c_ot_sb", "c_ot"), move(t_of, 0, "f_xt_sb", "f_xt"),
                             move(lambda g: g8[g][0:NE0, :], 1, "f_gt_sb", "f_gt", rows=NE0), f_gexp, f_gathered,
                             f_gelu, move(lambda g: B16[g][:], 0, "f_add_sb", "f_add"),
                             move(t_of, 0, "l_xt_sb", "l_xt"), l_exps, move(tile_of(3), 2, "l_at_sb", "l_at"),
                             x_k, move(t_of, 2, "x_xt_sb", "x_xt"), x_q, x_p, move(t_of, 0, "e_xt_sb", "e_xt"),
                             move(lambda g: g8[g][0:NE1, :], 1, "e_gt_sb", "e_gt", wt["bg"][:, 0:1], rows=NE1), e_exp,
                             move(lambda g: cT[g], 2, "e_ct_sb", "e_ct", rows=NE1), e_gelu):
                    for g in range(LANES):
                        step(g)

        @block.gpsimd
        def _(pool):
            step_of = [0]

            def const(ins, wait=False):
                ins.then_inc(constants, 1)

            def made(ins):
                step_of[0] += 1
                ins.then_inc(pool_made, 1)
                pool.wait_ge(pool_made, step_of[0])

            def fill(tile_, value):
                made(pool.memset(tile_, value))

            def keep(tile_, pattern, compare, base, channel, fill_=0.0):
                made(pool.affine_select(out=tile_, in_=tile_, pattern=pattern, compare_op=compare, fill=fill_,
                                        base=base, channel_multiplier=channel))

            for t in (ident, tri, strict, head_mask, head_cols):
                fill(t[:], 1.0)
            keep(ident[:], [[1, P]], ALU.is_equal, 0, -1)
            keep(tri[:], [[1, P]], ALU.is_ge, 0, -1)
            keep(strict[:], [[-1, P]], ALU.is_gt, 0, 1)
            heads = head_mask[:].rearrange("p (h q) -> p h q", h=NH)
            keep(heads, [[-HD, NH], [0, HD]], ALU.is_ge, 0, 1)
            keep(heads, [[HD, NH], [0, HD]], ALU.is_ge, HD - 1, -1)
            keep(head_cols[:], [[-HD, NH]], ALU.is_ge, 0, 1)
            keep(head_cols[:], [[HD, NH]], ALU.is_ge, HD - 1, -1)
            fill(ones_of_head[:], 0.0)
            for c in range(4):
                fill(ones_of_head[:, c, HD * c:HD * c + HD], 1.0)
            made(pool.iota(tok_id[:], pattern=[[0, 1]], base=0, channel_multiplier=1,
                           allow_small_or_imprecise_dtypes=True))
            made(pool.iota(tok_row[:], pattern=[[1, P]], base=0, channel_multiplier=0,
                           allow_small_or_imprecise_dtypes=True))
            fill(own_col[:], 1.0)
            keep(own_col[:].rearrange("p (e b) -> p e b", b=GB), [[-1, NE0], [-NE0, GB]], ALU.is_equal, 0, 1)
            fill(own_row[:], 1.0)
            keep(own_row[:], [[-NE0, GB], [-4, 2]], ALU.is_ge, 0, 1)
            keep(own_row[:], [[NE0, GB], [4, 2]], ALU.is_ge, 3, -1)
            fill(own_quarter[:], 0.0)
            for m in range(NE0):
                keep(own_quarter[:], [[-1, 4]], ALU.not_equal, -4 * m, 1, 1.0)
            fill(before[:], 1.0)
            keep(before[:], [[1, NE1], [-1, NE1]], ALU.is_gt, 0, 0)
            fill(ones4[:], 1.0)
            pool.memset(spare[:, 0:1], 0.0).then_inc(constants, 1)
            for g in range(LANES):
                pool.memset(spare[:, g + 1:g + 2], 0.0).then_inc(lane_free[g], 16)

            pool.wait_ge(constants, N_CONSTANTS)
            with pool.Fori(0, pairs, 1) as i:
                def rstd(name, produced):
                    def step(g):
                        pool.wait_ge(*at(i, g, produced))
                        pool.tensor_tensor(sm[6][g][:, 0:GB], sm[7][g][:, 0:GB], neg_half[:], ALU.pow)\
                            .then_inc(sig(name, g), 1)
                    return step

                def m_twice(g):
                    pool.wait_ge(*at(i, g, "m_xt_sb"))
                    apart(pool)
                    pool.tensor_scalar(flat(R[g]), flat(X[g]), 2.0, 0.0, ALU.mult, ALU.add)\
                        .then_inc(sig("m_twice", g), 1)

                def m_rd(g):
                    pool.wait_ge(*at(i, g, "m_decay"))
                    for b in range(GB):
                        if b >= 2:
                            pool.wait_ge(counted["m_seg"], nth(i, g, "m_seg", b - 2))
                        apart(pool)
                        for h in range(HS):
                            last = pool.tensor_scalar(PT[b % 2][g][:, h, :], tri[:],
                                                      sm[5][g][:, b * HS + h:b * HS + h + 1], 0.0, ALU.mult, ALU.add)
                        last.then_inc(counted["m_rd"], 1)

                def resid(name, ready, bias):
                    def step(g):
                        pool.wait_ge(*at(i, g, ready))
                        pool.tensor_tensor(R[g][:], X[g][:], spread(bcast[bias][:], 1, GB), ALU.add)\
                            .then_inc(sig(name, g), 1)
                    return step

                def x_zero(g):
                    pool.wait_ge(*at(i, g, "l_kf"))
                    apart(pool)
                    pool.memset(A47[g][:].rearrange("p b n -> p (b n)"), 0.0).then_inc(sig("x_zero", g), 1)

                for step in (rstd("m_rstd", "m_ms"), m_twice, m_rd, rstd("n0_rstd", "n0_eps"),
                             resid("c_resid", "n0_done", "xbo0"), rstd("n1_rstd", "n1_eps"),
                             rstd("n2_rstd", "n2_eps"), resid("l_resid", "n2_done", "lbo"), x_zero,
                             rstd("n3_rstd", "n3_eps"), resid("x_resid", "n3_done", "xbo1"),
                             rstd("n4_rstd", "n4_eps"), rstd("n5_rstd", "n5_eps")):
                    for g in range(LANES):
                        step(g)


def kernel(**a):
    import numpy as np
    import concourse.bacc as bacc
    from concourse.bass_utils import run_bass_kernel_spmd

    f = {k: np.asarray(v) for k, v in a.items()}
    col = lambda v: v.reshape(-1, 1)
    rows = lambda v, n: v.reshape(n, P, -1).transpose(1, 0, 2)
    order = np.array([HD * (4 * (pos % 4) + pos // 4) + d for d in range(HD) for pos in range(NH)])
    w = {
        "normw": col(f["L0_attn_norm_w"]), "inT": f["L0_attn_in_proj_w"].T,
        "convw": rows(f["L0_attn_conv_w"], 2), "convb": rows(f["L0_attn_conv_b"], 2)[:, :, 0],
        "negA": f["L0_attn_A_log"], "D2": np.repeat(f["L0_attn_D"], PD).reshape(2, P).T,
        "dtb": col(f["L0_attn_dt_bias"]), "outT": rows(f["L0_attn_out_proj_w"].T, 2),
        "wq0": f["L0_xattn_Wq"].T, "xbq0": col(f["L0_xattn_bq"]), "wk0": f["L0_xattn_Wk"].T,
        "xbk0": col(f["L0_xattn_bk"]), "wo0": f["L0_xattn_Wo"].T, "xbo0": f["L0_xattn_bo"],
        "gate": f["L0_ffn_gate_w"], "w1": f["L0_ffn_w1"].transpose(1, 0, 2),
        "w2": f["L0_ffn_w2"].reshape(NE0, FT0, P, P).transpose(2, 0, 1, 3),
        "lqkv": f["L1_attn_W_qkv"], "lout": f["L1_attn_W_out"], "lbo": f["L1_attn_b_out"],
        "wq1": f["L1_xattn_Wq"][order].T, "xbq1": col(f["L1_xattn_bq"][order]),
        "wk1": f["L1_xattn_Wk"][order].T, "xbk1": col(f["L1_xattn_bk"][order]),
        "wv1": f["L1_xattn_Wv"].T, "xbv": f["L1_xattn_bv"], "wo1": f["L1_xattn_Wo"].T, "xbo1": f["L1_xattn_bo"],
        "wg": f["L1_ffn_Wg"], "bg": col(f["L1_ffn_bg"]), "we1": f["L1_ffn_W1"].transpose(1, 0, 2),
        "b1": f["L1_ffn_b1"].reshape(NE1 * FT1, P).T,
        "we2": f["L1_ffn_W2"].reshape(NE1, FT1, P, P).transpose(2, 0, 1, 3), "b2": f["L1_ffn_b2"],
    }
    x, ctx = f["x"], f["ctx_1024"]
    nb = x.shape[0]
    arrays = {
        "in_x": x.transpose(1, 0, 2).reshape(P, nb * P), "in_ctx": ctx.transpose(1, 0, 2).reshape(P, nb * P),
        "in_ctxT": ctx.transpose(2, 0, 1).reshape(P, nb * P),
        "in_mask": f["mask_BxS2_bk0"].reshape(1, nb * P),
    }
    arrays.update({"in_w_" + k: v for k, v in w.items()})
    arrays = {k: np.ascontiguousarray(v) for k, v in arrays.items()}
    nc = bacc.Bacc("TRN2", target_bir_lowering=False, num_devices=1)
    t = {k: nc.dram_tensor(k, v.shape, mybir.dt.from_np(v.dtype), kind="ExternalInput").ap() for k, v in arrays.items()}
    out = nc.dram_tensor("out", (P, nb * P), F32, kind="ExternalOutput").ap()
    decoder(nc, t["in_x"], t["in_ctx"], t["in_ctxT"], t["in_mask"], {k: t["in_w_" + k] for k in w}, out)
    r = run_bass_kernel_spmd(nc, [arrays], core_ids=[0])
    y = r.results[0]["out"]
    return y.reshape(P, nb, P).transpose(1, 0, 2)
```

```python
from contextlib import ExitStack

import concourse.bass as bass
from concourse import mybir

ALU = mybir.AluOpType
ACT = mybir.ActivationFunctionType
AX = mybir.AxisListType
F32 = mybir.dt.float32
BF16 = mybir.dt.bfloat16
U8 = mybir.dt.uint8
U32 = mybir.dt.uint32

P = 128
GB = 4
W = GB * P
LANES = 2
HS, PD = 4, 64
NE0, HID0, CAP = 8, 512, 32
FT0 = HID0 // P
NH, HD = 16, 8
NE1, HID1 = 6, 256
FT1 = HID1 // P
SLOTS = 6
KROWS = SLOTS * HD
SHIFT0 = 2 * KROWS
SROWS = SHIFT0 + 4
MASKED = -1e30
LN_EPS, RMS_EPS, DEN_EPS = 1e-5, 1e-6, 1e-6
TINY = 2.0 ** -26
N_CONSTANTS = 6 + 2 * LANES

WEIGHTS = {
    "short": "negA normw D2 dtb convw convb xbq0 xbk0 xbo0 lbo xbq1 xbk1 xbv xbo1 bg b1 b2",
    "mamba": "inT outT",
    "cross": "wq0 wk0 wo0",
    "choice": "gate w1 w2",
    "linear": "lqkv lout",
    "heads": "wq1 wk1 wv1 wo1",
    "mixture": "wg we1 we2",
}

SEQUENCES = {
    "mamba_pe": "m_xt m_xs0 m_xs1 m_b m_c m_dtt m_gram m_dt m_z0 m_z1 m_xhr0 m_xhr1 m_out",
    "mamba_act": "m_xt_sb m_b_sb m_c_sb m_dtt_sb m_tanh0 m_tanh1 m_dt_exp m_dt_ln m_tz0 m_tz1",
    "mamba_dve": "m_stats m_moments m_sq m_ms m_norm m_tap00 m_tap01 m_tap02 m_tap03 m_tap10 m_tap11 m_tap12 m_tap13"
                 " m_xh0 m_xh1 m_gram_sb m_dt_sb m_dt_abs m_dt_one m_dt_den m_dt_rec m_dt_ratio m_dt_log1p m_dt_done"
                 " m_decay m_half m_sz0 m_sz1 m_dtx0 m_dtx1 m_skip0 m_skip1 m_gate0 m_gate1",
    "norm_dve": " ".join(f"n{n}_res n{n}_stats n{n}_mom n{n}_eps n{n}_done" for n in range(6)),
    "norm_pool": "m_rstd n0_rstd n1_rstd n2_rstd n3_rstd n4_rstd n5_rstd",
    "cross_pe": "c_kt c_xt c_q c_scores c_pt c_ot c_out",
    "cross_act": "c_kt_sb c_xt_sb c_q_sb c_exp c_ot_sb",
    "cross_dve": "c_mask c_max c_rsum c_pt_sb",
    "resid_pool": "m_twice c_resid l_resid x_resid",
    "choice_pe": "f_xt f_gt f_g f_pt f_bc f_rows f_xi f_add",
    "choice_act": "f_xt_sb f_gt_sb f_gexp f_xi_sb1 f_y_sb0 f_y_sb1 f_add_sb",
    "choice_dve": "f_gmax f_gsub f_gsum f_grec f_prob f_pt_sb"
                  + "".join(f" f_topv{r} f_topi{r} f_topw{r}" for r in range(CAP // 8)) + " f_idx f_idxm f_rowsel f_onehot f_xi_sb0 f_rows_sb f_scat",
    "linear_pe": "l_xt l_q l_kv0 l_kv1 l_kv l_num l_at l_out",
    "linear_act": "l_xt_sb l_eq l_ek l_v l_at_sb",
    "linear_dve": "l_qmin l_qf l_kmin l_kf l_kvm l_zm l_den l_rec l_att",
    "heads_pe": "x_k x_v x_xt x_q x_nmt x_out",
    "heads_act": "x_k_sb x_k_h x_xt_sb x_q_sb x_q_h",
    "heads_dve": "x_v_sb x_k_r1 x_k_m x_k_l x_q_r1 x_q_m x_q_l x_nm_h x_nm_l x_rden x_att",
    "heads_pool": "x_zero",
    "mixture_pe": "e_xt e_gt e_g e_ct e_b2",
    "mixture_act": "e_xt_sb e_gt_sb e_exp e_ct_sb",
    "mixture_dve": "e_g_sb e_above e_equal e_tied e_rank1 e_rank e_sel e_max e_sub e_msel e_sum e_rec e_comb e_acc0",
}
COUNTED = {"m_rd": GB, "m_seg": GB, "m_yb": GB, "m_l": GB, "m_mix": GB, "f_up": NE0, "f_act": NE0, "f_down": NE0,
           "x_a": 4 * GB, "x_amax": 4 * GB, "x_b": 4 * GB, "x_p": 4 * GB, "x_pv": 4 * GB,
           "e_up": NE1 * FT1, "e_act": NE1 * FT1, "e_down": NE1, "e_acc": NE1 - 1}


PERIOD, LAG = 243.62, 15


def schedule(steps):
    assert all(a[0] <= b[0] for a, b in zip(steps, steps[1:]))
    first = [(step, 0, 0) for due, step in steps if due < LAG]
    turns = [(due + (PERIOD if due < LAG else 0), 0, int(due < LAG), step) for due, step in steps]
    turns += [(due + LAG, 1, 0, step) for due, step in steps]
    steady = [(step, g, ahead) for _, g, ahead, step in sorted(turns, key=lambda turn: turn[:2])]
    return first, steady, [turn for turn in steady if not turn[2]]


def decoder(nc, x, ctx_r, ctx_t, mask, w, out):
    pairs = x.shape[1] // (W * LANES)
    stack = ExitStack()

    def sb(name, shape, dt=F32):
        return stack.enter_context(nc.sbuf_tensor(name, shape, dt))

    with stack:
        sequence = {q: [stack.enter_context(nc.semaphore(f"{q}{g}")) for g in range(LANES)] for q in SEQUENCES}
        counted = {name: [stack.enter_context(nc.semaphore(f"{name}_{g}")) for g in range(LANES)] for name in COUNTED}
        constants = stack.enter_context(nc.semaphore("constants"))
        scaled = stack.enter_context(nc.semaphore("scaled"))
        home = {step: (q, n) for q, steps in SEQUENCES.items() for n, step in enumerate(steps.split())}
        taken = {(q, g): 0 for q in SEQUENCES for g in range(LANES)}

        def at(i, g, step):
            q, n = home[step]
            return sequence[q][g], i * len(SEQUENCES[q].split()) + (n + 1)

        def sig(step, g):
            q, _ = home[step]
            steps = SEQUENCES[q].split()
            assert step == steps[taken[q, g] % len(steps)], step
            taken[q, g] += 1
            return sequence[q][g]

        def run(eng, steps):
            def take(turns, i):
                for step, g, ahead in turns:
                    step(i + 1 if ahead else i, g)

            first, steady, last = schedule(steps)
            take(first, 0)
            if pairs > 1:
                with eng.Fori(0, pairs - 1, 1) as i:
                    take(steady, i)
            take(last, pairs - 1)

        weights_in = {part: stack.enter_context(nc.semaphore(f"weights_in_{part}")) for part in WEIGHTS}
        x_in = [stack.enter_context(nc.semaphore(f"x_in{g}")) for g in range(LANES)]
        ctx_in = [stack.enter_context(nc.semaphore(f"ctx_in{g}")) for g in range(LANES)]
        rows_moved = [stack.enter_context(nc.semaphore(f"rows_moved{g}")) for g in range(LANES)]
        rows_out = [[stack.enter_context(nc.semaphore(f"rows_out{g}{half}")) for half in range(2)] for g in range(LANES)]
        q_out = [stack.enter_context(nc.semaphore(f"q_out{g}")) for g in range(LANES)]
        q_in = [stack.enter_context(nc.semaphore(f"q_in{g}")) for g in range(LANES)]
        k_out = [stack.enter_context(nc.semaphore(f"k_out{g}")) for g in range(LANES)]
        k_in = [stack.enter_context(nc.semaphore(f"k_in{g}")) for g in range(LANES)]
        shift_out = [stack.enter_context(nc.semaphore(f"shift_out{g}")) for g in range(LANES)]
        shift_in = [stack.enter_context(nc.semaphore(f"shift_in{g}")) for g in range(LANES)]
        lane_free = [stack.enter_context(nc.semaphore(f"lane_free{g}")) for g in range(LANES)]

        wt = {name: sb("w_" + name, list(ap.shape)) for name, ap in w.items()
              if name not in ("xbo0", "xbo1", "lbo", "xbv", "negA")}
        bcast = {name: sb("w_" + name, [P, ap.shape[0]]) for name, ap in w.items()
                 if name in ("xbo0", "xbo1", "lbo", "xbv", "negA")}

        def loaded(part):
            return weights_in[part], 16 * len(WEIGHTS[part].split())

        ident = sb("ident", [P, P])
        tri = sb("tri", [P, P])
        strict = sb("strict", [P, P])
        ones_row = sb("ones_row", [32, P], BF16)
        head_mask = sb("head_mask", [P, P])
        head_cols = sb("head_cols", [P, NH])
        ones_of_head = sb("ones_of_head", [P, 4, 32])
        tok_id = sb("tok_id", [P, 1])
        tok_row = sb("tok_row", [P, P])
        own_col = sb("own_col", [32, 32])
        own_quarter = sb("own_quarter", [32, 4])
        own_row = sb("own_row", [32, GB, 2])
        before = sb("before", [P, NE1, NE1])
        neg_half = sb("neg_half", [P, GB])
        a_half = sb("a_half", [P, 2])
        neg_a = sb("neg_a", [P, HS])
        wq_scaled_bias = sb("wq_scaled_bias", [P, 1])
        neg_a_exp = sb("neg_a_exp", [P, HS])
        ones4 = sb("ones4", [P, GB, 1])
        spare = sb("spare", [P, 1 + LANES])
        pool_made = stack.enter_context(nc.semaphore("pool_made"))

        def lane(name, shape, dt=F32):
            return [sb(f"{name}{g}", shape, dt) for g in range(LANES)]

        def seqs(ap):
            return ap.rearrange("p (b n) -> p b n", b=GB)

        def flat(ap):
            return (ap if isinstance(ap, bass.AP) else ap[:]).rearrange("p b n -> p (b n)")

        def spread(ap, axis, count):
            v = ap.unsqueeze(axis)
            return v.broadcast_to(tuple(v.shape[:axis]) + (count,) + tuple(v.shape[axis + 1:]))

        X = lane("X", [P, GB, P])
        CR = lane("CR", [P, GB, P])
        CT = lane("CT", [P, GB, P])
        MK = lane("MK", [1, W], U8)
        MB = lane("MB", [1, W], BF16)
        R = lane("R", [P, GB, P])
        T = lane("T", [P, GB, P])
        A03 = lane("A03_", [P, 4, W])
        A47 = lane("A47_", [P, 4, W])
        A = [[seqs((A03 if n < 4 else A47)[g][:, n % 4, :]) for g in range(LANES)] for n in range(8)]
        VM = [A47[g][:].rearrange("p b (h m) -> p b h m", m=32) for g in range(LANES)]
        B16 = lane("B16", [P, W], BF16)
        HFW = lane("HF_", [P, 4, W])
        HF = [[HFW[g][:, 2 * n:2 * n + 2, :] for g in range(LANES)] for n in range(2)]
        HTW = lane("HT_", [P, 2, W])
        HT = [[HTW[g][:, n, :].rearrange("p (f n) -> p f n", f=FT0) for g in range(LANES)] for n in range(2)]
        PTW = lane("PT_", [P, 2, W])
        PT = [[PTW[g][:, n, :].rearrange("p (h n) -> p h n", h=4) for g in range(LANES)] for n in range(2)]
        PARTS = [[(HTW if n < 4 else PTW)[g][:, (n % 4) // 2, (n % 2) * (W // 2):(n % 2 + 1) * (W // 2)].bitcast(BF16)
                  for g in range(LANES)] for n in range(6)]
        g8 = [HTW[g][0:8, 0, :] for g in range(LANES)]
        cT = [HTW[g][0:NE1, 1, :] for g in range(LANES)]
        idxm = [HTW[g][0:32, 1, :].bitcast(BF16).rearrange("p (c k) -> p c k", k=CAP) for g in range(LANES)]
        HFF = [HFW[g][:].rearrange("p a n -> p (a n)") for g in range(LANES)]
        vx = [HFF[g][:, 0:GB * (P + 2)].rearrange("p (b n) -> p b n", b=GB) for g in range(LANES)]
        r144 = [HFF[g][:, 2 * W:2 * W + GB * (P + NH)].rearrange("p (b n) -> p b n", b=GB) for g in range(LANES)]
        QS = lane("QS", [SROWS, NH // 2, 2, W], BF16)
        KS = lane("KS", [SROWS, NH // 2, W], BF16)
        st6 = lane("st6", [P, GB, 6])
        mv = lane("mv", [P, GB, 2])
        sm = [lane(f"sm{n}_", [P, 64]) for n in range(8)]
        small = [lane(f"small{n}_", [32, P]) for n in range(5)]
        topv = lane("topv", [32, CAP])
        topi = lane("topi", [32, CAP], U32)
        nmp = [[HTW[g][0:NH, n, 0:W // 2].bitcast(BF16) for g in range(LANES)] for n in range(2)]
        bank = [[stack.enter_context(nc.psum_tensor(f"bank{g}{k}", [P, W], F32)) for k in range(4)]
                for g in range(LANES)]
        q_parts = [nc.dram_tensor(f"q_parts{g}", [SLOTS, P, W], BF16, kind="Internal").ap() for g in range(LANES)]
        k_parts = [nc.dram_tensor(f"k_parts{g}", [SLOTS, P, W], BF16, kind="Internal").ap() for g in range(LANES)]
        y_rows = [nc.dram_tensor(f"y_rows{g}", [2, P, W], F32, kind="Internal").ap() for g in range(LANES)]
        s_parts = [nc.dram_tensor(f"s_parts{g}", [2, NH, W], BF16, kind="Internal").ap() for g in range(LANES)]

        def apart(eng):
            eng.nop(nofuse=True)

        def expert_cols(g, n):
            return A47[g][:, 2:4, :].rearrange("p t (e b k) -> p (t e) b k", e=4, b=GB)[:, :, 2 * n:2 * n + 2, :]

        def bank_experts(g, n):
            return bank[g][n][:].rearrange("p (b e k) -> p e b k", b=2, k=CAP)

        def nth(i, g, step, k):
            return i * COUNTED[step] + (k + 1)

        block = stack.enter_context(nc.Block())

        @block.sync
        def _(sp):
            def load(i, g):
                cols = bass.ds(i * (LANES * W) + g * W, W)
                sp.dma_start(A47[g][:, 0, :], x[:, cols]).then_inc(x_in[g], 16)
                sp.dma_start(flat(CT[g]), ctx_t[:, cols]).then_inc(ctx_in[g], 16)
                sp.dma_start(MK[g][:], mask[:, cols]).then_inc(ctx_in[g], 16)
                sp.dma_start(flat(CR[g]), ctx_r[:, cols]).then_inc(ctx_in[g], 16)

            def load_weights(part):
                for name in WEIGHTS[part].split():
                    ap = w[name]
                    dst, src = (bcast[name], ap.partition_broadcast(P)) if name in bcast else (wt[name], ap)
                    sp.dma_start(dst[:], src).then_inc(weights_in[part], 16)

            def load_next(i, g):
                if isinstance(i, int) and i == pairs - 1:
                    return
                sp.wait_ge(counted["x_pv"][g], nth(i, g, "x_pv", 4 * GB - 1))
                load(i + 1, g)

            def rows_to_dram(half):
                def step(i, g):
                    sp.wait_ge(*at(i, g, f"f_y_sb{half}"))
                    sp.dma_start(y_rows[g][half], A03[g][:, 2 + half, :]).then_inc(rows_out[g][half], 16)
                return step

            def rows_back(half):
                def step(i, g):
                    sp.wait_ge(rows_out[g][half], i * 16 + 16)
                    for q in range(4):
                        sp.dma_start(A[4 + half][g][32 * q:32 * q + 32],
                                     y_rows[g][half].rearrange("(b k) (q d) -> q k b d", b=GB, q=4)[q])\
                            .then_inc(rows_moved[g], 16)
                return step

            def q_to_dram(part):
                first, count = {"h": (0, 3), "m": (3, 2), "l": (5, 1)}[part]
                def step(i, g):
                    sp.wait_ge(*at(i, g, f"x_q_{part}"))
                    src = PARTS["hml".index(part)][g]
                    for s in range(first, first + count):
                        sp.dma_start(q_parts[g][s], src[:]).then_inc(q_out[g], 16)
                return step

            def k_to_dram(i, g):
                sp.wait_ge(*at(i, g, "x_k_l"))
                for s, part in enumerate("hmlhmh"):
                    sp.dma_start(k_parts[g][s], PARTS[3 + "hml".index(part)][g][:]).then_inc(k_out[g], 16)

            def stack_k(i, g):
                sp.wait_ge(k_out[g], i * (SLOTS * 16) + SLOTS * 16)
                kd = k_parts[g].rearrange("s (d r j) n -> (s d) r j n", d=HD, j=2)
                for j in range(2):
                    sp.dma_start(KS[g][KROWS * j:KROWS * j + KROWS], kd[:, :, j]).then_inc(k_in[g], 16)

            def stack_q(i, g):
                sp.wait_ge(q_out[g], i * (SLOTS * 16) + SLOTS * 16)
                qd = q_parts[g].rearrange("s (d r j) n -> (s d) r j n", d=HD, j=2)
                for j in range(2):
                    sp.dma_start(QS[g][KROWS * j:KROWS * j + KROWS, :, j], qd[:, :, j]).then_inc(q_in[g], 16)

            def stack_shift(i, g):
                sp.wait_ge(*at(i, g, "x_nm_l"))
                for n in range(2):
                    for j in range(2):
                        row = SHIFT0 + 2 * j + n
                        sp.dma_start(QS[g][row:row + 1, :, j], nmp[n][g][j:NH:2])\
                            .then_inc(shift_in[g], 16)

            def store(i, g):
                sp.wait_ge(*at(i, g, "n5_done"))
                sp.dma_start(out[:, bass.ds(i * (LANES * W) + g * W, W)],
                             flat(X[g])).then_inc(lane_free[g], 16)

            load(0, 0)
            load_weights("short")
            load_weights("mamba")
            load_weights("cross")
            load(0, 1)
            for part in ("choice", "linear", "heads", "mixture"):
                load_weights(part)
            run(sp, [
                (95.66, rows_to_dram(0)), (98.03, rows_back(0)), (101.763, rows_to_dram(1)),
                (104.143, rows_back(1)), (138.912, k_to_dram), (143.356, stack_k), (148.56, q_to_dram("h")),
                (149.508, q_to_dram("m")), (150.466, q_to_dram("l")), (152.935, stack_q), (170.53, stack_shift),
                (195.697, load_next), (246.62, store),
            ])
            for g in range(LANES):
                sp.wait_ge(lane_free[g], 16 * pairs + 16)

        @block.tensor
        def _(pe):
            pe.wait_ge(constants, N_CONSTANTS)
            mm, tr = pe.matmul, pe.transpose

            def to_c(g, k, src, step):
                for b in range(GB):
                    last = tr(bank[g][k][:, b * P:(b + 1) * P], src[:, b, :], ident[:])
                last.then_inc(sig(step, g), 1)

            def wide(g, k, lhsT, rhs, step):
                mm(bank[g][k][0:lhsT.shape[1], :], lhsT, rhs, start=True, stop=True).then_inc(sig(step, g), 1)

            def m_xt(i, g):
                pe.wait_ge(*at(i, g, "m_norm"))
                to_c(g, 0, R[g], "m_xt")

            def m_proj(i, g):
                pe.wait_ge(*loaded("mamba"))
                pe.wait_ge(*at(i, g, "m_xt_sb"))
                t = flat(T[g])
                wide(g, 1, wt["inT"][:, 256:384], t, "m_xs0")
                wide(g, 2, wt["inT"][:, 384:512], t, "m_xs1")
                wide(g, 3, wt["inT"][:, 512:640], t, "m_b")
                wide(g, 0, wt["inT"][:, 640:768], t, "m_c")

            def m_dtt(i, g):
                pe.wait_ge(*at(i, g, "m_b_sb"))
                wide(g, 3, wt["inT"][:, 768:772], flat(T[g]), "m_dtt")

            def m_gram(i, g):
                pe.wait_ge(*at(i, g, "m_c_sb"))
                for b in range(GB):
                    last = mm(bank[g][0][:, b * P:(b + 1) * P], A[0][g][:, b, :], A[1][g][:, b, :],
                              start=True, stop=True)
                last.then_inc(sig("m_gram", g), 1)

            def m_dt(i, g):
                pe.wait_ge(*at(i, g, "m_dtt_sb"))
                apart(pe)
                for b in range(GB):
                    last = tr(bank[g][3][:, b * HS:(b + 1) * HS], g8[g][0:HS, b * P:(b + 1) * P], ident[0:HS, 0:HS])
                last.then_inc(sig("m_dt", g), 1)

            def m_z(i, g):
                t = flat(T[g])
                pe.wait_ge(*at(i, g, "m_xh0"))
                wide(g, 1, wt["inT"][:, 0:128], t, "m_z0")
                pe.wait_ge(*at(i, g, "m_xh1"))
                wide(g, 2, wt["inT"][:, 128:256], t, "m_z1")

            def m_rows(i, g):
                pe.wait_ge(*at(i, g, "m_gram_sb"))
                to_c(g, 0, A[2][g], "m_xhr0")
                pe.wait_ge(*at(i, g, "m_dt_sb"))
                to_c(g, 3, A[3][g], "m_xhr1")

            def m_seg(b):
                def step(i, g):
                    pe.wait_ge(*at(i, g, "m_dtx1"))
                    pe.wait_ge(counted["m_rd"][g], nth(i, g, "m_rd", b))
                    if b >= 2:
                        pe.wait_ge(counted["m_l"][g], nth(i, g, "m_l", b - 2))
                    mm(bank[g][b % 2][:], strict[:], PTW[g][:, b % 2, :],
                       start=True, stop=True).then_inc(counted["m_seg"][g], 1)
                return step

            def m_yb(b):
                def step(i, g):
                    pe.wait_ge(counted["m_mix"][g], nth(i, g, "m_mix", b))
                    for h in range(HS):
                        rows = slice(PD * (h % 2), PD * (h % 2) + PD)
                        last = mm(bank[g][2 + h // 2][rows, b * P:(b + 1) * P],
                                  A[4 + h // 2][g][:, b, PD * (h % 2):PD * (h % 2) + PD],
                                  HT[b % 2][g][:, h, :], start=True, stop=True)
                    last.then_inc(counted["m_yb"][g], 1)
                return step

            def m_out(i, g):
                pe.wait_ge(*at(i, g, "m_gate1"))
                for b in range(GB):
                    for c in range(2):
                        last = mm(bank[g][0][:, b * P:(b + 1) * P], A[6 + c][g][:, b, :],
                                  wt["outT"][:, c, :], start=(c == 0), stop=(c == 1))
                last.then_inc(sig("m_out", g), 1)

            def c_kt(i, g):
                pe.wait_ge(*loaded("cross"))
                pe.wait_ge(ctx_in[g], i * 48 + 48)
                pe.wait_ge(*at(i, g, "m_skip1"))
                wide(g, 3, wt["wk0"][:], flat(CT[g]), "c_kt")

            def c_xt(i, g):
                pe.wait_ge(*at(i, g, "n0_done"))
                to_c(g, 0, X[g], "c_xt")

            def c_q(i, g):
                pe.wait_ge(*at(i, g, "c_xt_sb"))
                wide(g, 1, wt["wq0"][:], flat(T[g]), "c_q")

            def c_scores(i, g):
                pe.wait_ge(*at(i, g, "c_mask"))
                pe.wait_ge(*at(i, g, "c_q_sb"))
                mm(bank[g][2][:], ones_row[0:1, :], MB[g][:], start=True, stop=False, skip_group_check=True)
                for b in range(GB):
                    last = mm(bank[g][2][:, b * P:(b + 1) * P], A[1][g][:, b, :], A[0][g][:, b, :],
                              start=False, stop=True, skip_group_check=True)
                last.then_inc(sig("c_scores", g), 1)

            def c_pt(i, g):
                pe.wait_ge(*at(i, g, "c_exp"))
                to_c(g, 3, A[2][g], "c_pt")

            def c_ot(i, g):
                pe.wait_ge(*at(i, g, "c_pt_sb"))
                for b in range(GB):
                    last = mm(bank[g][0][:, b * P:(b + 1) * P], CR[g][:, b, :], A[3][g][:, b, :],
                              start=True, stop=True)
                last.then_inc(sig("c_ot", g), 1)

            def rows_times(g, k, lhs, rhs, step):
                for b in range(GB):
                    last = mm(bank[g][k][:, b * P:(b + 1) * P], lhs[:, b, :], rhs, start=True, stop=True)
                last.then_inc(sig(step, g), 1)

            def c_out(i, g):
                pe.wait_ge(*at(i, g, "c_ot_sb"))
                rows_times(g, 1, A[4][g], wt["wo0"][:], "c_out")

            def f_xt(i, g):
                pe.wait_ge(*at(i, g, "n1_done"))
                to_c(g, 0, X[g], "f_xt")

            def f_gt(i, g):
                pe.wait_ge(*loaded("choice"))
                pe.wait_ge(*at(i, g, "f_xt_sb"))
                wide(g, 1, wt["gate"][:], flat(T[g]), "f_gt")

            def f_gate_rows(i, g):
                pe.wait_ge(*at(i, g, "f_gt_sb"))
                apart(pe)
                for b in range(GB):
                    last = tr(bank[g][2][:, b * NE0:(b + 1) * NE0], g8[g][0:NE0, b * P:(b + 1) * P],
                              ident[0:NE0, 0:NE0])
                last.then_inc(sig("f_g", g), 1)

            def f_prob_t(i, g):
                pe.wait_ge(*at(i, g, "f_prob"))
                tr(bank[g][3][0:32, 0:P], sm[2][g][:, 0:32], ident[:]).then_inc(sig("f_pt", g), 1)

            def f_spread(i, g):
                pe.wait_ge(*at(i, g, "f_idxm"))
                for n in range(2):
                    last = mm(bank[g][n][:], ones_row[:], idxm[g][:, 16 * n:16 * n + 16, :], start=True, stop=True)
                last.then_inc(sig("f_bc", g), 1)
                pe.wait_ge(*at(i, g, "f_rowsel"))
                for n in range(2):
                    last = mm(bank[g][2][:, 8 * n:8 * n + 8], small[3 + n][g][:],
                              own_row[:].rearrange("p b h -> p (b h)"), start=True, stop=True)
                last.then_inc(sig("f_rows", g), 1)

            def f_gather(i, g):
                pe.wait_ge(*at(i, g, "f_onehot"))
                for b in range(GB):
                    for n in range(2):
                        last = mm(bank[g][b // 2][:, (b % 2) * 256 + n * P:(b % 2) * 256 + n * P + P], X[g][:, b, :],
                                  A[n][g][:, :, b * CAP:(b + 1) * CAP], start=True, stop=True)
                last.then_inc(sig("f_xi", g), 1)

            def f_up(e):
                def step(i, g):
                    if e == 0:
                        pe.wait_ge(*at(i, g, "f_xi_sb0"))
                        pe.wait_ge(*at(i, g, "f_xi_sb1"))
                    if e >= 2:
                        pe.wait_ge(counted["f_act"][g], nth(i, g, "f_act", e - 2))
                    for f in range(FT0):
                        last = mm(bank[g][e % 2][:, f * P:(f + 1) * P], wt["w1"][:, e, f * P:(f + 1) * P],
                                  A[6 + e // 4][g][:, e % 4, :], start=True, stop=True)
                    last.then_inc(counted["f_up"][g], 1)
                return step

            def f_down(e):
                def step(i, g):
                    if e == 0:
                        pe.wait_ge(*at(i, g, "f_rows_sb"))
                    pe.wait_ge(counted["f_act"][g], nth(i, g, "f_act", e))
                    for f in range(FT0):
                        last = mm(bank[g][2 + e // 4][:, (e % 4) * P:(e % 4 + 1) * P], HT[e % 2][g][:, f, :],
                                  wt["w2"][:, e, f, :], start=(f == 0), stop=(f == FT0 - 1))
                    last.then_inc(counted["f_down"][g], 1)
                return step

            def f_add(i, g):
                pe.wait_ge(*at(i, g, "f_scat"))
                pe.wait_ge(rows_moved[g], i * (8 * 16) + 8 * 16)
                for b in range(GB):
                    for h in range(2):
                        last = mm(bank[g][0][:, b * P:(b + 1) * P], HFW[g][:, h, b * P:(b + 1) * P], A[4 + h][g][:, b, :],
                                  start=(h == 0), stop=(h == 1))
                last.then_inc(sig("f_add", g), 1)

            def l_xt(i, g):
                pe.wait_ge(*at(i, g, "n2_done"))
                to_c(g, 0, X[g], "l_xt")

            def l_q(i, g):
                pe.wait_ge(*loaded("linear"))
                pe.wait_ge(*at(i, g, "l_xt_sb"))
                wide(g, 1, wt["lqkv"][:, 0:P], flat(T[g]), "l_q")
                for b in range(GB):
                    last = mm(bank[g][2 + b // 2][:, (b % 2) * 256:(b % 2) * 256 + 256], T[g][:, b, :],
                              wt["lqkv"][:, P:3 * P], start=True, stop=True)
                    if b % 2:
                        last.then_inc(sig(f"l_kv{b // 2}", g), 1)

            def l_kv(i, g):
                pe.wait_ge(*at(i, g, "l_kf"))
                pe.wait_ge(*at(i, g, "l_v"))
                for b in range(GB):
                    last = mm(bank[g][2 + b // 2][:, (b % 2) * 256:(b % 2) * 256 + P + 1], A[1][g][:, b, :],
                              vx[g][:, b, 0:P + 1], start=True, stop=True)
                last.then_inc(sig("l_kv", g), 1)

            def l_num(i, g):
                pe.wait_ge(*at(i, g, "l_zm"))
                for b in range(GB):
                    last = mm(bank[g][b // 2][:, (b % 2) * 256:(b % 2) * 256 + P + NH], A[0][g][:, b, :],
                              r144[g][:, b, :], start=True, stop=True)
                last.then_inc(sig("l_num", g), 1)

            def l_at(i, g):
                pe.wait_ge(*at(i, g, "l_att"))
                to_c(g, 2, A[2][g], "l_at")

            def l_out(i, g):
                pe.wait_ge(*at(i, g, "l_at_sb"))
                rows_times(g, 3, A[3][g], wt["lout"][:], "l_out")

            def x_k(i, g):
                pe.wait_ge(*loaded("heads"))
                pe.wait_ge(*at(i, g, "l_att"))
                wide(g, 0, wt["wk1"][:], flat(CT[g]), "x_k")
                rows_times(g, 1, CT[g], wt["wv1"][:], "x_v")

            def x_xt(i, g):
                pe.wait_ge(*at(i, g, "n3_done"))
                to_c(g, 2, X[g], "x_xt")

            def x_q(i, g):
                pe.wait_ge(*at(i, g, "x_xt_sb"))
                wide(g, 3, wt["wq1"][:], flat(T[g]), "x_q")

            def x_max(b):
                def step(i, g):
                    if b == 0:
                        pe.wait_ge(k_in[g], i * 32 + 32)
                        pe.wait_ge(q_in[g], i * 32 + 32)
                        pe.wait_ge(*at(i, g, "x_v_sb"))
                        pe.wait_ge(*at(i, g, "x_q_sb"))
                    for c in range(4):
                        n = 4 * b + c
                        if n >= 4:
                            pe.wait_ge(counted["x_amax"][g], nth(i, g, "x_amax", n - 4))
                        for m in range(4):
                            pos = 4 * c + m
                            last = mm(bank[g][n % 4][:, m * P:(m + 1) * P],
                                      QS[g][0:SHIFT0, pos // 2, pos % 2, b * P:(b + 1) * P],
                                      KS[g][0:SHIFT0, pos // 2, b * P:(b + 1) * P], start=True, stop=True)
                        last.then_inc(counted["x_a"][g], 1)
                return step

            def x_nmt(i, g):
                pe.wait_ge(counted["x_amax"][g], nth(i, g, "x_amax", 4 * GB - 1))
                for b in range(GB):
                    last = tr(bank[g][0][0:NH, b * P:(b + 1) * P], sm[0][g][:, b * NH:(b + 1) * NH], ident[:])
                last.then_inc(sig("x_nmt", g), 1)

            def x_weights(n):
                b, c = n // 4, n % 4

                def step(i, g):
                    if n == 0:
                        pe.wait_ge(shift_in[g], i * 64 + 64)
                        pe.wait_ge(*at(i, g, "x_nm_l"))
                    if n >= 2:
                        pe.wait_ge(counted["x_p"][g], nth(i, g, "x_p", n - 2))
                    for r in range(2):
                        last = mm(bank[g][n % 2][:, r * 256:(r + 1) * 256],
                                  KS[g][0:SROWS, 2 * c + r, b * P:(b + 1) * P],
                                  QS[g][0:SROWS, 2 * c + r, :, b * P:(b + 1) * P], start=True, stop=True)
                    last.then_inc(counted["x_b"][g], 1)
                return step

            def x_values(n):
                b, c = n // 4, n % 4

                def step(i, g):
                    pe.wait_ge(counted["x_p"][g], nth(i, g, "x_p", n))
                    for lhs, k in ((VM[g][:, b, c::4], 2), (spread(ones_of_head[:, c, :], 1, 4), 3)):
                        for m in range(4):
                            last = mm(bank[g][k][32 * m:32 * m + 32, b * P:(b + 1) * P], lhs[:, m],
                                      PT[n % 2][g][:, m, :], start=(c == 0), stop=(c == 3),
                                      skip_group_check=True)
                    last.then_inc(counted["x_pv"][g], 1)
                return step

            def x_out(i, g):
                pe.wait_ge(*at(i, g, "x_att"))
                rows_times(g, 0, A[3][g], wt["wo1"][:], "x_out")

            def e_xt(i, g):
                pe.wait_ge(*at(i, g, "n4_done"))
                to_c(g, 0, X[g], "e_xt")

            def e_gt(i, g):
                pe.wait_ge(*loaded("mixture"))
                pe.wait_ge(*at(i, g, "e_xt_sb"))
                wide(g, 1, wt["wg"][:], flat(T[g]), "e_gt")

            def e_gate_rows(i, g):
                pe.wait_ge(*at(i, g, "e_gt_sb"))
                apart(pe)
                for b in range(GB):
                    last = tr(bank[g][2][:, b * NE1:(b + 1) * NE1], g8[g][0:NE1, b * P:(b + 1) * P],
                              ident[0:NE1, 0:NE1])
                last.then_inc(sig("e_g", g), 1)

            def e_ct(i, g):
                pe.wait_ge(*at(i, g, "e_comb"))
                for b in range(GB):
                    last = tr(bank[g][2][0:NE1, b * P:(b + 1) * P], sm[6][g][:, b * NE1:(b + 1) * NE1], ident[:])
                last.then_inc(sig("e_ct", g), 1)

            def e_b2(i, g):
                pe.wait_ge(*at(i, g, "e_ct_sb"))
                rows_times(g, 3, seqs(cT[g]), wt["b2"][:], "e_b2")

            def e_up(n):
                e, f = n // FT1, n % FT1

                def step(i, g):
                    if n == 0:
                        pe.wait_ge(*at(i, g, "e_gt_sb"))
                    if n >= 2:
                        pe.wait_ge(counted["e_act"][g], nth(i, g, "e_act", n - 2))
                    mm(bank[g][n % 2][:], wt["we1"][:, e, f * P:(f + 1) * P],
                       flat(T[g]), start=True, stop=True).then_inc(counted["e_up"][g], 1)
                return step

            def e_down(e):
                def step(i, g):
                    pe.wait_ge(counted["e_act"][g], nth(i, g, "e_act", FT1 * e + FT1 - 1))
                    if e == 1:
                        pe.wait_ge(*at(i, g, "e_acc0"))
                    if e >= 2:
                        pe.wait_ge(counted["e_acc"][g], nth(i, g, "e_acc", e - 2))
                    for b in range(GB):
                        for f in range(FT1):
                            last = mm(bank[g][2 + e % 2][:, b * P:(b + 1) * P], HF[e % 2][g][:, f, b * P:(b + 1) * P],
                                      wt["we2"][:, e, f, :], start=(f == 0), stop=(f == FT1 - 1))
                    last.then_inc(counted["e_down"][g], 1)
                return step

            run(pe, [
                (4.02, m_xt), (6.13, m_proj), (12.53, m_dtt), (13.48, m_gram), (14.41, m_dt), (15.67, m_z),
                (17.39, m_rows), (23.22, m_seg(0)), (24.93, m_seg(1)), (26.63, m_yb(0)), (27.8, m_seg(2)),
                (29.09, m_yb(1)), (29.68, m_seg(3)), (30.72, m_yb(2)), (32.17, m_yb(3)), (35.76, m_out),
                (39.026, c_kt), (44.141, c_xt), (46.109, c_q), (48.876, c_scores), (53.591, c_pt), (56.341, c_ot),
                (58.399, c_out), (65.283, f_xt), (66.979, f_gt), (69.612, f_gate_rows), (71.533, f_prob_t),
                (77.678, f_spread), (80.374, f_gather), (84.654, f_up(0)), (86.165, f_up(1)), (87.824, f_down(0)),
                (89.562, f_up(2)), (90.518, f_down(1)), (91.463, f_up(3)), (92.408, f_down(2)), (93.27, f_up(4)),
                (94.129, f_down(3)), (94.998, f_up(5)), (95.858, f_down(4)), (96.717, f_up(6)), (97.576, f_down(5)),
                (98.435, f_up(7)), (99.304, f_down(6)), (100.242, f_down(7)), (108.438, f_add), (117.789, l_xt),
                (119.714, l_q), (126.17, l_kv), (128.737, l_num), (132.374, l_at), (133.129, x_k), (136.147, l_out),
                (143.554, x_xt), (145.45, x_q), (154.81, x_max(0)), (159.52, x_max(1)), (161.6, x_max(2)),
                (163.99, x_max(3)), (168.16, x_nmt), (174.86, x_weights(0)), (175.28, x_weights(1)),
                (176.19, x_values(0)), (177.33, x_weights(2)), (177.76, x_values(1)), (178.9, x_weights(3)),
                (179.33, x_values(2)), (180.47, x_weights(4)), (180.9, x_values(3)), (182.04, x_weights(5)),
                (182.47, x_values(4)), (183.55, x_weights(6)), (183.77, x_values(5)), (184.36, x_weights(7)),
                (184.64, x_values(6)), (186.73, x_weights(8)), (186.73, x_values(7)), (189.73, x_weights(9)),
                (189.73, x_values(8)), (189.73, x_weights(10)), (189.73, x_values(9)), (189.73, x_weights(11)),
                (189.73, x_values(10)), (189.73, x_weights(12)), (189.73, x_values(11)), (189.73, x_weights(13)),
                (189.73, x_values(12)), (190.27, x_weights(14)), (190.49, x_values(13)), (191.07, x_weights(15)),
                (191.36, x_values(14)), (192.16, x_values(15)), (197.17, x_out), (207.571, e_xt), (209.398, e_gt),
                (212.327, e_gate_rows), (212.884, e_up(0)), (214.679, e_up(1)), (216.48, e_ct), (218.61, e_b2),
                (219.48, e_up(2)), (220.34, e_up(3)), (221.19, e_down(0)), (222.94, e_up(4)), (223.8, e_up(5)),
                (224.65, e_down(1)), (226.4, e_up(6)), (227.26, e_up(7)), (228.12, e_down(2)), (229.86, e_up(8)),
                (230.661, e_up(9)), (231.171, e_down(3)), (232.221, e_up(10)), (232.737, e_up(11)),
                (233.253, e_down(4)), (235.263, e_down(5)),
            ])

        @block.vector
        def _(dve):
            def const(ins):
                ins.then_inc(constants, 1)

            const(dve.memset(ones_row[:], 1.0))
            const(dve.memset(neg_half[:], -0.5))
            for g in range(LANES):
                const(dve.memset(QS[g][:].rearrange("p r j n -> p (r j n)"), 0.0))
                const(dve.memset(KS[g][:].rearrange("p r n -> p (r n)"), 1.0))
            dve.wait_ge(*loaded("short"))
            const(dve.tensor_scalar(a_half[:], wt["D2"][:], 0.5, None, ALU.mult))
            const(dve.tensor_scalar(wq_scaled_bias[:], wt["xbq1"][:], HD ** -0.5, None, ALU.mult))
            dve.wait_ge(scaled, 1)
            const(dve.tensor_scalar(neg_a[:], neg_a_exp[:], -1.0, None, ALU.mult))
            dve.wait_ge(constants, N_CONSTANTS)

            def rsum(out_, in_, op=ALU.add, negate=False):
                return dve.tensor_reduce(out_, in_, AX.X, op, negate=negate)

            def stats_steps(i, g, src, pre):
                for b in range(GB):
                    last = dve.bn_stats(st6[g][:, b, :], src[:, b, :])
                last.then_inc(sig(f"{pre}_stats", g), 1)
                dve.wait_ge(*at(i, g, f"{pre}_stats"))
                apart(dve)
                for b in range(GB):
                    last = dve.bn_aggr(mv[g][:, b, :], st6[g][:, b, :])
                return last

            def norm_stats(n):
                def step(i, g):
                    dve.wait_ge(*at(i, g, f"n{n}_res"))
                    stats_steps(i, g, R[g], f"n{n}").then_inc(sig(f"n{n}_mom", g), 1)
                    dve.wait_ge(*at(i, g, f"n{n}_mom"))
                    dve.tensor_scalar(sm[7][g][:, 0:GB], mv[g][:, :, 1], LN_EPS, None,
                                      ALU.add).then_inc(sig(f"n{n}_eps", g), 1)
                return step

            def norm_rows(n):
                def step(i, g):
                    if n == 0:
                        dve.wait_ge(lane_free[g], i * 16 + 16)
                    dve.wait_ge(*at(i, g, f"n{n}_rstd"))
                    for b in range(GB):
                        last = dve.tensor_scalar(X[g][:, b, :], R[g][:, b, :], mv[g][:, b, 0:1],
                                                 sm[6][g][:, b:b + 1], ALU.subtract, ALU.mult)
                    last.then_inc(sig(f"n{n}_done", g), 1)
                return step

            def res(n, k, produced, resid=None):
                def step(i, g):
                    dve.wait_ge(*at(i, g, produced))
                    if resid:
                        dve.wait_ge(*at(i, g, resid))
                    dve.tensor_tensor(flat(R[g]), bank[g][k][:], flat(R[g]),
                                      ALU.add).then_inc(sig(f"n{n}_res", g), 1)
                return step

            def m_stats(i, g):
                dve.wait_ge(x_in[g], i * 16 + 16)
                stats_steps(i, g, A[4][g], "m").then_inc(sig("m_moments", g), 1)
                dve.wait_ge(*at(i, g, "m_moments"))
                dve.tensor_tensor(sm[0][g][:, 0:GB], mv[g][:, :, 0], mv[g][:, :, 0], ALU.mult)\
                   .then_inc(sig("m_sq", g), 1)
                dve.wait_ge(*at(i, g, "m_sq"))
                dve.scalar_tensor_tensor(sm[7][g][:, 0:GB], mv[g][:, :, 1], RMS_EPS, sm[0][g][:, 0:GB],
                                         ALU.add, ALU.add).then_inc(sig("m_ms", g), 1)

            def m_norm(i, g):
                dve.wait_ge(*at(i, g, "m_rstd"))
                for b in range(GB):
                    last = dve.tensor_scalar(R[g][:, b, :], A[4][g][:, b, :], sm[6][g][:, b:b + 1], None, ALU.mult)
                last.then_inc(sig("m_norm", g), 1)

            def m_conv(i, g):
                for c in range(2):
                    dve.wait_ge(*at(i, g, f"m_xs{c}"))
                    u, xs = A[6 + c][g], seqs(bank[g][1 + c][:])
                    dve.tensor_scalar(u, xs, wt["convw"][:, c, 3:4], wt["convb"][:, c:c + 1], ALU.mult, ALU.add)\
                       .then_inc(sig(f"m_tap{c}0", g), 1)
                    for k in range(1, 4):
                        dve.wait_ge(*at(i, g, f"m_tap{c}{k - 1}"))
                        dve.scalar_tensor_tensor(u[:, :, k:], xs[:, :, :P - k], wt["convw"][:, c, 3 - k:4 - k],
                                                 u[:, :, k:], ALU.mult, ALU.add).then_inc(sig(f"m_tap{c}{k}", g), 1)

            def m_silu(i, g):
                for c in range(2):
                    dve.wait_ge(*at(i, g, f"m_tanh{c}"))
                    dve.scalar_tensor_tensor(A[2 + c][g], seqs(HFW[g][:, 1 + c, :]), 1.0, A[6 + c][g],
                                             ALU.add, ALU.mult).then_inc(sig(f"m_xh{c}", g), 1)

            def m_gram(i, g):
                dve.wait_ge(*at(i, g, "m_gram"))
                dve.tensor_tensor(seqs(HFW[g][:, 0, :]), seqs(bank[g][0][:]), spread(tri[:], 1, GB), ALU.mult)\
                   .then_inc(sig("m_gram_sb", g), 1)

            def m_dt_rows(i, g):
                dve.wait_ge(*at(i, g, "m_dt"))
                dve.tensor_copy(sm[0][g][:, 0:16], bank[g][3][:, 0:16]).then_inc(sig("m_dt_sb", g), 1)
                dve.wait_ge(*at(i, g, "m_dt_sb"))
                dve.scalar_tensor_tensor(sm[1][g][:, 0:16], sm[0][g][:, 0:16], -1.0, sm[0][g][:, 0:16],
                                         ALU.mult, ALU.max)\
                   .then_inc(sig("m_dt_abs", g), 1)

            def m_dt_one(i, g):
                dve.wait_ge(*at(i, g, "m_dt_exp"))
                dve.tensor_scalar(sm[3][g][:, 0:16], sm[2][g][:, 0:16], 1.0, None, ALU.add)\
                   .then_inc(sig("m_dt_one", g), 1)
                dve.wait_ge(*at(i, g, "m_dt_one"))
                dve.tensor_scalar(sm[4][g][:, 0:16], sm[3][g][:, 0:16], 1.0, TINY, ALU.subtract, ALU.max)\
                   .then_inc(sig("m_dt_den", g), 1)
                dve.wait_ge(*at(i, g, "m_dt_den"))
                dve.reciprocal(sm[5][g][:, 0:16], sm[4][g][:, 0:16]).then_inc(sig("m_dt_rec", g), 1)

            def m_dt(i, g):
                dve.wait_ge(*at(i, g, "m_dt_ln"))
                dve.wait_ge(*at(i, g, "m_dt_rec"))
                dve.scalar_tensor_tensor(sm[4][g][:, 0:16], sm[1][g][:, 0:16], TINY, sm[5][g][:, 0:16],
                                         ALU.max, ALU.mult).then_inc(sig("m_dt_ratio", g), 1)
                dve.wait_ge(*at(i, g, "m_dt_ratio"))
                dve.tensor_tensor(sm[5][g][:, 0:16], sm[4][g][:, 0:16], sm[2][g][:, 0:16], ALU.mult)\
                   .then_inc(sig("m_dt_log1p", g), 1)
                dve.wait_ge(*at(i, g, "m_dt_log1p"))
                dve.scalar_tensor_tensor(sm[3][g][:, 0:16], sm[0][g][:, 0:16], 0.0, sm[5][g][:, 0:16],
                                         ALU.max, ALU.add).then_inc(sig("m_dt_done", g), 1)
                dve.wait_ge(*at(i, g, "m_dt_done"))
                dt = sm[3][g][:, 0:16].rearrange("p (b h) -> p b h", b=GB)
                dve.tensor_tensor(sm[5][g][:, 0:16].rearrange("p (b h) -> p b h", b=GB), dt,
                                  spread(neg_a[:], 1, GB), ALU.mult).then_inc(sig("m_decay", g), 1)
                dve.tensor_scalar(sm[4][g][:, 0:16], sm[3][g][:, 0:16], 0.5, None, ALU.mult)\
                   .then_inc(sig("m_half", g), 1)

            def m_gates(i, g):
                for c in range(2):
                    dve.wait_ge(*at(i, g, f"m_tz{c}"))
                    dve.scalar_tensor_tensor(A[c][g], seqs(HFW[g][:, 3 if c == 0 else 1, :]), 1.0,
                                             seqs(bank[g][1 + c][:]), ALU.add, ALU.mult)\
                       .then_inc(sig(f"m_sz{c}", g), 1)
                dve.wait_ge(*at(i, g, "m_half"))
                dve.wait_ge(*at(i, g, "m_twice"))
                half = sm[4][g][:, 0:16].rearrange("p (b h) -> p b h", b=GB)
                for c in range(2):
                    dve.wait_ge(*at(i, g, f"m_xhr{c}"))
                    dve.tensor_tensor(A[4 + c][g].rearrange("p b (h q) -> p b h q", h=2),
                                      seqs(bank[g][3 * c][:]).rearrange("p b (h q) -> p b h q", h=2),
                                      spread(half[:, :, 2 * c:2 * c + 2], 3, PD), ALU.mult)\
                       .then_inc(sig(f"m_dtx{c}", g), 1)

            def m_mix(b):
                def step(i, g):
                    gram = seqs(HFW[g][:, 0, :])
                    dve.wait_ge(counted["m_l"][g], nth(i, g, "m_l", b))
                    if b >= 2:
                        dve.wait_ge(counted["m_yb"][g], nth(i, g, "m_yb", b - 2))
                    dve.tensor_tensor(HT[b % 2][g], HFW[g][:, 2 + b % 2, :].rearrange("p (h n) -> p h n", h=HS),
                                      spread(gram[:, b, :], 1, HS), ALU.mult).then_inc(counted["m_mix"][g], 1)
                return step

            def m_skip(i, g):
                dve.wait_ge(counted["m_yb"][g], nth(i, g, "m_yb", GB - 1))
                for c in range(2):
                    dve.scalar_tensor_tensor(A[6 + c][g], A[2 + c][g], a_half[:, c:c + 1],
                                             seqs(bank[g][2 + c][:]), ALU.mult, ALU.add)\
                       .then_inc(sig(f"m_skip{c}", g), 1)
                for c in range(2):
                    dve.wait_ge(*at(i, g, f"m_skip{c}"))
                    dve.tensor_tensor(A[6 + c][g], A[6 + c][g], A[c][g], ALU.mult)\
                       .then_inc(sig(f"m_gate{c}", g), 1)

            def m_res(i, g):
                dve.wait_ge(*at(i, g, "m_out"))
                dve.wait_ge(*at(i, g, "m_twice"))
                dve.scalar_tensor_tensor(R[g][:], seqs(bank[g][0][:]), 0.5, R[g][:],
                                         ALU.mult, ALU.add).then_inc(sig("n0_res", g), 1)

            def c_mask(i, g):
                dve.wait_ge(ctx_in[g], i * 48 + 48)
                dve.tensor_scalar(MB[g][:], MK[g][:], MASKED, None, ALU.mult).then_inc(sig("c_mask", g), 1)

            def c_max(i, g):
                dve.wait_ge(*at(i, g, "c_scores"))
                rsum(sm[0][g][:, 0:GB], seqs(bank[g][2][:]), ALU.max, negate=True).then_inc(sig("c_max", g), 1)

            def c_rsum(i, g):
                dve.wait_ge(*at(i, g, "c_exp"))
                dve.reciprocal(sm[2][g][:, 0:GB], sm[1][g][:, 0:GB]).then_inc(sig("c_rsum", g), 1)

            def c_pt(i, g):
                dve.wait_ge(*at(i, g, "c_pt"))
                dve.tensor_copy(A[3][g], seqs(bank[g][3][:])).then_inc(sig("c_pt_sb", g), 1)

            def c_res(i, g):
                dve.wait_ge(*at(i, g, "c_out"))
                dve.wait_ge(*at(i, g, "c_resid"))
                dve.wait_ge(*at(i, g, "c_rsum"))
                for b in range(GB):
                    last = dve.scalar_tensor_tensor(R[g][:, b, :], bank[g][1][:, b * P:(b + 1) * P],
                                                    sm[2][g][:, b:b + 1], R[g][:, b, :], ALU.mult, ALU.add)
                last.then_inc(sig("n1_res", g), 1)

            def f_max(i, g):
                dve.wait_ge(*at(i, g, "f_g"))
                gate = bank[g][2][:, 0:32].rearrange("p (b e) -> p b e", b=GB)
                rsum(sm[0][g][:, 0:GB], gate, ALU.max).then_inc(sig("f_gmax", g), 1)
                dve.wait_ge(*at(i, g, "f_gmax"))
                dve.tensor_tensor(sm[1][g][:, 0:32].rearrange("p (b e) -> p b e", b=GB), gate,
                                  spread(sm[0][g][:, 0:GB], 2, NE0), ALU.subtract).then_inc(sig("f_gsub", g), 1)

            def f_prob(i, g):
                dve.wait_ge(*at(i, g, "f_gexp"))
                ex = sm[3][g][:, 0:32].rearrange("p (b e) -> p b e", b=GB)
                rsum(sm[4][g][:, 0:GB], ex).then_inc(sig("f_gsum", g), 1)
                dve.wait_ge(*at(i, g, "f_gsum"))
                dve.reciprocal(sm[5][g][:, 0:GB], sm[4][g][:, 0:GB]).then_inc(sig("f_grec", g), 1)
                dve.wait_ge(*at(i, g, "f_grec"))
                dve.tensor_tensor(sm[2][g][:, 0:32].rearrange("p (b e) -> p b e", b=GB), ex,
                                  spread(sm[5][g][:, 0:GB], 2, NE0), ALU.mult).then_inc(sig("f_prob", g), 1)

            def f_top(r):
                def step(i, g):
                    src, dst, k = small[r % 2][g], small[1 - r % 2][g], slice(8 * r, 8 * r + 8)
                    if r == 0:
                        dve.wait_ge(*at(i, g, "f_pt"))
                        dve.tensor_copy(src[:], bank[g][3][0:32, 0:P]).then_inc(sig("f_pt_sb", g), 1)
                        dve.wait_ge(*at(i, g, "f_pt_sb"))
                    else:
                        dve.wait_ge(*at(i, g, f"f_topw{r - 1}"))
                    apart(dve)
                    dve.max(topv[g][:, k], src[:]).then_inc(sig(f"f_topv{r}", g), 1)
                    dve.wait_ge(*at(i, g, f"f_topv{r}"))
                    apart(dve)
                    dve.max_index(topi[g][:, k], topv[g][:, k], src[:]).then_inc(sig(f"f_topi{r}", g), 1)
                    dve.match_replace(dst[:], topv[g][:, k], src[:], -1.0).then_inc(sig(f"f_topw{r}", g), 1)
                return step

            def f_index(i, g):
                dve.wait_ge(*at(i, g, f"f_topi{CAP // 8 - 1}"))
                dve.tensor_copy(small[2][g][:, 0:CAP], topi[g][:]).then_inc(sig("f_idx", g), 1)
                dve.wait_ge(*at(i, g, "f_idx"))
                dve.tensor_tensor(idxm[g], spread(small[2][g][:, 0:CAP], 1, 32),
                                  spread(own_col[:], 2, CAP), ALU.mult).then_inc(sig("f_idxm", g), 1)
                for n, src in ((3, small[2][g][:, 0:CAP]), (4, topv[g][:])):
                    last = dve.tensor_tensor(small[n][g][:].rearrange("p (q k) -> p q k", q=4), spread(src, 1, 4),
                                             spread(own_quarter[:], 2, CAP), ALU.mult)
                last.then_inc(sig("f_rowsel", g), 1)

            def f_onehot(i, g):
                dve.wait_ge(*at(i, g, "f_bc"))
                for n in range(2):
                    last = dve.tensor_scalar(A03[g][:, n, :], bank[g][n][:], tok_id[:, 0:1], None, ALU.is_equal)
                last.then_inc(sig("f_onehot", g), 1)

            def f_scat(i, g):
                dve.wait_ge(*at(i, g, "f_rows"))
                dve.tensor_copy(sm[0][g][:, 0:16], bank[g][2][:, 0:16]).then_inc(sig("f_rows_sb", g), 1)
                dve.wait_ge(*at(i, g, "f_rows_sb"))
                for b in range(GB):
                    for h in range(2):
                        n = 2 * b + h
                        last = dve.tensor_scalar(HFW[g][:, h, b * P:(b + 1) * P], tok_row[:], sm[0][g][:, n:n + 1],
                                                 sm[0][g][:, 8 + n:9 + n], ALU.is_equal, ALU.mult)
                last.then_inc(sig("f_scat", g), 1)

            def f_gathered(i, g):
                dve.wait_ge(*at(i, g, "f_xi"))
                dve.tensor_copy(expert_cols(g, 0), bank_experts(g, 0)).then_inc(sig("f_xi_sb0", g), 1)

            def f_res(i, g):
                dve.wait_ge(*at(i, g, "f_add_sb"))
                dve.tensor_tensor(flat(R[g]), flat(X[g]), B16[g][:], ALU.add).then_inc(sig("n2_res", g), 1)

            def l_feat(i, g):
                dve.wait_ge(*at(i, g, "l_eq"))
                dve.tensor_scalar(A[4][g], A[4][g], 1.0, None, ALU.min).then_inc(sig("l_qmin", g), 1)
                dve.wait_ge(*at(i, g, "l_qmin"))
                dve.scalar_tensor_tensor(A[0][g], seqs(bank[g][1][:]), 1.0, A[4][g], ALU.add, ALU.max)\
                   .then_inc(sig("l_qf", g), 1)
                dve.wait_ge(*at(i, g, "l_v"))
                dve.tensor_scalar(A[5][g], A[5][g], 1.0, None, ALU.min).then_inc(sig("l_kmin", g), 1)
                dve.wait_ge(*at(i, g, "l_kmin"))
                for n in range(2):
                    kk = bank[g][2 + n][:].rearrange("p (b n) -> p b n", b=2)[:, :, 0:P]
                    last = dve.scalar_tensor_tensor(A[1][g][:, 2 * n:2 * n + 2, :], kk, 1.0,
                                                    A[5][g][:, 2 * n:2 * n + 2, :], ALU.add, ALU.max)
                last.then_inc(sig("l_kf", g), 1)

            def l_heads(i, g):
                dve.wait_ge(*at(i, g, "l_kv"))
                for n in range(2):
                    kv = bank[g][2 + n][:].rearrange("p (b n) -> p b n", b=2)
                    last = dve.tensor_tensor(r144[g][:, 2 * n:2 * n + 2, 0:P], kv[:, :, 0:P],
                                             spread(head_mask[:], 1, 2), ALU.mult)
                last.then_inc(sig("l_kvm", g), 1)
                for n in range(2):
                    kv = bank[g][2 + n][:].rearrange("p (b n) -> p b n", b=2)
                    last = dve.tensor_tensor(r144[g][:, 2 * n:2 * n + 2, P:P + NH],
                                             kv[:, :, P:P + 1].broadcast_to((P, 2, NH)),
                                             spread(head_cols[:], 1, 2), ALU.mult)
                last.then_inc(sig("l_zm", g), 1)

            def l_div(i, g):
                dve.wait_ge(*at(i, g, "l_num"))
                den = sm[0][g][:].rearrange("p (b h) -> p b h", b=GB)
                for n in range(2):
                    kv = bank[g][n][:].rearrange("p (b n) -> p b n", b=2)
                    last = dve.tensor_scalar(den[:, 2 * n:2 * n + 2, :], kv[:, :, P:P + NH], DEN_EPS, None, ALU.add)
                last.then_inc(sig("l_den", g), 1)
                dve.wait_ge(*at(i, g, "l_den"))
                dve.reciprocal(sm[1][g][:], sm[0][g][:]).then_inc(sig("l_rec", g), 1)
                dve.wait_ge(*at(i, g, "l_rec"))
                rec = sm[1][g][:].rearrange("p (b h) -> p b h", b=GB)
                for n in range(2):
                    kv = bank[g][n][:].rearrange("p (b n) -> p b n", b=2)
                    last = dve.tensor_tensor(
                        A[2][g][:, 2 * n:2 * n + 2, :].rearrange("p b (h q) -> p b h q", h=NH),
                        kv[:, :, 0:P].rearrange("p b (h q) -> p b h q", h=NH),
                        spread(rec[:, 2 * n:2 * n + 2, :], 3, HD), ALU.mult)
                last.then_inc(sig("l_att", g), 1)

            def x_v(i, g):
                dve.wait_ge(*at(i, g, "x_v"))
                dve.wait_ge(*at(i, g, "x_zero"))
                for c in range(4):
                    spot = VM[g][:, :, c::4, HD * c:HD * c + HD]
                    last = dve.tensor_tensor(
                        spot, bank[g][1][:].rearrange("p (b m c q) -> p b m c q", b=GB, m=4, c=4)[:, :, :, c],
                        spread(bcast["xbv"][:].rearrange("p (m c q) -> p m c q", m=4, c=4)[:, :, c], 1, GB), ALU.add)
                last.then_inc(sig("x_v_sb", g), 1)

            def x_kparts(i, g):
                split(i, g, "k", 3, A[1], A[2])

            def split(i, g, side, n, full, rest):
                dve.wait_ge(*at(i, g, f"x_{side}_h"))
                dve.tensor_tensor(flat(rest[g]), flat(full[g]), PARTS[n][g], ALU.subtract)\
                   .then_inc(sig(f"x_{side}_r1", g), 1)
                dve.wait_ge(*at(i, g, f"x_{side}_r1"))
                dve.tensor_copy(PARTS[n + 1][g], flat(rest[g])).then_inc(sig(f"x_{side}_m", g), 1)
                dve.wait_ge(*at(i, g, f"x_{side}_m"))
                dve.tensor_tensor(PARTS[n + 2][g], flat(rest[g]), PARTS[n + 1][g], ALU.subtract)\
                   .then_inc(sig(f"x_{side}_l", g), 1)

            def x_qparts(i, g):
                split(i, g, "q", 0, A[0], A[3])

            def x_max(b):
                def step(i, g):
                    for c in range(4):
                        n = 4 * b + c
                        dve.wait_ge(counted["x_a"][g], nth(i, g, "x_a", n))
                        rsum(sm[0][g][:, b * NH + 4 * c:b * NH + 4 * c + 4], seqs(bank[g][n % 4][:]), ALU.max,
                             negate=True).then_inc(counted["x_amax"][g], 1)
                return step

            def x_shift(i, g):
                dve.wait_ge(*at(i, g, "x_nmt"))
                dve.tensor_copy(nmp[0][g][:], bank[g][0][0:NH, :]).then_inc(sig("x_nm_h", g), 1)
                dve.wait_ge(*at(i, g, "x_nm_h"))
                dve.tensor_tensor(nmp[1][g][:], bank[g][0][0:NH, :], nmp[0][g][:], ALU.subtract)\
                   .then_inc(sig("x_nm_l", g), 1)

            def x_div(i, g):
                dve.wait_ge(counted["x_pv"][g], nth(i, g, "x_pv", 4 * GB - 1))
                dve.reciprocal(A[2][g], seqs(bank[g][3][:])).then_inc(sig("x_rden", g), 1)
                dve.wait_ge(*at(i, g, "x_rden"))
                dve.tensor_tensor(A[3][g], seqs(bank[g][2][:]), A[2][g], ALU.mult).then_inc(sig("x_att", g), 1)

            def e_rank(i, g):
                dve.wait_ge(*at(i, g, "e_g"))
                dve.tensor_copy(sm[0][g][:, 0:24], bank[g][2][:, 0:24]).then_inc(sig("e_g_sb", g), 1)
                dve.wait_ge(*at(i, g, "e_g_sb"))
                lg = sm[0][g][:, 0:24].rearrange("p (b e) -> p b e", b=GB)
                above = HFW[g][:, 0, 0:144].rearrange("p (b e j) -> p b e j", b=GB, e=NE1)
                equal = HFW[g][:, 1, 0:144].rearrange("p (b e j) -> p b e j", b=GB, e=NE1)
                mine, other = spread(lg, 3, NE1), spread(lg, 2, NE1)
                dve.tensor_tensor(above, other, mine, ALU.is_gt).then_inc(sig("e_above", g), 1)
                dve.tensor_tensor(equal, other, mine, ALU.is_equal).then_inc(sig("e_equal", g), 1)
                dve.wait_ge(*at(i, g, "e_equal"))
                dve.tensor_tensor(equal, equal, spread(before[:], 1, GB), ALU.mult).then_inc(sig("e_tied", g), 1)
                dve.wait_ge(*at(i, g, "e_tied"))
                dve.tensor_tensor(above, above, equal, ALU.add).then_inc(sig("e_rank1", g), 1)
                dve.wait_ge(*at(i, g, "e_rank1"))
                rank = sm[1][g][:, 0:24].rearrange("p (b e) -> p b e", b=GB)
                rsum(rank, above).then_inc(sig("e_rank", g), 1)
                dve.wait_ge(*at(i, g, "e_rank"))
                dve.tensor_scalar(sm[2][g][:, 0:24], sm[1][g][:, 0:24], 2.0, None, ALU.is_lt)\
                   .then_inc(sig("e_sel", g), 1)
                rsum(sm[3][g][:, 0:GB], lg, ALU.max).then_inc(sig("e_max", g), 1)
                dve.wait_ge(*at(i, g, "e_max"))
                dve.tensor_tensor(sm[4][g][:, 0:24].rearrange("p (b e) -> p b e", b=GB), lg,
                                  spread(sm[3][g][:, 0:GB], 2, NE1), ALU.subtract).then_inc(sig("e_sub", g), 1)

            def e_comb(i, g):
                dve.wait_ge(*at(i, g, "e_exp"))
                dve.tensor_tensor(sm[1][g][:, 0:24], sm[5][g][:, 0:24], sm[2][g][:, 0:24], ALU.mult)\
                   .then_inc(sig("e_msel", g), 1)
                dve.wait_ge(*at(i, g, "e_msel"))
                ex = sm[1][g][:, 0:24].rearrange("p (b e) -> p b e", b=GB)
                rsum(sm[3][g][:, 0:GB], ex).then_inc(sig("e_sum", g), 1)
                dve.wait_ge(*at(i, g, "e_sum"))
                dve.reciprocal(sm[4][g][:, 0:GB], sm[3][g][:, 0:GB]).then_inc(sig("e_rec", g), 1)
                dve.wait_ge(*at(i, g, "e_rec"))
                dve.tensor_tensor(sm[6][g][:, 0:24].rearrange("p (b e) -> p b e", b=GB), ex,
                                  spread(sm[4][g][:, 0:GB], 2, NE1), ALU.mult).then_inc(sig("e_comb", g), 1)

            def e_acc0(i, g):
                dve.wait_ge(*at(i, g, "e_b2"))
                dve.tensor_tensor(flat(R[g]), bank[g][3][:], flat(X[g]), ALU.add).then_inc(sig("e_acc0", g), 1)

            def e_acc(e):
                def step(i, g):
                    dve.wait_ge(counted["e_down"][g], nth(i, g, "e_down", e))
                    if e:
                        dve.wait_ge(counted["e_acc"][g], nth(i, g, "e_acc", e - 1))
                    else:
                        dve.wait_ge(*at(i, g, "e_acc0"))
                    for b in range(GB):
                        last = dve.scalar_tensor_tensor(
                            R[g][:, b, :], bank[g][2 + e % 2][:, b * P:(b + 1) * P],
                            sm[6][g][:, b * NE1 + e:b * NE1 + e + 1], R[g][:, b, :], ALU.mult, ALU.add)
                    last.then_inc(sig("n5_res", g) if e == NE1 - 1 else counted["e_acc"][g], 1)
                return step

            run(dve, [
                (0, m_stats), (2.95, m_norm), (8.03, m_conv), (14.81, m_silu), (16.02, m_gram), (16.62, m_dt_rows),
                (17.29, m_dt_one), (18.68, m_dt), (20.45, m_gates), (25.75, m_mix(0)), (27.46, m_mix(1)),
                (29.91, m_mix(2)), (31.36, m_mix(3)), (32.87, m_skip), (39.221, m_res), (39.969, norm_stats(0)),
                (42.829, norm_rows(0)), (43.885, c_mask), (51.265, c_max), (53.458, c_rsum), (54.657, c_pt),
                (60.252, c_res), (61.402, norm_stats(1)), (64.035, norm_rows(1)), (70.129, f_max), (70.821, f_prob),
                (71.932, f_top(0)), (73.356, f_top(1)), (74.379, f_top(2)), (75.39, f_top(3)), (76.18, f_index),
                (78.715, f_onehot), (83.801, f_gathered), (84.325, f_scat), (113.109, f_res),
                (113.83, norm_stats(2)), (116.525, norm_rows(2)), (123.594, l_feat), (128.313, l_heads),
                (130.729, l_div), (136.345, x_v), (137.135, x_kparts), (138.912, res(3, 3, "l_out", "l_resid")),
                (139.623, norm_stats(3)), (142.29, norm_rows(3)), (148.698, x_qparts), (158.43, x_max(0)),
                (160.82, x_max(1)), (163.21, x_max(2)), (165.61, x_max(3)), (169.21, x_shift), (193.65, x_div),
                (202.146, res(4, 0, "x_out", "x_resid")), (203.468, norm_stats(4)), (206.227, norm_rows(4)),
                (212.884, e_rank), (215.56, e_comb), (219.67, e_acc0), (223.13, e_acc(0)), (226.59, e_acc(1)),
                (230.05, e_acc(2)), (232.335, e_acc(3)), (235.529, e_acc(4)), (237.963, e_acc(5)),
                (239.285, norm_stats(5)), (242.54, norm_rows(5)),
            ])

        @block.scalar
        def _(act):
            act.wait_ge(*loaded("short"))
            act.activation(neg_a_exp[:], bcast["negA"][:], ACT.Exp).then_inc(scaled, 1)
            act.wait_ge(constants, N_CONSTANTS)
            def move(dst, k, step, produced, bias=None, scale=1.0, rows=P):
                def run(i, g):
                    act.wait_ge(*at(i, g, produced))
                    kw = {} if bias is None else {"bias": bias}
                    act.activation(dst(g), bank[g][k][0:rows, :], ACT.Identity if bias is not None else ACT.Copy,
                                   scale=scale, **kw).then_inc(sig(step, g), 1)
                return run

            def m_xt(i, g):
                act.wait_ge(*at(i, g, "m_xt"))
                act.activation(flat(T[g]), bank[g][0][:], ACT.Copy, scale=wt["normw"][:, 0:1])\
                   .then_inc(sig("m_xt_sb", g), 1)

            def m_tanh(i, g):
                for c in range(2):
                    act.wait_ge(*at(i, g, f"m_tap{c}3"))
                    act.activation(HFW[g][:, 1 + c, :], A47[g][:, 2 + c, :], ACT.Tanh, scale=0.5)\
                       .then_inc(sig(f"m_tanh{c}", g), 1)

            def m_dt_exp(i, g):
                act.wait_ge(*at(i, g, "m_dt_abs"))
                act.activation(sm[2][g][:, 0:16], sm[1][g][:, 0:16], ACT.Exp, scale=-1.0)\
                   .then_inc(sig("m_dt_exp", g), 1)

            def m_dt_ln(i, g):
                act.wait_ge(*at(i, g, "m_dt_one"))
                act.activation(sm[1][g][:, 0:16], sm[3][g][:, 0:16], ACT.Ln).then_inc(sig("m_dt_ln", g), 1)

            def m_tz(i, g):
                for c in range(2):
                    act.wait_ge(*at(i, g, f"m_z{c}"))
                    act.activation(HFW[g][:, 3 if c == 0 else 1, :], bank[g][1 + c][:], ACT.Tanh, scale=0.5)\
                       .then_inc(sig(f"m_tz{c}", g), 1)

            def m_l(b):
                def step(i, g):
                    act.wait_ge(counted["m_seg"][g], nth(i, g, "m_seg", b))
                    if b >= 2:
                        act.wait_ge(counted["m_mix"][g], nth(i, g, "m_mix", b - 2))
                    act.activation(HFW[g][:, 2 + b % 2, :], bank[g][b % 2][:], ACT.Exp).then_inc(counted["m_l"][g], 1)
                return step

            def c_exp(i, g):
                act.wait_ge(*at(i, g, "c_max"))
                for b in range(GB):
                    last = act.activation(A[2][g][:, b, :], bank[g][2][:, b * P:(b + 1) * P], ACT.Exp,
                                          bias=sm[0][g][:, b:b + 1], accum_out=sm[1][g][:, b:b + 1])
                last.then_inc(sig("c_exp", g), 1)

            def f_gexp(i, g):
                act.wait_ge(*at(i, g, "f_gsub"))
                act.activation(sm[3][g][:, 0:32], sm[1][g][:, 0:32], ACT.Exp).then_inc(sig("f_gexp", g), 1)

            def f_gathered(i, g):
                act.wait_ge(*at(i, g, "f_xi"))
                act.activation(expert_cols(g, 1), bank_experts(g, 1), ACT.Copy).then_inc(sig("f_xi_sb1", g), 1)

            def f_gelu(e):
                def step(i, g):
                    act.wait_ge(counted["f_up"][g], nth(i, g, "f_up", e))
                    act.activation(HTW[g][:, e % 2, :], bank[g][e % 2][:], ACT.Gelu_apprx_tanh)\
                       .then_inc(counted["f_act"][g], 1)
                return step

            def l_exps(i, g):
                act.wait_ge(*at(i, g, "l_q"))
                act.activation(A47[g][:, 0, :], bank[g][1][:], ACT.Exp).then_inc(sig("l_eq", g), 1)
                for n in range(2):
                    act.wait_ge(*at(i, g, f"l_kv{n}"))
                    kv = bank[g][2 + n][:].rearrange("p (b n) -> p b n", b=2)
                    last = act.activation(A[5][g][:, 2 * n:2 * n + 2, :], kv[:, :, 0:P], ACT.Exp)
                last.then_inc(sig("l_ek", g), 1)
                act.wait_ge(*at(i, g, "f_add"))
                for n in range(2):
                    kv = bank[g][2 + n][:].rearrange("p (b n) -> p b n", b=2)
                    act.activation(vx[g][:, 2 * n:2 * n + 2, 0:P], kv[:, :, P:2 * P], ACT.Copy)
                act.activation(vx[g][:, :, P:P + 1], ones4[:], ACT.Copy).then_inc(sig("l_v", g), 1)

            def f_y(half):
                def step(i, g):
                    act.wait_ge(counted["f_down"][g], nth(i, g, "f_down", 4 * half + 3))
                    act.activation(A03[g][:, 2 + half, :], bank[g][2 + half][:], ACT.Copy)\
                       .then_inc(sig(f"f_y_sb{half}", g), 1)
                return step

            def x_k(i, g):
                move(lambda g: A03[g][:, 1, :], 0, "x_k_sb", "x_k", wt["xbk1"][:, 0:1])(i, g)
                act.wait_ge(*at(i, g, "x_k_sb"))
                act.activation(PARTS[3][g], A03[g][:, 1, :], ACT.Copy).then_inc(sig("x_k_h", g), 1)

            def x_q(i, g):
                move(lambda g: A03[g][:, 0, :], 3, "x_q_sb", "x_q", wq_scaled_bias[:, 0:1], HD ** -0.5)(i, g)
                act.wait_ge(*at(i, g, "x_q_sb"))
                act.activation(PARTS[0][g], A03[g][:, 0, :], ACT.Copy).then_inc(sig("x_q_h", g), 1)

            def x_p(n):
                def step(i, g):
                    act.wait_ge(counted["x_b"][g], nth(i, g, "x_b", n))
                    if n >= 2:
                        act.wait_ge(counted["x_pv"][g], nth(i, g, "x_pv", n - 2))
                    act.activation(PTW[g][:, n % 2, :], bank[g][n % 2][:], ACT.Exp).then_inc(counted["x_p"][g], 1)
                return step

            def e_exp(i, g):
                act.wait_ge(*at(i, g, "e_sub"))
                act.activation(sm[5][g][:, 0:24], sm[4][g][:, 0:24], ACT.Exp).then_inc(sig("e_exp", g), 1)

            def e_gelu(n):
                e, f = n // FT1, n % FT1

                def step(i, g):
                    act.wait_ge(counted["e_up"][g], nth(i, g, "e_up", n))
                    if e >= 2:
                        act.wait_ge(counted["e_down"][g], nth(i, g, "e_down", e - 2))
                    act.activation(HFW[g][:, 2 * (e % 2) + f, :], bank[g][n % 2][:], ACT.Gelu,
                                   bias=wt["b1"][:, n:n + 1]).then_inc(counted["e_act"][g], 1)
                return step

            def tile_of(n):
                return lambda g: A03[g][:, n, :] if n < 4 else A47[g][:, n - 4, :]

            t_of = lambda g: flat(T[g])
            run(act, [
                (5.14, m_xt), (11.44, move(tile_of(0), 3, "m_b_sb", "m_b")),
                (12.72, move(tile_of(1), 0, "m_c_sb", "m_c")),
                (13.58, move(lambda g: g8[g][0:HS, :], 3, "m_dtt_sb", "m_dtt", wt["dtb"][:, 0:1], rows=HS)),
                (14.15, m_tanh), (17.04, m_dt_exp), (18.43, m_dt_ln), (19.82, m_tz), (25.82, m_l(0)),
                (27.53, m_l(1)), (29.28, m_l(2)), (30.73, m_l(3)),
                (40.102, move(tile_of(0), 3, "c_kt_sb", "c_kt", wt["xbk0"][:, 0:1])),
                (45.217, move(t_of, 0, "c_xt_sb", "c_xt")),
                (48.056, move(tile_of(1), 1, "c_q_sb", "c_q", wt["xbq0"][:, 0:1])), (52.013, c_exp),
                (57.551, move(tile_of(4), 0, "c_ot_sb", "c_ot")), (66.307, move(t_of, 0, "f_xt_sb", "f_xt")),
                (68.832, move(lambda g: g8[g][0:NE0, :], 1, "f_gt_sb", "f_gt", rows=NE0)), (69.105, f_gexp),
                (82.457, f_gathered), (87.824, f_gelu(0)), (88.041, f_gelu(1)), (90.724, f_gelu(2)),
                (92.599, f_gelu(3)), (94.327, f_gelu(4)), (95.186, f_y(0)), (96.045, f_gelu(5)),
                (97.773, f_gelu(6)), (99.492, f_gelu(7)), (101.299, f_y(1)),
                (112.487, move(lambda g: B16[g][:], 0, "f_add_sb", "f_add")),
                (118.826, move(t_of, 0, "l_xt_sb", "l_xt")), (121.591, l_exps),
                (133.307, move(tile_of(3), 2, "l_at_sb", "l_at")), (134.864, x_k),
                (144.59, move(t_of, 2, "x_xt_sb", "x_xt")), (147.326, x_q), (175.48, x_p(0)), (175.96, x_p(1)),
                (177.95, x_p(2)), (178.09, x_p(3)), (178.09, x_p(4)), (182.66, x_p(5)), (183.96, x_p(6)),
                (184.77, x_p(7)), (185.64, x_p(8)), (186.45, x_p(9)), (187.32, x_p(10)), (188.13, x_p(11)),
                (189, x_p(12)), (189.81, x_p(13)), (190.68, x_p(14)), (191.49, x_p(15)),
                (208.673, move(t_of, 0, "e_xt_sb", "e_xt")),
                (211.403, move(lambda g: g8[g][0:NE1, :], 1, "e_gt_sb", "e_gt", wt["bg"][:, 0:1], rows=NE1)),
                (215.31, e_exp), (216.71, e_gelu(0)), (217.28, e_gelu(1)),
                (217.85, move(lambda g: cT[g], 2, "e_ct_sb", "e_ct", rows=NE1)), (220.53, e_gelu(2)),
                (221.39, e_gelu(3)), (223.99, e_gelu(4)), (224.85, e_gelu(5)), (227.45, e_gelu(6)),
                (228.31, e_gelu(7)), (230.775, e_gelu(8)), (231.291, e_gelu(9)), (232.851, e_gelu(10)),
                (233.367, e_gelu(11)),
            ])

        @block.gpsimd
        def _(pool):
            step_of = [0]

            def const(ins, wait=False):
                ins.then_inc(constants, 1)

            def made(ins):
                step_of[0] += 1
                ins.then_inc(pool_made, 1)
                pool.wait_ge(pool_made, step_of[0])

            def fill(tile_, value):
                made(pool.memset(tile_, value))

            def keep(tile_, pattern, compare, base, channel, fill_=0.0):
                made(pool.affine_select(out=tile_, in_=tile_, pattern=pattern, compare_op=compare, fill=fill_,
                                        base=base, channel_multiplier=channel))

            for t in (ident, tri, strict, head_mask, head_cols):
                fill(t[:], 1.0)
            keep(ident[:], [[1, P]], ALU.is_equal, 0, -1)
            keep(tri[:], [[1, P]], ALU.is_ge, 0, -1)
            keep(strict[:], [[-1, P]], ALU.is_gt, 0, 1)
            heads = head_mask[:].rearrange("p (h q) -> p h q", h=NH)
            keep(heads, [[-HD, NH], [0, HD]], ALU.is_ge, 0, 1)
            keep(heads, [[HD, NH], [0, HD]], ALU.is_ge, HD - 1, -1)
            keep(head_cols[:], [[-HD, NH]], ALU.is_ge, 0, 1)
            keep(head_cols[:], [[HD, NH]], ALU.is_ge, HD - 1, -1)
            fill(ones_of_head[:], 0.0)
            for c in range(4):
                fill(ones_of_head[:, c, HD * c:HD * c + HD], 1.0)
            made(pool.iota(tok_id[:], pattern=[[0, 1]], base=0, channel_multiplier=1,
                           allow_small_or_imprecise_dtypes=True))
            made(pool.iota(tok_row[:], pattern=[[1, P]], base=0, channel_multiplier=0,
                           allow_small_or_imprecise_dtypes=True))
            fill(own_col[:], 1.0)
            keep(own_col[:].rearrange("p (e b) -> p e b", b=GB), [[-1, NE0], [-NE0, GB]], ALU.is_equal, 0, 1)
            fill(own_row[:], 1.0)
            keep(own_row[:], [[-NE0, GB], [-4, 2]], ALU.is_ge, 0, 1)
            keep(own_row[:], [[NE0, GB], [4, 2]], ALU.is_ge, 3, -1)
            fill(own_quarter[:], 0.0)
            for m in range(NE0):
                keep(own_quarter[:], [[-1, 4]], ALU.not_equal, -4 * m, 1, 1.0)
            fill(before[:], 1.0)
            keep(before[:], [[1, NE1], [-1, NE1]], ALU.is_gt, 0, 0)
            fill(ones4[:], 1.0)
            pool.memset(spare[:, 0:1], 0.0).then_inc(constants, 1)
            for g in range(LANES):
                pool.memset(spare[:, g + 1:g + 2], 0.0).then_inc(lane_free[g], 16)

            pool.wait_ge(constants, N_CONSTANTS)
            def rstd(name, produced):
                def step(i, g):
                    pool.wait_ge(*at(i, g, produced))
                    pool.tensor_tensor(sm[6][g][:, 0:GB], sm[7][g][:, 0:GB], neg_half[:], ALU.pow)\
                        .then_inc(sig(name, g), 1)
                return step

            def m_twice(i, g):
                pool.wait_ge(*at(i, g, "m_xt_sb"))
                apart(pool)
                pool.tensor_scalar(flat(R[g]), flat(A[4][g]), 2.0, 0.0, ALU.mult, ALU.add)\
                    .then_inc(sig("m_twice", g), 1)

            def m_rd(b):
                def step(i, g):
                    if b < 2:
                        pool.wait_ge(*at(i, g, "m_decay"))
                    else:
                        pool.wait_ge(counted["m_seg"][g], nth(i, g, "m_seg", b - 2))
                    apart(pool)
                    for h in range(HS):
                        last = pool.tensor_scalar(PT[b % 2][g][:, h, :], tri[:],
                                                  sm[5][g][:, b * HS + h:b * HS + h + 1], 0.0, ALU.mult, ALU.add)
                    last.then_inc(counted["m_rd"][g], 1)
                return step

            def resid(name, ready, bias):
                def step(i, g):
                    pool.wait_ge(*at(i, g, ready))
                    pool.tensor_tensor(R[g][:], X[g][:], spread(bcast[bias][:], 1, GB), ALU.add)\
                        .then_inc(sig(name, g), 1)
                return step

            def x_zero(i, g):
                pool.wait_ge(*at(i, g, "l_kf"))
                apart(pool)
                pool.memset(A47[g][:].rearrange("p b n -> p (b n)"), 0.0).then_inc(sig("x_zero", g), 1)

            run(pool, [
                (1.93, rstd("m_rstd", "m_ms")), (5.94, m_twice), (19.6, m_rd(0)), (21.01, m_rd(1)), (22.2, m_rd(2)),
                (26.91, m_rd(3)), (41.691, rstd("n0_rstd", "n0_eps")),
                (44.038, resid("c_resid", "n0_done", "xbo0")), (63.04, rstd("n1_rstd", "n1_eps")),
                (115.51, rstd("n2_rstd", "n2_eps")), (117.69, resid("l_resid", "n2_done", "lbo")), (126.13, x_zero),
                (140.923, rstd("n3_rstd", "n3_eps")), (143.455, resid("x_resid", "n3_done", "xbo1")),
                (205.156, rstd("n4_rstd", "n4_eps")), (241.316, rstd("n5_rstd", "n5_eps")),
            ])



def kernel(**a):
    import numpy as np
    import concourse.bacc as bacc
    from concourse.bass_utils import run_bass_kernel_spmd

    f = {k: np.asarray(v) for k, v in a.items()}
    col = lambda v: v.reshape(-1, 1)
    rows = lambda v, n: v.reshape(n, P, -1).transpose(1, 0, 2)
    order = np.array([HD * (4 * (pos % 4) + pos // 4) + d for d in range(HD) for pos in range(NH)])
    w = {
        "normw": col(f["L0_attn_norm_w"]), "inT": f["L0_attn_in_proj_w"].T,
        "convw": rows(f["L0_attn_conv_w"], 2), "convb": rows(f["L0_attn_conv_b"], 2)[:, :, 0],
        "negA": f["L0_attn_A_log"], "D2": np.repeat(f["L0_attn_D"], PD).reshape(2, P).T,
        "dtb": col(f["L0_attn_dt_bias"]), "outT": rows(f["L0_attn_out_proj_w"].T, 2),
        "wq0": f["L0_xattn_Wq"].T, "xbq0": col(f["L0_xattn_bq"]), "wk0": f["L0_xattn_Wk"].T,
        "xbk0": col(f["L0_xattn_bk"]), "wo0": f["L0_xattn_Wo"].T, "xbo0": f["L0_xattn_bo"],
        "gate": f["L0_ffn_gate_w"], "w1": f["L0_ffn_w1"].transpose(1, 0, 2),
        "w2": f["L0_ffn_w2"].reshape(NE0, FT0, P, P).transpose(2, 0, 1, 3),
        "lqkv": f["L1_attn_W_qkv"], "lout": f["L1_attn_W_out"], "lbo": f["L1_attn_b_out"],
        "wq1": f["L1_xattn_Wq"][order].T, "xbq1": col(f["L1_xattn_bq"][order]),
        "wk1": f["L1_xattn_Wk"][order].T, "xbk1": col(f["L1_xattn_bk"][order]),
        "wv1": f["L1_xattn_Wv"].T, "xbv": f["L1_xattn_bv"], "wo1": f["L1_xattn_Wo"].T, "xbo1": f["L1_xattn_bo"],
        "wg": f["L1_ffn_Wg"], "bg": col(f["L1_ffn_bg"]), "we1": f["L1_ffn_W1"].transpose(1, 0, 2),
        "b1": f["L1_ffn_b1"].reshape(NE1 * FT1, P).T,
        "we2": f["L1_ffn_W2"].reshape(NE1, FT1, P, P).transpose(2, 0, 1, 3), "b2": f["L1_ffn_b2"],
    }
    x, ctx = f["x"], f["ctx_1024"]
    nb = x.shape[0]
    arrays = {
        "in_x": x.transpose(1, 0, 2).reshape(P, nb * P), "in_ctx": ctx.transpose(1, 0, 2).reshape(P, nb * P),
        "in_ctxT": ctx.transpose(2, 0, 1).reshape(P, nb * P),
        "in_mask": f["mask_BxS2_bk0"].reshape(1, nb * P),
    }
    arrays.update({"in_w_" + k: v for k, v in w.items()})
    arrays = {k: np.ascontiguousarray(v) for k, v in arrays.items()}
    nc = bacc.Bacc("TRN2", target_bir_lowering=False, num_devices=1)
    t = {k: nc.dram_tensor(k, v.shape, mybir.dt.from_np(v.dtype), kind="ExternalInput").ap() for k, v in arrays.items()}
    out = nc.dram_tensor("out", (P, nb * P), F32, kind="ExternalOutput").ap()
    decoder(nc, t["in_x"], t["in_ctx"], t["in_ctxT"], t["in_mask"], {k: t["in_w_" + k] for k in w}, out)
    r = run_bass_kernel_spmd(nc, [arrays], core_ids=[0])
    y = r.results[0]["out"]
    return y.reshape(P, nb, P).transpose(1, 0, 2)
```

```python
from contextlib import ExitStack

import numpy as np

import concourse.bass as bass
from concourse import mybir

ALU = mybir.AluOpType
ACT = mybir.ActivationFunctionType
AX = mybir.AxisListType
F32 = mybir.dt.float32
BF16 = mybir.dt.bfloat16
U8 = mybir.dt.uint8
U32 = mybir.dt.uint32

P = 128
GB = 4
W = GB * P
LANES = 2
HS, PD = 4, 64
NE0, HID0, CAP = 8, 512, 32
FT0 = HID0 // P
NH, HD = 16, 8
NE1, HID1 = 6, 256
FT1 = HID1 // P
SLOTS = 6
KROWS = SLOTS * HD
SHIFT0 = 2 * KROWS
SROWS = SHIFT0 + 4
MASKED = -1e30
N_CONSTANTS = 6
TWO_ONES = float(np.uint32(0x3F803F80).view(np.float32))
LN_EPS, RMS_EPS, DEN_EPS = 1e-5, 1e-6, 1e-6
TINY = 2.0 ** -26

WEIGHTS = {
    "mamba": "columns shapes rows inT dtT",
    "cross": "outT wq0 wk0 wo0",
    "choice": "gate w1 w2",
    "linear": "lqkv lout",
    "heads": "wq1 wk1 wv1 wo1",
    "mixture": "wg b2 we1 we2",
}
COLUMNS = {"normw": 1, "D2": 2, "convw0": 4, "convw1": 4, "convb": 2, "dtb": 1, "xbq0": 1, "xbk0": 1, "xbq1": 1,
           "xbk1": 1, "bg": 1, "b1": NE1 * FT1}
SHAPES = {
    "ident": P, "tri": P,
    "strict": P,
    "head_mask": P,
    "head_cols": NH,
    "ones_of_head": 4 * 32,
    "tok_id": 1, "tok_row": P,
    "own_col": 32,
    "own_quarter": 4,
    "own_row": 2 * GB,
    "before": NE1 * NE1,
}
ROWS = {"A_log": HS, "xbo0": P, "lbo": P, "xbv": P, "xbo1": P}

SEQUENCES = {
    "mamba_pe": "m_xt m_xs0 m_xs1 m_b m_c m_dtt m_gram m_dt m_z0 m_z1 m_xhr0 m_xhr1 m_out0 m_out1",
    "mamba_act": "m_xt_sb m_b_sb m_c_sb m_dtt_sb m_tanh0 m_tanh1 m_dt_exp m_dt_ln m_tz0 m_tz1",
    "mamba_dve": "m_stats m_moments m_sq m_ms m_norm0 m_norm1 m_norm2 m_norm3"
                 " m_tap00 m_tap01 m_tap02 m_tap03 m_tap10 m_tap11 m_tap12 m_tap13"
                 " m_xh0 m_xh1 m_gram_sb m_dt_sb m_dt_abs m_dt_one m_dt_den m_dt_rec m_dt_ratio m_dt_log1p m_dt_done"
                 " m_decay m_half m_sz0 m_sz1 m_dtx0 m_dtx1"
                 " m_skip00 m_skip01 m_gate00 m_gate01 m_skip10 m_skip11 m_gate10 m_gate11",
    "norm_dve": " ".join(f"n{n}_res0 n{n}_res1 n{n}_stats n{n}_mom n{n}_eps n{n}_row0 n{n}_row1 n{n}_row2 n{n}_row3"
                         for n in range(6)),
    "norm_pool": "m_rstd n0_rstd n1_rstd n2_rstd n3_rstd n4_rstd n5_rstd",
    "cross_pe": "c_kt c_xt c_q c_scores c_pt c_ot c_out0 c_out1",
    "cross_act": "c_kt_sb c_xt_sb c_q_sb c_exp0 c_exp1 c_exp2 c_exp3 c_ot_sb",
    "cross_dve": "c_mask c_max c_rsum c_pt_sb",
    "choice_pool": "f_scat",
    "resid_pool": "m_twice c_resid l_resid x_resid",
    "choice_pe": "f_xt f_gt f_g f_pt f_bc0 f_bc1 f_rows f_xi f_add",
    "choice_act": "f_xt_sb f_gt_sb f_gexp f_xi_sb1 f_y_sb0 f_y_sb1 f_add_sb",
    "choice_dve": "f_gmax f_gsub f_gsum f_grec f_prob f_pt_sb"
                  + "".join(f" f_topv{r} f_topi{r} f_topw{r}" for r in range(CAP // 8))
                  + " f_idx f_idxm0 f_idxm1 f_rowsel f_onehot f_xi_sb0 f_rows_sb",
    "linear_pe": "l_xt l_kv0 l_kv1 l_q l_kv l_num l_at l_out0 l_out1",
    "linear_act": "l_xt_sb l_ek l_v l_eq l_at_sb",
    "linear_dve": "l_kmin l_kf l_qmin l_qf l_kvm l_zm l_den l_rec l_att",
    "heads_pe": "x_k x_v0 x_v1 x_xt x_q x_nmt x_out0 x_out1",
    "heads_act": "x_k_sb x_k_h x_xt_sb x_q_sb x_q_h",
    "heads_dve": "x_v_sb x_k_r1 x_k_m x_k_l x_q_r1 x_q_m x_q_l x_nm_h x_nm_l"
                 + "".join(f" x_rden{b} x_att{b}" for b in range(GB)),
    "heads_pool": "x_zero",
    "mixture_pe": "e_xt e_gt e_g e_ct e_b20 e_b21",
    "mixture_act": "e_xt_sb e_gt_sb e_exp e_ct_sb",
    "mixture_dve": "e_g_sb e_above e_equal e_tied e_rank1 e_rank e_sel e_max e_sub e_msel e_sum e_rec e_comb e_acc0",
}
COUNTED = {"m_rd": GB, "m_seg": GB, "m_yb": GB, "m_l": GB, "m_mix": GB, "f_up": NE0, "f_act": NE0, "f_down": NE0,
           "x_a": 4 * GB, "x_amax": 4 * GB, "x_b": 4 * GB, "x_p": 4 * GB, "x_pv": 4 * GB,
           "e_up": NE1 * FT1, "e_act": NE1 * FT1, "e_down": NE1, "e_acc": NE1 - 1}


PERIOD, LAG = 216.62, 14.5


def schedule(steps):
    assert all(a[0] <= b[0] for a, b in zip(steps, steps[1:]))
    first = [(step, 0, 0) for due, step in steps if due < LAG]
    turns = [(due + (PERIOD if due < LAG else 0), 0, int(due < LAG), step) for due, step in steps]
    turns += [(due + LAG, 1, 0, step) for due, step in steps]
    steady = [(step, g, ahead) for _, g, ahead, step in sorted(turns, key=lambda turn: turn[:2])]
    return first, steady, [turn for turn in steady if not turn[2]]


def decoder(nc, x, ctx_r, ctx_t, mask, w, out):
    pairs = x.shape[1] // (W * LANES)
    stack = ExitStack()

    def sb(name, shape, dt=F32):
        return stack.enter_context(nc.sbuf_tensor(name, shape, dt))

    with stack:
        sequence = {q: [stack.enter_context(nc.semaphore(f"{q}{g}")) for g in range(LANES)] for q in SEQUENCES}
        counted = {name: [stack.enter_context(nc.semaphore(f"{name}_{g}")) for g in range(LANES)] for name in COUNTED}
        constants = stack.enter_context(nc.semaphore("constants"))
        stacks_set = [stack.enter_context(nc.semaphore(f"stacks_set{g}")) for g in range(LANES)]
        scaled = stack.enter_context(nc.semaphore("scaled"))
        home = {step: (q, n) for q, steps in SEQUENCES.items() for n, step in enumerate(steps.split())}
        taken = {(q, g): 0 for q in SEQUENCES for g in range(LANES)}

        def at(i, g, step):
            q, n = home[step]
            return sequence[q][g], i * len(SEQUENCES[q].split()) + (n + 1)

        def sig(step, g):
            q, _ = home[step]
            steps = SEQUENCES[q].split()
            assert step == steps[taken[q, g] % len(steps)], step
            taken[q, g] += 1
            return sequence[q][g]

        def run(eng, steps):
            def take(turns, i):
                for step, g, ahead in turns:
                    step(i + 1 if ahead else i, g)

            first, steady, last = schedule(steps)
            take(first, 0)
            if pairs > 1:
                with eng.Fori(0, pairs - 1, 1) as i:
                    take(steady, i)
            take(last, pairs - 1)

        weights_in = {part: stack.enter_context(nc.semaphore(f"weights_in_{part}")) for part in WEIGHTS}
        x_in = [stack.enter_context(nc.semaphore(f"x_in{g}")) for g in range(LANES)]
        ctx_in = [stack.enter_context(nc.semaphore(f"ctx_in{g}")) for g in range(LANES)]
        rows_moved = [stack.enter_context(nc.semaphore(f"rows_moved{g}")) for g in range(LANES)]
        rows_out = [[stack.enter_context(nc.semaphore(f"rows_out{g}{half}")) for half in range(2)]
                    for g in range(LANES)]
        q_out = [stack.enter_context(nc.semaphore(f"q_out{g}")) for g in range(LANES)]
        q_in = [stack.enter_context(nc.semaphore(f"q_in{g}")) for g in range(LANES)]
        k_out = [stack.enter_context(nc.semaphore(f"k_out{g}")) for g in range(LANES)]
        k_in = [stack.enter_context(nc.semaphore(f"k_in{g}")) for g in range(LANES)]
        shift_in = [stack.enter_context(nc.semaphore(f"shift_in{g}")) for g in range(LANES)]
        lane_free = [stack.enter_context(nc.semaphore(f"lane_free{g}")) for g in range(LANES)]

        wt = {name: sb("w_" + name, [P, sum(ROWS.values())] if name == "rows" else list(ap.shape))
              for name, ap in w.items()}

        def parts_of(tile_, widths):
            ends = np.cumsum(list(widths.values()))
            return {name: tile_[:, int(end) - width:int(end)] for (name, width), end in zip(widths.items(), ends)}

        col, row, shape = (parts_of(wt[name], widths)
                           for name, widths in (("columns", COLUMNS), ("rows", ROWS), ("shapes", SHAPES)))

        def loaded(part):
            return weights_in[part], 16 * len(WEIGHTS[part].split())

        ident, tri, strict, head_mask, head_cols, tok_id, tok_row = (
            shape[name] for name in ("ident", "tri", "strict", "head_mask", "head_cols", "tok_id", "tok_row"))
        ones_of_head = shape["ones_of_head"].rearrange("p (c m) -> p c m", c=4)
        own_col, own_quarter = shape["own_col"][0:32], shape["own_quarter"][0:32]
        own_row = shape["own_row"][0:32].rearrange("p (b h) -> p b h", b=GB)
        before = shape["before"].rearrange("p (e j) -> p e j", e=NE1)
        ones_row = sb("ones_row", [32, P], BF16)
        ones = sb("ones", [P, 1])
        neg_half = sb("neg_half", [P, GB])
        a_half = sb("a_half", [P, 2])
        neg_a = sb("neg_a", [P, HS])
        neg_a_exp = sb("neg_a_exp", [P, HS])
        wq_scaled_bias = sb("wq_scaled_bias", [P, 1])
        spare = sb("spare", [P, LANES])

        def lane(name, dims, dt=F32):
            return [sb(f"{name}{g}", dims, dt) for g in range(LANES)]

        def seqs(ap):
            return ap.rearrange("p (b n) -> p b n", b=GB)

        def flat(ap):
            return (ap if isinstance(ap, bass.AP) else ap[:]).rearrange("p b n -> p (b n)")

        def spread(ap, axis, count):
            v = ap.unsqueeze(axis)
            return v.broadcast_to(tuple(v.shape[:axis]) + (count,) + tuple(v.shape[axis + 1:]))

        X = lane("X", [P, GB, P])
        CR = lane("CR", [P, GB, P])
        CT = lane("CT", [P, GB, P])
        MK = lane("MK", [1, W], U8)
        MB = lane("MB", [1, W], BF16)
        R = lane("R", [P, GB, P])
        T = lane("T", [P, GB, P])
        A03 = lane("A03_", [P, 4, W])
        A47 = lane("A47_", [P, 4, W])
        A = [[seqs((A03 if n < 4 else A47)[g][:, n % 4, :]) for g in range(LANES)] for n in range(8)]
        VM = [A47[g][:].rearrange("p b (h m) -> p b h m", m=32) for g in range(LANES)]
        B16 = lane("B16", [P, W], BF16)
        HFW = lane("HF_", [P, 4, W])
        HF = [[HFW[g][:, 2 * n:2 * n + 2, :] for g in range(LANES)] for n in range(2)]
        HTW = lane("HT_", [P, 2, W])
        HT = [[HTW[g][:, n, :].rearrange("p (f n) -> p f n", f=FT0) for g in range(LANES)] for n in range(2)]
        PTW = lane("PT_", [P, 2, W])
        PT = [[PTW[g][:, n, :].rearrange("p (h n) -> p h n", h=4) for g in range(LANES)] for n in range(2)]
        PARTS = [[(HTW if n < 4 else PTW)[g][:, (n % 4) // 2, (n % 2) * (W // 2):(n % 2 + 1) * (W // 2)].bitcast(BF16)
                  for g in range(LANES)] for n in range(6)]
        gT = [HTW[g][:, 0, 0:P] for g in range(LANES)]
        cT = [HTW[g][0:NE1, 1, :] for g in range(LANES)]
        idxm = [HTW[g][0:32, 1, :].bitcast(BF16).rearrange("p (c k) -> p c k", k=CAP) for g in range(LANES)]
        HFF = [HFW[g][:].rearrange("p a n -> p (a n)") for g in range(LANES)]
        vx = [HFF[g][:, 0:GB * (P + 2)].rearrange("p (b n) -> p b n", b=GB) for g in range(LANES)]
        r144 = [HFF[g][:, 2 * W:2 * W + GB * (P + NH)].rearrange("p (b n) -> p b n", b=GB) for g in range(LANES)]
        QS = lane("QS", [SROWS, NH // 2, 2, W], BF16)
        KS = lane("KS", [SROWS, NH // 2, W], BF16)
        st6 = lane("st6", [P, GB, 6])
        mv = lane("mv", [P, GB, 2])
        sm = [lane(f"sm{n}_", [P, 64]) for n in range(8)]
        small = [lane(f"small{n}_", [32, P]) for n in range(5)]
        topv = lane("topv", [32, CAP])
        topi = lane("topi", [32, CAP], U32)
        nmp = [[HTW[g][0:NH, n, 0:W // 2].bitcast(BF16) for g in range(LANES)] for n in range(2)]
        bank = [[stack.enter_context(nc.psum_tensor(f"bank{g}{k}", [P, W], F32)) for k in range(4)]
                for g in range(LANES)]
        q_parts = [nc.dram_tensor(f"q_parts{g}", [SLOTS, P, W], BF16, kind="Internal").ap() for g in range(LANES)]
        k_parts = [nc.dram_tensor(f"k_parts{g}", [SLOTS, P, W], BF16, kind="Internal").ap() for g in range(LANES)]
        y_rows = [nc.dram_tensor(f"y_rows{g}", [2, P, W], F32, kind="Internal").ap() for g in range(LANES)]

        def apart(eng):
            eng.nop(nofuse=True)

        def expert_cols(g, n):
            return A47[g][:, 2:4, :].rearrange("p t (e b k) -> p (t e) b k", e=4, b=GB)[:, :, 2 * n:2 * n + 2, :]

        def set_stacks(eng, g):
            eng.memset(QS[g][:].rearrange("p r j n -> p (r j n)").bitcast(F32), 0.0).then_inc(stacks_set[g], 1)
            eng.wait_ge(stacks_set[g], 1)
            eng.memset(KS[g][SHIFT0:SROWS].rearrange("p r n -> p (r n)").bitcast(F32), TWO_ONES)\
                .then_inc(stacks_set[g], 1)
            eng.wait_ge(stacks_set[g], 2)

        def gate_rows(g, k, count):
            return bank[g][k][:, 0:P].rearrange("p (b e) -> p b e", b=GB)[:, :, 0:count]

        def bank_experts(g, n):
            return bank[g][n][:].rearrange("p (b e k) -> p e b k", b=2, k=CAP)

        def nth(i, g, step, k):
            return i * COUNTED[step] + (k + 1)

        block = stack.enter_context(nc.Block())

        @block.sync
        def _(sp):
            def load_x(i, g):
                sp.dma_start(A47[g][:, 0, :], x[:, columns_of(i, g)]).then_inc(x_in[g], 16)

            def load_ctx(i, g):
                cols = columns_of(i, g)
                sp.dma_start(flat(CT[g]), ctx_t[:, cols]).then_inc(ctx_in[g], 16)
                sp.dma_start(MK[g][:], mask[:, cols]).then_inc(ctx_in[g], 16)
                sp.dma_start(flat(CR[g]), ctx_r[:, cols]).then_inc(ctx_in[g], 16)

            def columns_of(i, g):
                return bass.ds(i * (LANES * W) + g * W, W)

            def load_weights(part):
                for name in WEIGHTS[part].split():
                    src = w[name].partition_broadcast(P) if name == "rows" else w[name]
                    sp.dma_start(wt[name][:], src).then_inc(weights_in[part], 16)

            def load_next(i, g):
                if isinstance(i, int) and i == pairs - 1:
                    return
                sp.wait_ge(counted["x_pv"][g], nth(i, g, "x_pv", 4 * GB - 1))
                load_x(i + 1, g)
                load_ctx(i + 1, g)

            def rows_to_dram(half):
                def step(i, g):
                    sp.wait_ge(*at(i, g, f"f_y_sb{half}"))
                    sp.dma_start(y_rows[g][half], A03[g][:, 2 + half, :]).then_inc(rows_out[g][half], 16)
                return step

            def rows_back(half):
                def step(i, g):
                    sp.wait_ge(rows_out[g][half], i * 16 + 16)
                    for q in range(4):
                        sp.dma_start(A[4 + half][g][32 * q:32 * q + 32],
                                     y_rows[g][half].rearrange("(b k) (q d) -> q k b d", b=GB, q=4)[q])\
                            .then_inc(rows_moved[g], 16)
                return step

            def q_to_dram(part):
                slots = {"h": slice(0, 3), "m": slice(3, 5), "l": slice(5, 6)}[part]

                def step(i, g):
                    sp.wait_ge(*at(i, g, f"x_q_{part}"))
                    to_slots(q_parts[g][slots], PARTS["hml".index(part)][g]).then_inc(q_out[g], 16)
                return step

            def to_slots(slots, part):
                return sp.dma_start(slots.rearrange("s p n -> p s n"), spread(part, 1, slots.shape[0]))

            def k_to_dram(i, g):
                sp.wait_ge(*at(i, g, "x_k_l"))
                for part, slots in ((0, slice(4, 6)), (0, slice(0, 1)), (1, slice(1, 4, 2)), (2, slice(2, 3))):
                    to_slots(k_parts[g][slots], PARTS[3 + part][g]).then_inc(k_out[g], 16)

            def stack_k(i, g):
                sp.wait_ge(stacks_set[g], 2)
                sp.wait_ge(k_out[g], i * 64 + 64)
                kd = k_parts[g].rearrange("s (d r j) n -> (s d) r j n", d=HD, j=2)
                for j in range(2):
                    sp.dma_start(KS[g][KROWS * j:KROWS * j + KROWS], kd[:, :, j]).then_inc(k_in[g], 16)

            def stack_q(i, g):
                sp.wait_ge(q_out[g], i * 48 + 48)
                qd = q_parts[g].rearrange("s (d r j) n -> (s d) r j n", d=HD, j=2)
                for j in range(2):
                    sp.dma_start(QS[g][KROWS * j:KROWS * j + KROWS, :, j], qd[:, :, j]).then_inc(q_in[g], 16)

            def stack_shift(i, g):
                sp.wait_ge(*at(i, g, "x_nm_l"))
                for n in range(2):
                    for j in range(2):
                        row = SHIFT0 + 2 * j + n
                        sp.dma_start(QS[g][row:row + 1, :, j], nmp[n][g][j:NH:2])\
                            .then_inc(shift_in[g], 16)

            def store(i, g):
                sp.wait_ge(*at(i, g, "n5_row3"))
                sp.dma_start(out[:, bass.ds(i * (LANES * W) + g * W, W)],
                             flat(X[g])).then_inc(lane_free[g], 16)

            load_x(0, 0)
            load_weights("mamba")
            load_x(0, 1)
            load_ctx(0, 0)
            load_weights("cross")
            load_ctx(0, 1)
            for part in ("choice", "linear", "heads", "mixture"):
                load_weights(part)
            run(sp, [
                (55.331, rows_to_dram(0)), (55.931, rows_back(0)), (55.931, rows_to_dram(1)),
                (57.431, rows_back(1)), (78.747, k_to_dram), (78.747, stack_k), (78.747, q_to_dram("h")),
                (78.747, q_to_dram("m")), (78.747, q_to_dram("l")), (78.747, stack_q), (104.125, stack_shift),
                (135.239, load_next), (203.544, store),
            ])
            for g in range(LANES):
                sp.wait_ge(lane_free[g], 16 * pairs + 16)

        @block.tensor
        def _(pe):
            pe.wait_ge(*loaded("mamba"))
            pe.wait_ge(constants, N_CONSTANTS)
            mm, tr = pe.matmul, pe.transpose

            def to_c(g, k, src, step, ready=(None,) * GB):
                for b in range(GB):
                    if ready[b]:
                        pe.wait_ge(*ready[b])
                    last = tr(bank[g][k][:, b * P:(b + 1) * P], src[:, b, :], ident)
                last.then_inc(sig(step, g), 1)

            def wide(g, k, lhsT, rhs, step):
                mm(bank[g][k][0:lhsT.shape[1], :], lhsT, rhs, start=True, stop=True).then_inc(sig(step, g), 1)

            def gates(g, k, lhsT, step):
                for b in range(GB):
                    last = mm(bank[g][k][32 * b:32 * b + 32, 0:P], lhsT, T[g][:, b, :], start=True, stop=True)
                last.then_inc(sig(step, g), 1)

            def m_xt(i, g):
                to_c(g, 0, R[g], "m_xt", [at(i, g, f"m_norm{b}") for b in range(GB)])

            def m_proj(i, g):
                pe.wait_ge(*loaded("mamba"))
                pe.wait_ge(*at(i, g, "m_xt_sb"))
                t = flat(T[g])
                wide(g, 1, wt["inT"][:, 256:384], t, "m_xs0")
                wide(g, 2, wt["inT"][:, 384:512], t, "m_xs1")
                wide(g, 3, wt["inT"][:, 512:640], t, "m_b")
                wide(g, 0, wt["inT"][:, 640:768], t, "m_c")

            def m_dtt(i, g):
                pe.wait_ge(*at(i, g, "m_b_sb"))
                gates(g, 3, wt["dtT"][:], "m_dtt")

            def m_gram(i, g):
                pe.wait_ge(*at(i, g, "m_c_sb"))
                for b in range(GB):
                    last = mm(bank[g][0][:, b * P:(b + 1) * P], A[0][g][:, b, :], A[1][g][:, b, :],
                              start=True, stop=True)
                last.then_inc(sig("m_gram", g), 1)

            def m_dt(i, g):
                pe.wait_ge(*at(i, g, "m_dtt_sb"))
                apart(pe)
                tr(bank[g][3][:, 0:P], gT[g], ident).then_inc(sig("m_dt", g), 1)

            def m_z(i, g):
                t = flat(T[g])
                pe.wait_ge(*at(i, g, "m_xh0"))
                wide(g, 1, wt["inT"][:, 0:128], t, "m_z0")
                pe.wait_ge(*at(i, g, "m_xh1"))
                wide(g, 2, wt["inT"][:, 128:256], t, "m_z1")

            def m_rows(i, g):
                pe.wait_ge(*at(i, g, "m_gram_sb"))
                to_c(g, 0, A[2][g], "m_xhr0")
                pe.wait_ge(*at(i, g, "m_dt_sb"))
                to_c(g, 3, A[3][g], "m_xhr1")

            def m_seg(b):
                def step(i, g):
                    pe.wait_ge(*at(i, g, "m_dtx1"))
                    pe.wait_ge(counted["m_rd"][g], nth(i, g, "m_rd", b))
                    if b >= 2:
                        pe.wait_ge(counted["m_l"][g], nth(i, g, "m_l", b - 2))
                    mm(bank[g][b % 2][:], strict, PTW[g][:, b % 2, :],
                       start=True, stop=True).then_inc(counted["m_seg"][g], 1)
                return step

            def m_yb(b):
                def step(i, g):
                    pe.wait_ge(counted["m_mix"][g], nth(i, g, "m_mix", b))
                    for h in range(HS):
                        rows = slice(PD * (h % 2), PD * (h % 2) + PD)
                        last = mm(bank[g][2 + b // 2][rows, (2 * (h // 2) + b % 2) * P:(2 * (h // 2) + b % 2 + 1) * P],
                                  A[4 + h // 2][g][:, b, PD * (h % 2):PD * (h % 2) + PD],
                                  HT[b % 2][g][:, h, :], start=True, stop=True)
                    last.then_inc(counted["m_yb"][g], 1)
                return step

            def m_out(i, g):
                pe.wait_ge(*loaded("cross"))
                for b in range(GB):
                    if b % 2 == 0:
                        pe.wait_ge(*at(i, g, f"m_gate{b // 2}1"))
                    for c in range(2):
                        last = mm(bank[g][b // 2][:, b * P:(b + 1) * P], A[6 + c][g][:, b, :],
                                  wt["outT"][:, c, :], start=(c == 0), stop=(c == 1))
                    if b % 2:
                        last.then_inc(sig(f"m_out{b // 2}", g), 1)

            def c_kt(i, g):
                pe.wait_ge(*loaded("cross"))
                pe.wait_ge(ctx_in[g], i * 48 + 48)
                pe.wait_ge(*at(i, g, "m_skip11"))
                wide(g, 3, wt["wk0"][:], flat(CT[g]), "c_kt")

            def c_xt(i, g):
                to_c(g, 0, X[g], "c_xt", [at(i, g, f"n0_row{b}") for b in range(GB)])

            def c_q(i, g):
                pe.wait_ge(*at(i, g, "c_xt_sb"))
                wide(g, 1, wt["wq0"][:], flat(T[g]), "c_q")

            def c_scores(i, g):
                pe.wait_ge(*at(i, g, "c_mask"))
                pe.wait_ge(*at(i, g, "c_q_sb"))
                mm(bank[g][2][:], ones_row[0:1, :], MB[g][:], start=True, stop=False, skip_group_check=True)
                for b in range(GB):
                    last = mm(bank[g][2][:, b * P:(b + 1) * P], A[1][g][:, b, :], A[0][g][:, b, :],
                              start=False, stop=True, skip_group_check=True)
                last.then_inc(sig("c_scores", g), 1)

            def c_pt(i, g):
                to_c(g, 3, A[2][g], "c_pt", [at(i, g, f"c_exp{b}") for b in range(GB)])

            def c_ot(i, g):
                pe.wait_ge(*at(i, g, "c_pt_sb"))
                for b in range(GB):
                    last = mm(bank[g][0][:, b * P:(b + 1) * P], CR[g][:, b, :], A[3][g][:, b, :],
                              start=True, stop=True)
                last.then_inc(sig("c_ot", g), 1)

            def rows_times(g, k, lhs, rhs, step):
                for b in range(GB):
                    last = mm(bank[g][k[b // 2]][:, b * P:(b + 1) * P], lhs[:, b, :], rhs, start=True, stop=True)
                    if b % 2:
                        last.then_inc(sig(f"{step}{b // 2}", g), 1)

            def c_out(i, g):
                pe.wait_ge(*at(i, g, "c_ot_sb"))
                rows_times(g, (1, 2), A[4][g], wt["wo0"][:], "c_out")

            def f_xt(i, g):
                to_c(g, 0, X[g], "f_xt", [at(i, g, f"n1_row{b}") for b in range(GB)])

            def f_gt(i, g):
                pe.wait_ge(*loaded("choice"))
                pe.wait_ge(*at(i, g, "f_xt_sb"))
                gates(g, 1, wt["gate"][:], "f_gt")

            def f_gate_rows(i, g):
                pe.wait_ge(*at(i, g, "f_gt_sb"))
                apart(pe)
                tr(bank[g][2][:, 0:P], gT[g], ident).then_inc(sig("f_g", g), 1)

            def f_prob_t(i, g):
                pe.wait_ge(*at(i, g, "f_prob"))
                tr(bank[g][3][0:32, 0:P], sm[2][g][:, 0:32], ident).then_inc(sig("f_pt", g), 1)

            def f_spread(i, g):
                for n in range(2):
                    pe.wait_ge(*at(i, g, f"f_idxm{n}"))
                    mm(bank[g][n][:], ones_row[:], idxm[g][:, 16 * n:16 * n + 16, :], start=True, stop=True)\
                        .then_inc(sig(f"f_bc{n}", g), 1)
                pe.wait_ge(*at(i, g, "f_rowsel"))
                for n in range(2):
                    last = mm(bank[g][2][:, 8 * n:8 * n + 8], small[3 + n][g][:],
                              own_row.rearrange("p b h -> p (b h)"), start=True, stop=True)
                last.then_inc(sig("f_rows", g), 1)

            def f_gather(i, g):
                pe.wait_ge(*at(i, g, "f_onehot"))
                for b in range(GB):
                    for n in range(2):
                        last = mm(bank[g][b // 2][:, (b % 2) * 256 + n * P:(b % 2) * 256 + n * P + P], X[g][:, b, :],
                                  A[n][g][:, :, b * CAP:(b + 1) * CAP], start=True, stop=True)
                last.then_inc(sig("f_xi", g), 1)

            def f_up(e):
                def step(i, g):
                    if e == 0:
                        pe.wait_ge(*at(i, g, "f_xi_sb0"))
                        pe.wait_ge(*at(i, g, "f_xi_sb1"))
                    if e >= 2:
                        pe.wait_ge(counted["f_act"][g], nth(i, g, "f_act", e - 2))
                    for f in range(FT0):
                        last = mm(bank[g][e % 2][:, f * P:(f + 1) * P], wt["w1"][:, e, f * P:(f + 1) * P],
                                  A[6 + e // 4][g][:, e % 4, :], start=True, stop=True)
                    last.then_inc(counted["f_up"][g], 1)
                return step

            def f_down(e):
                def step(i, g):
                    if e == 0:
                        pe.wait_ge(*at(i, g, "f_rows_sb"))
                    pe.wait_ge(counted["f_act"][g], nth(i, g, "f_act", e))
                    for f in range(FT0):
                        last = mm(bank[g][2 + e // 4][:, (e % 4) * P:(e % 4 + 1) * P], HT[e % 2][g][:, f, :],
                                  wt["w2"][:, e, f, :], start=(f == 0), stop=(f == FT0 - 1))
                    last.then_inc(counted["f_down"][g], 1)
                return step

            def f_add(i, g):
                pe.wait_ge(*at(i, g, "f_scat"))
                pe.wait_ge(rows_moved[g], i * (8 * 16) + 8 * 16)
                for b in range(GB):
                    for h in range(2):
                        last = mm(bank[g][0][:, b * P:(b + 1) * P], HFW[g][:, h, b * P:(b + 1) * P],
                                  A[4 + h][g][:, b, :], start=(h == 0), stop=(h == 1))
                last.then_inc(sig("f_add", g), 1)

            def l_xt(i, g):
                to_c(g, 0, X[g], "l_xt", [at(i, g, f"n2_row{b}") for b in range(GB)])

            def l_q(i, g):
                pe.wait_ge(*loaded("linear"))
                pe.wait_ge(*at(i, g, "l_xt_sb"))
                for b in range(GB):
                    last = mm(bank[g][2 + b // 2][:, (b % 2) * 256:(b % 2) * 256 + 256], T[g][:, b, :],
                              wt["lqkv"][:, P:3 * P], start=True, stop=True)
                    if b % 2:
                        last.then_inc(sig(f"l_kv{b // 2}", g), 1)
                wide(g, 1, wt["lqkv"][:, 0:P], flat(T[g]), "l_q")

            def l_kv(i, g):
                pe.wait_ge(*at(i, g, "l_kf"))
                pe.wait_ge(*at(i, g, "l_v"))
                for b in range(GB):
                    last = mm(bank[g][2 + b // 2][:, (b % 2) * 256:(b % 2) * 256 + P + 1], A[1][g][:, b, :],
                              vx[g][:, b, 0:P + 1], start=True, stop=True)
                last.then_inc(sig("l_kv", g), 1)

            def l_num(i, g):
                pe.wait_ge(*at(i, g, "l_zm"))
                for b in range(GB):
                    last = mm(bank[g][b // 2][:, (b % 2) * 256:(b % 2) * 256 + P + NH], A[0][g][:, b, :],
                              r144[g][:, b, :], start=True, stop=True)
                last.then_inc(sig("l_num", g), 1)

            def l_at(i, g):
                pe.wait_ge(*at(i, g, "l_att"))
                to_c(g, 2, A[2][g], "l_at")

            def l_out(i, g):
                pe.wait_ge(*at(i, g, "l_at_sb"))
                rows_times(g, (3, 2), A[3][g], wt["lout"][:], "l_out")

            def x_k(i, g):
                pe.wait_ge(*loaded("heads"))
                pe.wait_ge(*at(i, g, "l_att"))
                wide(g, 0, wt["wk1"][:], flat(CT[g]), "x_k")
                rows_times(g, (1, 1), CT[g], wt["wv1"][:], "x_v")

            def x_xt(i, g):
                to_c(g, 2, X[g], "x_xt", [at(i, g, f"n3_row{b}") for b in range(GB)])

            def x_q(i, g):
                pe.wait_ge(*at(i, g, "x_xt_sb"))
                wide(g, 3, wt["wq1"][:], flat(T[g]), "x_q")

            def x_max(b):
                def step(i, g):
                    if b == 0:
                        pe.wait_ge(stacks_set[g], 2)
                        pe.wait_ge(k_in[g], i * 32 + 32)
                        pe.wait_ge(q_in[g], i * 32 + 32)
                        pe.wait_ge(*at(i, g, "x_v_sb"))
                        pe.wait_ge(*at(i, g, "x_q_sb"))
                    for c in range(4):
                        n = 4 * b + c
                        if n >= 4:
                            pe.wait_ge(counted["x_amax"][g], nth(i, g, "x_amax", n - 4))
                        for m in range(4):
                            pos = 4 * c + m
                            last = mm(bank[g][n % 4][:, m * P:(m + 1) * P],
                                      QS[g][0:SHIFT0, pos // 2, pos % 2, b * P:(b + 1) * P],
                                      KS[g][0:SHIFT0, pos // 2, b * P:(b + 1) * P], start=True, stop=True)
                        last.then_inc(counted["x_a"][g], 1)
                return step

            def x_nmt(i, g):
                pe.wait_ge(counted["x_amax"][g], nth(i, g, "x_amax", 4 * GB - 1))
                for b in range(GB):
                    last = tr(bank[g][0][0:NH, b * P:(b + 1) * P], sm[0][g][:, b * NH:(b + 1) * NH], ident)
                last.then_inc(sig("x_nmt", g), 1)

            def x_weights(n):
                b, c = n // 4, n % 4

                def step(i, g):
                    if n == 0:
                        pe.wait_ge(shift_in[g], i * 64 + 64)
                        pe.wait_ge(*at(i, g, "x_nm_l"))
                    if n >= 2:
                        pe.wait_ge(counted["x_p"][g], nth(i, g, "x_p", n - 2))
                    for r in range(2):
                        last = mm(bank[g][n % 2][:, r * 256:(r + 1) * 256],
                                  KS[g][0:SROWS, 2 * c + r, b * P:(b + 1) * P],
                                  QS[g][0:SROWS, 2 * c + r, :, b * P:(b + 1) * P], start=True, stop=True)
                    last.then_inc(counted["x_b"][g], 1)
                return step

            def x_values(n):
                b, c = n // 4, n % 4

                def step(i, g):
                    if c == 0 and b >= 2:
                        pe.wait_ge(*at(i, g, f"x_att{b - 2}"))
                    pe.wait_ge(counted["x_p"][g], nth(i, g, "x_p", n))
                    for lhs, cols in ((VM[g][:, b, c::4], slice(0, P)),
                                      (spread(ones_of_head[:, c, :], 1, 4), slice(P, 2 * P))):
                        for m in range(4):
                            last = mm(bank[g][2 + b % 2][32 * m:32 * m + 32, cols], lhs[:, m],
                                      PT[n % 2][g][:, m, :], start=(c == 0 and cols.start == 0), stop=(c == 3),
                                      skip_group_check=True)
                    last.then_inc(counted["x_pv"][g], 1)
                return step

            def x_out(i, g):
                pe.wait_ge(*at(i, g, "x_att3"))
                rows_times(g, (0, 1), A[3][g], wt["wo1"][:], "x_out")

            def e_xt(i, g):
                to_c(g, 0, X[g], "e_xt", [at(i, g, f"n4_row{b}") for b in range(GB)])

            def e_gt(i, g):
                pe.wait_ge(*loaded("mixture"))
                pe.wait_ge(*at(i, g, "e_xt_sb"))
                gates(g, 1, wt["wg"][:], "e_gt")

            def e_gate_rows(i, g):
                pe.wait_ge(*at(i, g, "e_gt_sb"))
                apart(pe)
                tr(bank[g][2][:, 0:P], gT[g], ident).then_inc(sig("e_g", g), 1)

            def e_ct(i, g):
                pe.wait_ge(*at(i, g, "e_comb"))
                for b in range(GB):
                    last = tr(bank[g][2][0:NE1, b * P:(b + 1) * P], sm[6][g][:, b * NE1:(b + 1) * NE1], ident)
                last.then_inc(sig("e_ct", g), 1)

            def e_b2(i, g):
                pe.wait_ge(*at(i, g, "e_ct_sb"))
                rows_times(g, (3, 3), seqs(cT[g]), wt["b2"][:], "e_b2")

            def e_up(n):
                e, f = n // FT1, n % FT1

                def step(i, g):
                    if n == 0:
                        pe.wait_ge(*at(i, g, "e_gt_sb"))
                    if n >= 2:
                        pe.wait_ge(counted["e_act"][g], nth(i, g, "e_act", n - 2))
                    mm(bank[g][n % 2][:], wt["we1"][:, e, f * P:(f + 1) * P],
                       flat(T[g]), start=True, stop=True).then_inc(counted["e_up"][g], 1)
                return step

            def e_down(e):
                def step(i, g):
                    pe.wait_ge(counted["e_act"][g], nth(i, g, "e_act", FT1 * e + FT1 - 1))
                    if e == 1:
                        pe.wait_ge(*at(i, g, "e_acc0"))
                    if e >= 2:
                        pe.wait_ge(counted["e_acc"][g], nth(i, g, "e_acc", e - 2))
                    for b in range(GB):
                        for f in range(FT1):
                            last = mm(bank[g][2 + e % 2][:, b * P:(b + 1) * P], HF[e % 2][g][:, f, b * P:(b + 1) * P],
                                      wt["we2"][:, e, f, :], start=(f == 0), stop=(f == FT1 - 1))
                    last.then_inc(counted["e_down"][g], 1)
                return step

            run(pe, [
                (3.193, m_xt), (4.298, m_proj), (6, m_dtt), (9, m_gram), (9, m_dt), (17.506, m_z), (18.59, m_rows),
                (19.101, m_seg(0)), (21.516, m_seg(1)), (26.955, m_yb(0)), (26.955, m_seg(2)), (26.955, m_yb(1)),
                (28.929, m_seg(3)), (31.49, m_yb(2)), (32.722, m_yb(3)), (33.458, m_out), (33.458, c_kt),
                (42.014, c_xt), (45.435, c_q), (47.345, c_scores), (51.619, c_pt), (53.561, c_ot), (56.617, c_out),
                (63.894, f_xt), (64.793, f_gt), (65.493, f_gate_rows), (66.398, f_prob_t), (72.958, f_spread),
                (75.974, f_gather), (78.447, f_up(0)), (80.83, f_up(1)), (81.452, f_down(0)), (81.452, f_up(2)),
                (82.004, f_down(1)), (82.004, f_up(3)), (82.004, f_down(2)), (82.004, f_up(4)), (82.004, f_down(3)),
                (82.004, f_up(5)), (82.004, f_down(4)), (82.004, f_up(6)), (82.004, f_down(5)), (82.004, f_up(7)),
                (82.004, f_down(6)), (88.004, f_down(7)), (96.232, f_add), (105.779, l_xt), (105.779, l_q),
                (109.301, l_kv), (109.489, l_num), (116.341, l_at), (116.341, l_out), (116.341, x_k),
                (121.575, x_xt), (124.755, x_q), (138.782, x_max(0)), (140.355, x_max(1)), (148.765, x_max(2)),
                (149.919, x_max(3)), (153.204, x_nmt), (160.396, x_weights(0)), (163.149, x_weights(1)),
                (164.031, x_values(0)), (164.56, x_weights(2)), (164.56, x_values(1)), (165.104, x_weights(3)),
                (165.812, x_values(2)), (165.915, x_weights(4)), (165.915, x_values(3)), (165.915, x_weights(5)),
                (166.406, x_values(4)), (166.406, x_weights(6)), (166.406, x_values(5)), (168.657, x_weights(7)),
                (168.657, x_values(6)), (168.657, x_weights(8)), (169.695, x_values(7)), (169.695, x_weights(9)),
                (169.695, x_values(8)), (171.095, x_weights(10)), (172.426, x_values(9)), (173.826, x_weights(11)),
                (173.887, x_values(10)), (173.887, x_weights(12)), (173.887, x_values(11)),
                (173.887, x_weights(13)), (173.887, x_values(12)), (173.887, x_weights(14)),
                (173.887, x_values(13)), (173.887, x_weights(15)), (176.086, x_values(14)), (176.086, x_values(15)),
                (179.318, x_out), (183.749, e_xt), (185.403, e_gt), (186.949, e_gate_rows), (190.06, e_up(0)),
                (190.847, e_up(1)), (190.847, e_ct), (195.602, e_b2), (196.256, e_up(2)), (196.642, e_up(3)),
                (197.187, e_down(0)), (198.254, e_up(4)), (200.83, e_up(5)), (203.512, e_down(1)),
                (203.512, e_up(6)), (203.512, e_up(7)), (203.512, e_down(2)), (204.937, e_up(8)),
                (204.937, e_up(9)), (206.191, e_down(3)), (206.682, e_up(10)), (206.682, e_up(11)),
                (206.682, e_down(4)), (208.101, e_down(5)),
            ])

        @block.vector
        def _(dve):
            def const(ins):
                ins.then_inc(constants, 1)

            const(dve.memset(ones[:], 1.0))
            const(dve.memset(neg_half[:], -0.5))
            const(dve.memset(ones_row[:], 1.0))
            set_stacks(dve, 0)
            dve.wait_ge(*loaded("mamba"))
            const(dve.tensor_scalar(a_half[:], col["D2"], 0.5, None, ALU.mult))
            const(dve.tensor_scalar(wq_scaled_bias[:], col["xbq1"], HD ** -0.5, None, ALU.mult))
            dve.wait_ge(scaled, 1)
            const(dve.tensor_scalar(neg_a[:], neg_a_exp[:], -1.0, None, ALU.mult))
            dve.wait_ge(constants, N_CONSTANTS)

            def rsum(out_, in_, op=ALU.add, negate=False):
                return dve.tensor_reduce(out_, in_, AX.X, op, negate=negate)

            def stats_steps(i, g, src, pre, ready=(None, None)):
                for b in range(GB):
                    if b % 2 == 0 and ready[b // 2]:
                        dve.wait_ge(*ready[b // 2])
                        apart(dve)
                    last = dve.bn_stats(st6[g][:, b, :], src[:, b, :])
                last.then_inc(sig(f"{pre}_stats", g), 1)
                dve.wait_ge(*at(i, g, f"{pre}_stats"))
                apart(dve)
                for b in range(GB):
                    last = dve.bn_aggr(mv[g][:, b, :], st6[g][:, b, :])
                return last

            def norm_stats(n):
                def step(i, g):
                    stats_steps(i, g, R[g], f"n{n}", [at(i, g, f"n{n}_res{h}") for h in range(2)])\
                        .then_inc(sig(f"n{n}_mom", g), 1)
                    dve.wait_ge(*at(i, g, f"n{n}_mom"))
                    dve.tensor_scalar(sm[7][g][:, 0:GB], mv[g][:, :, 1], LN_EPS, None,
                                      ALU.add).then_inc(sig(f"n{n}_eps", g), 1)
                return step

            def norm_rows(n):
                def step(i, g):
                    if n == 0:
                        dve.wait_ge(lane_free[g], i * 16 + 16)
                    dve.wait_ge(*at(i, g, f"n{n}_rstd"))
                    for b in range(GB):
                        dve.tensor_scalar(X[g][:, b, :], R[g][:, b, :], mv[g][:, b, 0:1], sm[6][g][:, b:b + 1],
                                          ALU.subtract, ALU.mult).then_inc(sig(f"n{n}_row{b}", g), 1)
                return step

            def res(n, k, produced, resid, scale=None):
                def step(i, g):
                    dve.wait_ge(*at(i, g, resid))
                    for h in range(2):
                        dve.wait_ge(*at(i, g, f"{produced}{h}"))
                        dst, src = R[g][:, 2 * h:2 * h + 2], seqs(bank[g][k[h]][:])[:, 2 * h:2 * h + 2]
                        if scale:
                            ins = dve.scalar_tensor_tensor(dst, src, scale, dst, ALU.mult, ALU.add)
                        else:
                            ins = dve.tensor_tensor(dst, src, dst, ALU.add)
                        ins.then_inc(sig(f"n{n}_res{h}", g), 1)
                return step

            def m_stats(i, g):
                dve.wait_ge(x_in[g], i * 16 + 16)
                stats_steps(i, g, A[4][g], "m").then_inc(sig("m_moments", g), 1)
                dve.wait_ge(*at(i, g, "m_moments"))
                dve.tensor_tensor(sm[0][g][:, 0:GB], mv[g][:, :, 0], mv[g][:, :, 0], ALU.mult)\
                   .then_inc(sig("m_sq", g), 1)
                dve.wait_ge(*at(i, g, "m_sq"))
                dve.scalar_tensor_tensor(sm[7][g][:, 0:GB], mv[g][:, :, 1], RMS_EPS, sm[0][g][:, 0:GB],
                                         ALU.add, ALU.add).then_inc(sig("m_ms", g), 1)

            def m_norm(i, g):
                dve.wait_ge(*at(i, g, "m_rstd"))
                for b in range(GB):
                    dve.tensor_scalar(R[g][:, b, :], A[4][g][:, b, :], sm[6][g][:, b:b + 1], None, ALU.mult)\
                       .then_inc(sig(f"m_norm{b}", g), 1)

            def m_conv(i, g):
                for c in range(2):
                    dve.wait_ge(*at(i, g, f"m_xs{c}"))
                    u, xs = A[6 + c][g], seqs(bank[g][1 + c][:])
                    dve.tensor_scalar(u, xs, col[f"convw{c}"][:, 3:4], col["convb"][:, c:c + 1], ALU.mult, ALU.add)\
                       .then_inc(sig(f"m_tap{c}0", g), 1)
                    for k in range(1, 4):
                        dve.wait_ge(*at(i, g, f"m_tap{c}{k - 1}"))
                        dve.scalar_tensor_tensor(u[:, :, k:], xs[:, :, :P - k], col[f"convw{c}"][:, 3 - k:4 - k],
                                                 u[:, :, k:], ALU.mult, ALU.add).then_inc(sig(f"m_tap{c}{k}", g), 1)

            def m_silu(i, g):
                for c in range(2):
                    dve.wait_ge(*at(i, g, f"m_tanh{c}"))
                    dve.scalar_tensor_tensor(A[2 + c][g], seqs(HFW[g][:, 1 + c, :]), 1.0, A[6 + c][g],
                                             ALU.add, ALU.mult).then_inc(sig(f"m_xh{c}", g), 1)

            def m_gram(i, g):
                dve.wait_ge(*at(i, g, "m_gram"))
                dve.tensor_tensor(seqs(HFW[g][:, 0, :]), seqs(bank[g][0][:]), spread(tri, 1, GB), ALU.mult)\
                   .then_inc(sig("m_gram_sb", g), 1)

            def m_dt_rows(i, g):
                dve.wait_ge(*at(i, g, "m_dt"))
                dve.tensor_copy(sm[0][g][:, 0:16].rearrange("p (b h) -> p b h", b=GB), gate_rows(g, 3, HS))\
                   .then_inc(sig("m_dt_sb", g), 1)
                dve.wait_ge(*at(i, g, "m_dt_sb"))
                dve.scalar_tensor_tensor(sm[1][g][:, 0:16], sm[0][g][:, 0:16], -1.0, sm[0][g][:, 0:16],
                                         ALU.mult, ALU.max)\
                   .then_inc(sig("m_dt_abs", g), 1)

            def m_dt_one(i, g):
                dve.wait_ge(*at(i, g, "m_dt_exp"))
                dve.tensor_scalar(sm[3][g][:, 0:16], sm[2][g][:, 0:16], 1.0, None, ALU.add)\
                   .then_inc(sig("m_dt_one", g), 1)
                dve.wait_ge(*at(i, g, "m_dt_one"))
                dve.tensor_scalar(sm[4][g][:, 0:16], sm[3][g][:, 0:16], 1.0, TINY, ALU.subtract, ALU.max)\
                   .then_inc(sig("m_dt_den", g), 1)
                dve.wait_ge(*at(i, g, "m_dt_den"))
                dve.reciprocal(sm[5][g][:, 0:16], sm[4][g][:, 0:16]).then_inc(sig("m_dt_rec", g), 1)

            def m_dt(i, g):
                dve.wait_ge(*at(i, g, "m_dt_ln"))
                dve.wait_ge(*at(i, g, "m_dt_rec"))
                dve.scalar_tensor_tensor(sm[4][g][:, 0:16], sm[1][g][:, 0:16], TINY, sm[5][g][:, 0:16],
                                         ALU.max, ALU.mult).then_inc(sig("m_dt_ratio", g), 1)
                dve.wait_ge(*at(i, g, "m_dt_ratio"))
                dve.tensor_tensor(sm[5][g][:, 0:16], sm[4][g][:, 0:16], sm[2][g][:, 0:16], ALU.mult)\
                   .then_inc(sig("m_dt_log1p", g), 1)
                dve.wait_ge(*at(i, g, "m_dt_log1p"))
                dve.scalar_tensor_tensor(sm[3][g][:, 0:16], sm[0][g][:, 0:16], 0.0, sm[5][g][:, 0:16],
                                         ALU.max, ALU.add).then_inc(sig("m_dt_done", g), 1)
                dve.wait_ge(*at(i, g, "m_dt_done"))
                dt = sm[3][g][:, 0:16].rearrange("p (b h) -> p b h", b=GB)
                dve.tensor_tensor(sm[5][g][:, 0:16].rearrange("p (b h) -> p b h", b=GB), dt,
                                  spread(neg_a[:], 1, GB), ALU.mult).then_inc(sig("m_decay", g), 1)
                dve.tensor_scalar(sm[4][g][:, 0:16], sm[3][g][:, 0:16], 0.5, None, ALU.mult)\
                   .then_inc(sig("m_half", g), 1)

            def m_gates(i, g):
                for c in range(2):
                    dve.wait_ge(*at(i, g, f"m_tz{c}"))
                    dve.scalar_tensor_tensor(A[c][g], seqs(HFW[g][:, 3 if c == 0 else 1, :]), 1.0,
                                             seqs(bank[g][1 + c][:]), ALU.add, ALU.mult)\
                       .then_inc(sig(f"m_sz{c}", g), 1)
                dve.wait_ge(*at(i, g, "m_half"))
                dve.wait_ge(*at(i, g, "m_twice"))
                half = sm[4][g][:, 0:16].rearrange("p (b h) -> p b h", b=GB)
                for c in range(2):
                    dve.wait_ge(*at(i, g, f"m_xhr{c}"))
                    dve.tensor_tensor(A[4 + c][g].rearrange("p b (h q) -> p b h q", h=2),
                                      seqs(bank[g][3 * c][:]).rearrange("p b (h q) -> p b h q", h=2),
                                      spread(half[:, :, 2 * c:2 * c + 2], 3, PD), ALU.mult)\
                       .then_inc(sig(f"m_dtx{c}", g), 1)

            def m_mix(b):
                def step(i, g):
                    gram = seqs(HFW[g][:, 0, :])
                    dve.wait_ge(counted["m_l"][g], nth(i, g, "m_l", b))
                    if b >= 2:
                        dve.wait_ge(counted["m_yb"][g], nth(i, g, "m_yb", b - 2))
                    dve.tensor_tensor(HT[b % 2][g], HFW[g][:, 2 + b % 2, :].rearrange("p (h n) -> p h n", h=HS),
                                      spread(gram[:, b, :], 1, HS), ALU.mult).then_inc(counted["m_mix"][g], 1)
                return step

            def m_skip(half):
                def step(i, g):
                    b2 = slice(2 * half, 2 * half + 2)
                    dve.wait_ge(counted["m_yb"][g], nth(i, g, "m_yb", 2 * half + 1))
                    for c in range(2):
                        dve.scalar_tensor_tensor(A[6 + c][g][:, b2], A[2 + c][g][:, b2], a_half[:, c:c + 1],
                                                 seqs(bank[g][2 + half][:])[:, 2 * c:2 * c + 2], ALU.mult, ALU.add)\
                           .then_inc(sig(f"m_skip{half}{c}", g), 1)
                    for c in range(2):
                        dve.wait_ge(*at(i, g, f"m_skip{half}{c}"))
                        dve.tensor_tensor(A[6 + c][g][:, b2], A[6 + c][g][:, b2], A[c][g][:, b2], ALU.mult)\
                           .then_inc(sig(f"m_gate{half}{c}", g), 1)
                return step

            def c_mask(i, g):
                dve.wait_ge(ctx_in[g], i * 48 + 48)
                dve.tensor_scalar(MB[g][:], MK[g][:], MASKED, None, ALU.mult).then_inc(sig("c_mask", g), 1)

            def c_max(i, g):
                dve.wait_ge(*at(i, g, "c_scores"))
                rsum(sm[0][g][:, 0:GB], seqs(bank[g][2][:]), ALU.max, negate=True).then_inc(sig("c_max", g), 1)

            def c_rsum(i, g):
                dve.wait_ge(*at(i, g, "c_exp3"))
                dve.reciprocal(sm[2][g][:, 0:GB], sm[1][g][:, 0:GB]).then_inc(sig("c_rsum", g), 1)

            def c_pt(i, g):
                dve.wait_ge(*at(i, g, "c_pt"))
                dve.tensor_copy(A[3][g], seqs(bank[g][3][:])).then_inc(sig("c_pt_sb", g), 1)

            def c_res(i, g):
                dve.wait_ge(*at(i, g, "c_resid"))
                dve.wait_ge(*at(i, g, "c_rsum"))
                for b in range(GB):
                    if b % 2 == 0:
                        dve.wait_ge(*at(i, g, f"c_out{b // 2}"))
                    last = dve.scalar_tensor_tensor(R[g][:, b, :], bank[g][1 + b // 2][:, b * P:(b + 1) * P],
                                                    sm[2][g][:, b:b + 1], R[g][:, b, :], ALU.mult, ALU.add)
                    if b % 2:
                        last.then_inc(sig(f"n1_res{b // 2}", g), 1)

            def f_max(i, g):
                dve.wait_ge(*at(i, g, "f_g"))
                gate = gate_rows(g, 2, NE0)
                rsum(sm[0][g][:, 0:GB], gate, ALU.max).then_inc(sig("f_gmax", g), 1)
                dve.wait_ge(*at(i, g, "f_gmax"))
                dve.tensor_tensor(sm[1][g][:, 0:32].rearrange("p (b e) -> p b e", b=GB), gate,
                                  spread(sm[0][g][:, 0:GB], 2, NE0), ALU.subtract).then_inc(sig("f_gsub", g), 1)

            def f_prob(i, g):
                dve.wait_ge(*at(i, g, "f_gexp"))
                ex = sm[3][g][:, 0:32].rearrange("p (b e) -> p b e", b=GB)
                rsum(sm[4][g][:, 0:GB], ex).then_inc(sig("f_gsum", g), 1)
                dve.wait_ge(*at(i, g, "f_gsum"))
                dve.reciprocal(sm[5][g][:, 0:GB], sm[4][g][:, 0:GB]).then_inc(sig("f_grec", g), 1)
                dve.wait_ge(*at(i, g, "f_grec"))
                dve.tensor_tensor(sm[2][g][:, 0:32].rearrange("p (b e) -> p b e", b=GB), ex,
                                  spread(sm[5][g][:, 0:GB], 2, NE0), ALU.mult).then_inc(sig("f_prob", g), 1)

            def f_top(r):
                def step(i, g):
                    src, dst, k = small[r % 2][g], small[1 - r % 2][g], slice(8 * r, 8 * r + 8)
                    if r == 0:
                        dve.wait_ge(*at(i, g, "f_pt"))
                        dve.tensor_copy(src[:], bank[g][3][0:32, 0:P]).then_inc(sig("f_pt_sb", g), 1)
                        dve.wait_ge(*at(i, g, "f_pt_sb"))
                    else:
                        dve.wait_ge(*at(i, g, f"f_topw{r - 1}"))
                    apart(dve)
                    dve.max(topv[g][:, k], src[:]).then_inc(sig(f"f_topv{r}", g), 1)
                    dve.wait_ge(*at(i, g, f"f_topv{r}"))
                    apart(dve)
                    dve.max_index(topi[g][:, k], topv[g][:, k], src[:]).then_inc(sig(f"f_topi{r}", g), 1)
                    dve.match_replace(dst[:], topv[g][:, k], src[:], -1.0).then_inc(sig(f"f_topw{r}", g), 1)
                return step

            def f_index(i, g):
                dve.wait_ge(*at(i, g, f"f_topi{CAP // 8 - 1}"))
                dve.tensor_copy(small[2][g][:, 0:CAP], topi[g][:]).then_inc(sig("f_idx", g), 1)
                dve.wait_ge(*at(i, g, "f_idx"))
                for n in range(2):
                    dve.tensor_tensor(idxm[g][:, 16 * n:16 * n + 16], spread(small[2][g][:, 0:CAP], 1, 16),
                                      spread(own_col[:, 16 * n:16 * n + 16], 2, CAP), ALU.mult)\
                       .then_inc(sig(f"f_idxm{n}", g), 1)
                for n, src in ((3, small[2][g][:, 0:CAP]), (4, topv[g][:])):
                    last = dve.tensor_tensor(small[n][g][:].rearrange("p (q k) -> p q k", q=4), spread(src, 1, 4),
                                             spread(own_quarter, 2, CAP), ALU.mult)
                last.then_inc(sig("f_rowsel", g), 1)

            def f_onehot(i, g):
                for n in range(2):
                    dve.wait_ge(*at(i, g, f"f_bc{n}"))
                    last = dve.tensor_scalar(A03[g][:, n, :], bank[g][n][:], tok_id[:, 0:1], None, ALU.is_equal)
                last.then_inc(sig("f_onehot", g), 1)

            def f_rows_sb(i, g):
                dve.wait_ge(*at(i, g, "f_rows"))
                dve.tensor_copy(sm[0][g][:, 0:16], bank[g][2][:, 0:16]).then_inc(sig("f_rows_sb", g), 1)

            def f_gathered(i, g):
                dve.wait_ge(*at(i, g, "f_xi"))
                dve.tensor_copy(expert_cols(g, 0), bank_experts(g, 0)).then_inc(sig("f_xi_sb0", g), 1)

            def f_res(i, g):
                dve.wait_ge(*at(i, g, "f_add_sb"))
                for h in range(2):
                    cols = slice(2 * h * P, (2 * h + 2) * P)
                    dve.tensor_tensor(flat(R[g])[:, cols], flat(X[g])[:, cols], B16[g][:, cols], ALU.add)\
                       .then_inc(sig(f"n2_res{h}", g), 1)

            def l_kfeat(i, g):
                dve.wait_ge(*at(i, g, "l_v"))
                dve.tensor_scalar(A[5][g], A[5][g], 1.0, None, ALU.min).then_inc(sig("l_kmin", g), 1)
                dve.wait_ge(*at(i, g, "l_kmin"))
                for n in range(2):
                    kk = bank[g][2 + n][:].rearrange("p (b n) -> p b n", b=2)[:, :, 0:P]
                    last = dve.scalar_tensor_tensor(A[1][g][:, 2 * n:2 * n + 2, :], kk, 1.0,
                                                    A[5][g][:, 2 * n:2 * n + 2, :], ALU.add, ALU.max)
                last.then_inc(sig("l_kf", g), 1)

            def l_qfeat(i, g):
                dve.wait_ge(*at(i, g, "l_eq"))
                dve.tensor_scalar(A[4][g], A[4][g], 1.0, None, ALU.min).then_inc(sig("l_qmin", g), 1)
                dve.wait_ge(*at(i, g, "l_qmin"))
                dve.scalar_tensor_tensor(A[0][g], seqs(bank[g][1][:]), 1.0, A[4][g], ALU.add, ALU.max)\
                   .then_inc(sig("l_qf", g), 1)

            def l_heads(i, g):
                dve.wait_ge(*at(i, g, "l_kv"))
                for n in range(2):
                    kv = bank[g][2 + n][:].rearrange("p (b n) -> p b n", b=2)
                    last = dve.tensor_tensor(r144[g][:, 2 * n:2 * n + 2, 0:P], kv[:, :, 0:P],
                                             spread(head_mask, 1, 2), ALU.mult)
                last.then_inc(sig("l_kvm", g), 1)
                for n in range(2):
                    kv = bank[g][2 + n][:].rearrange("p (b n) -> p b n", b=2)
                    last = dve.tensor_tensor(r144[g][:, 2 * n:2 * n + 2, P:P + NH],
                                             kv[:, :, P:P + 1].broadcast_to((P, 2, NH)),
                                             spread(head_cols, 1, 2), ALU.mult)
                last.then_inc(sig("l_zm", g), 1)

            def l_div(i, g):
                dve.wait_ge(*at(i, g, "l_num"))
                den = sm[0][g][:].rearrange("p (b h) -> p b h", b=GB)
                for n in range(2):
                    kv = bank[g][n][:].rearrange("p (b n) -> p b n", b=2)
                    last = dve.tensor_scalar(den[:, 2 * n:2 * n + 2, :], kv[:, :, P:P + NH], DEN_EPS, None, ALU.add)
                last.then_inc(sig("l_den", g), 1)
                dve.wait_ge(*at(i, g, "l_den"))
                dve.reciprocal(sm[1][g][:], sm[0][g][:]).then_inc(sig("l_rec", g), 1)
                dve.wait_ge(*at(i, g, "l_rec"))
                rec = sm[1][g][:].rearrange("p (b h) -> p b h", b=GB)
                for n in range(2):
                    kv = bank[g][n][:].rearrange("p (b n) -> p b n", b=2)
                    last = dve.tensor_tensor(
                        A[2][g][:, 2 * n:2 * n + 2, :].rearrange("p b (h q) -> p b h q", h=NH),
                        kv[:, :, 0:P].rearrange("p b (h q) -> p b h q", h=NH),
                        spread(rec[:, 2 * n:2 * n + 2, :], 3, HD), ALU.mult)
                last.then_inc(sig("l_att", g), 1)

            def x_v(i, g):
                dve.wait_ge(*at(i, g, "x_v1"))
                dve.wait_ge(*at(i, g, "x_zero"))
                for c in range(4):
                    spot = VM[g][:, :, c::4, HD * c:HD * c + HD]
                    last = dve.tensor_tensor(
                        spot, bank[g][1][:].rearrange("p (b m c q) -> p b m c q", b=GB, m=4, c=4)[:, :, :, c],
                        spread(row["xbv"].rearrange("p (m c q) -> p m c q", m=4, c=4)[:, :, c], 1, GB), ALU.add)
                last.then_inc(sig("x_v_sb", g), 1)

            def x_kparts(i, g):
                split(i, g, "k", 3, A[1], A[2])

            def split(i, g, side, n, full, rest):
                dve.wait_ge(*at(i, g, f"x_{side}_h"))
                dve.tensor_tensor(flat(rest[g]), flat(full[g]), PARTS[n][g], ALU.subtract)\
                   .then_inc(sig(f"x_{side}_r1", g), 1)
                dve.wait_ge(*at(i, g, f"x_{side}_r1"))
                dve.tensor_copy(PARTS[n + 1][g], flat(rest[g])).then_inc(sig(f"x_{side}_m", g), 1)
                dve.wait_ge(*at(i, g, f"x_{side}_m"))
                dve.tensor_tensor(PARTS[n + 2][g], flat(rest[g]), PARTS[n + 1][g], ALU.subtract)\
                   .then_inc(sig(f"x_{side}_l", g), 1)

            def x_qparts(i, g):
                split(i, g, "q", 0, A[0], A[3])

            def x_max(b):
                def step(i, g):
                    for c in range(4):
                        n = 4 * b + c
                        dve.wait_ge(counted["x_a"][g], nth(i, g, "x_a", n))
                        rsum(sm[0][g][:, b * NH + 4 * c:b * NH + 4 * c + 4], seqs(bank[g][n % 4][:]), ALU.max,
                             negate=True).then_inc(counted["x_amax"][g], 1)
                return step

            def x_shift(i, g):
                dve.wait_ge(*at(i, g, "x_nmt"))
                dve.tensor_copy(nmp[0][g][:], bank[g][0][0:NH, :]).then_inc(sig("x_nm_h", g), 1)
                dve.wait_ge(*at(i, g, "x_nm_h"))
                dve.tensor_tensor(nmp[1][g][:], bank[g][0][0:NH, :], nmp[0][g][:], ALU.subtract)\
                   .then_inc(sig("x_nm_l", g), 1)

            def x_div(b):
                def step(i, g):
                    dve.wait_ge(counted["x_pv"][g], nth(i, g, "x_pv", 4 * b + 3))
                    dve.reciprocal(A[2][g][:, b, :], bank[g][2 + b % 2][:, P:2 * P]).then_inc(sig(f"x_rden{b}", g), 1)
                    dve.wait_ge(*at(i, g, f"x_rden{b}"))
                    dve.tensor_tensor(A[3][g][:, b, :], bank[g][2 + b % 2][:, 0:P], A[2][g][:, b, :], ALU.mult)\
                       .then_inc(sig(f"x_att{b}", g), 1)
                return step

            def e_rank(i, g):
                dve.wait_ge(*at(i, g, "e_g"))
                dve.tensor_copy(sm[0][g][:, 0:24].rearrange("p (b e) -> p b e", b=GB), gate_rows(g, 2, NE1))\
                   .then_inc(sig("e_g_sb", g), 1)
                dve.wait_ge(*at(i, g, "e_g_sb"))
                lg = sm[0][g][:, 0:24].rearrange("p (b e) -> p b e", b=GB)
                above = HFW[g][:, 0, 0:144].rearrange("p (b e j) -> p b e j", b=GB, e=NE1)
                equal = HFW[g][:, 1, 0:144].rearrange("p (b e j) -> p b e j", b=GB, e=NE1)
                mine, other = spread(lg, 3, NE1), spread(lg, 2, NE1)
                dve.tensor_tensor(above, other, mine, ALU.is_gt).then_inc(sig("e_above", g), 1)
                dve.tensor_tensor(equal, other, mine, ALU.is_equal).then_inc(sig("e_equal", g), 1)
                dve.wait_ge(*at(i, g, "e_equal"))
                dve.tensor_tensor(equal, equal, spread(before, 1, GB), ALU.mult).then_inc(sig("e_tied", g), 1)
                dve.wait_ge(*at(i, g, "e_tied"))
                dve.tensor_tensor(above, above, equal, ALU.add).then_inc(sig("e_rank1", g), 1)
                dve.wait_ge(*at(i, g, "e_rank1"))
                rank = sm[1][g][:, 0:24].rearrange("p (b e) -> p b e", b=GB)
                rsum(rank, above).then_inc(sig("e_rank", g), 1)
                dve.wait_ge(*at(i, g, "e_rank"))
                dve.tensor_scalar(sm[2][g][:, 0:24], sm[1][g][:, 0:24], 2.0, None, ALU.is_lt)\
                   .then_inc(sig("e_sel", g), 1)
                rsum(sm[3][g][:, 0:GB], lg, ALU.max).then_inc(sig("e_max", g), 1)
                dve.wait_ge(*at(i, g, "e_max"))
                dve.tensor_tensor(sm[4][g][:, 0:24].rearrange("p (b e) -> p b e", b=GB), lg,
                                  spread(sm[3][g][:, 0:GB], 2, NE1), ALU.subtract).then_inc(sig("e_sub", g), 1)

            def e_comb(i, g):
                dve.wait_ge(*at(i, g, "e_exp"))
                dve.tensor_tensor(sm[1][g][:, 0:24], sm[5][g][:, 0:24], sm[2][g][:, 0:24], ALU.mult)\
                   .then_inc(sig("e_msel", g), 1)
                dve.wait_ge(*at(i, g, "e_msel"))
                ex = sm[1][g][:, 0:24].rearrange("p (b e) -> p b e", b=GB)
                rsum(sm[3][g][:, 0:GB], ex).then_inc(sig("e_sum", g), 1)
                dve.wait_ge(*at(i, g, "e_sum"))
                dve.reciprocal(sm[4][g][:, 0:GB], sm[3][g][:, 0:GB]).then_inc(sig("e_rec", g), 1)
                dve.wait_ge(*at(i, g, "e_rec"))
                dve.tensor_tensor(sm[6][g][:, 0:24].rearrange("p (b e) -> p b e", b=GB), ex,
                                  spread(sm[4][g][:, 0:GB], 2, NE1), ALU.mult).then_inc(sig("e_comb", g), 1)

            def e_acc0(i, g):
                dve.wait_ge(*at(i, g, "e_b21"))
                dve.tensor_tensor(flat(R[g]), bank[g][3][:], flat(X[g]), ALU.add).then_inc(sig("e_acc0", g), 1)

            def e_acc(e):
                def step(i, g):
                    dve.wait_ge(counted["e_down"][g], nth(i, g, "e_down", e))
                    if e:
                        dve.wait_ge(counted["e_acc"][g], nth(i, g, "e_acc", e - 1))
                    else:
                        dve.wait_ge(*at(i, g, "e_acc0"))
                    for b in range(GB):
                        last = dve.scalar_tensor_tensor(
                            R[g][:, b, :], bank[g][2 + e % 2][:, b * P:(b + 1) * P],
                            sm[6][g][:, b * NE1 + e:b * NE1 + e + 1], R[g][:, b, :], ALU.mult, ALU.add)
                        if e == NE1 - 1 and b % 2:
                            last.then_inc(sig(f"n5_res{b // 2}", g), 1)
                    if e < NE1 - 1:
                        last.then_inc(counted["e_acc"][g], 1)
                return step

            run(dve, [
                (3, m_stats), (3, m_norm), (5.557, m_conv), (8.275, m_silu), (9.449, m_gram), (9.449, m_dt_rows),
                (12.176, m_dt_one), (18.49, m_dt), (19.175, m_gates), (22.577, m_mix(0)), (23.828, m_mix(1)),
                (26.387, m_mix(2)), (26.976, m_skip(0)), (28.508, m_mix(3)), (33.472, m_skip(1)),
                (35.937, res(0, (0, 1), "m_out", "m_twice", 0.5)), (36.721, norm_stats(0)), (40.17, norm_rows(0)),
                (44.491, c_mask), (49.958, c_max), (54.587, c_rsum), (54.587, c_pt), (60.257, c_res),
                (61.469, norm_stats(1)), (64.063, norm_rows(1)), (64.473, f_max), (64.473, f_prob),
                (69.451, f_top(0)), (69.451, f_top(1)), (69.451, f_top(2)), (69.451, f_top(3)), (70.951, f_index),
                (74.56, f_onehot), (76.183, f_gathered), (81.105, f_rows_sb), (96.643, f_res),
                (97.523, norm_stats(2)), (100.389, norm_rows(2)), (105.981, l_kfeat), (106.832, l_qfeat),
                (106.832, l_heads), (108.475, l_div), (112.486, res(3, (3, 2), "l_out", "l_resid")),
                (114.486, norm_stats(3)), (115.237, x_v), (116.133, x_kparts), (117.663, norm_rows(3)),
                (126.954, x_qparts), (140.729, x_max(0)), (141.429, x_max(1)), (150.119, x_max(2)),
                (150.119, x_max(3)), (154.924, x_shift), (169.168, x_div(0)), (173.002, x_div(1)),
                (176.486, x_div(2)), (177.986, x_div(3)), (180.976, res(4, (0, 1), "x_out", "x_resid")),
                (180.976, norm_stats(4)), (183.686, norm_rows(4)), (189.449, e_rank), (191.058, e_comb),
                (199.169, e_acc0), (199.923, e_acc(0)), (205.921, e_acc(1)), (205.921, e_acc(2)),
                (205.921, e_acc(3)), (209.262, e_acc(4)), (209.262, e_acc(5)), (209.962, norm_stats(5)),
                (211.711, norm_rows(5)),
            ])

        @block.scalar
        def _(act):
            act.wait_ge(*loaded("mamba"))
            act.activation(neg_a_exp[:], row["A_log"], ACT.Exp).then_inc(scaled, 1)
            act.wait_ge(constants, N_CONSTANTS)

            def move(dst, k, step, produced, bias=None, scale=1.0, rows=P, cols=W):
                def run(i, g):
                    act.wait_ge(*at(i, g, produced))
                    kw = {} if bias is None else {"bias": bias}
                    act.activation(dst(g), bank[g][k][0:rows, 0:cols], ACT.Identity if bias is not None else ACT.Copy,
                                   scale=scale, **kw).then_inc(sig(step, g), 1)
                return run

            def m_xt(i, g):
                act.wait_ge(*at(i, g, "m_xt"))
                act.activation(flat(T[g]), bank[g][0][:], ACT.Copy, scale=col["normw"])\
                   .then_inc(sig("m_xt_sb", g), 1)

            def m_tanh(i, g):
                for c in range(2):
                    act.wait_ge(*at(i, g, f"m_tap{c}3"))
                    act.activation(HFW[g][:, 1 + c, :], A47[g][:, 2 + c, :], ACT.Tanh, scale=0.5)\
                       .then_inc(sig(f"m_tanh{c}", g), 1)

            def m_dt_exp(i, g):
                act.wait_ge(*at(i, g, "m_dt_abs"))
                act.activation(sm[2][g][:, 0:16], sm[1][g][:, 0:16], ACT.Exp, scale=-1.0)\
                   .then_inc(sig("m_dt_exp", g), 1)

            def m_dt_ln(i, g):
                act.wait_ge(*at(i, g, "m_dt_one"))
                act.activation(sm[1][g][:, 0:16], sm[3][g][:, 0:16], ACT.Ln).then_inc(sig("m_dt_ln", g), 1)

            def m_tz(i, g):
                for c in range(2):
                    act.wait_ge(*at(i, g, f"m_z{c}"))
                    act.activation(HFW[g][:, 3 if c == 0 else 1, :], bank[g][1 + c][:], ACT.Tanh, scale=0.5)\
                       .then_inc(sig(f"m_tz{c}", g), 1)

            def m_l(b):
                def step(i, g):
                    act.wait_ge(counted["m_seg"][g], nth(i, g, "m_seg", b))
                    if b >= 2:
                        act.wait_ge(counted["m_mix"][g], nth(i, g, "m_mix", b - 2))
                    act.activation(HFW[g][:, 2 + b % 2, :], bank[g][b % 2][:], ACT.Exp).then_inc(counted["m_l"][g], 1)
                return step

            def c_exp(i, g):
                act.wait_ge(*at(i, g, "c_max"))
                for b in range(GB):
                    act.activation(A[2][g][:, b, :], bank[g][2][:, b * P:(b + 1) * P], ACT.Exp,
                                   bias=sm[0][g][:, b:b + 1], accum_out=sm[1][g][:, b:b + 1])\
                       .then_inc(sig(f"c_exp{b}", g), 1)

            def f_gexp(i, g):
                act.wait_ge(*at(i, g, "f_gsub"))
                act.activation(sm[3][g][:, 0:32], sm[1][g][:, 0:32], ACT.Exp).then_inc(sig("f_gexp", g), 1)

            def f_gathered(i, g):
                act.wait_ge(*at(i, g, "f_xi"))
                act.activation(expert_cols(g, 1), bank_experts(g, 1), ACT.Copy).then_inc(sig("f_xi_sb1", g), 1)

            def f_gelu(e):
                def step(i, g):
                    act.wait_ge(counted["f_up"][g], nth(i, g, "f_up", e))
                    act.activation(HTW[g][:, e % 2, :], bank[g][e % 2][:], ACT.Gelu_apprx_tanh)\
                       .then_inc(counted["f_act"][g], 1)
                return step

            def l_kexp(i, g):
                for n in range(2):
                    act.wait_ge(*at(i, g, f"l_kv{n}"))
                    kv = bank[g][2 + n][:].rearrange("p (b n) -> p b n", b=2)
                    last = act.activation(A[5][g][:, 2 * n:2 * n + 2, :], kv[:, :, 0:P], ACT.Exp)
                last.then_inc(sig("l_ek", g), 1)
                act.wait_ge(*at(i, g, "f_add"))
                for n in range(2):
                    kv = bank[g][2 + n][:].rearrange("p (b n) -> p b n", b=2)
                    act.activation(vx[g][:, 2 * n:2 * n + 2, 0:P], kv[:, :, P:2 * P], ACT.Copy)
                act.activation(vx[g][:, :, P:P + 1], spread(ones[:], 1, GB), ACT.Copy).then_inc(sig("l_v", g), 1)

            def l_qexp(i, g):
                act.wait_ge(*at(i, g, "l_q"))
                act.activation(A47[g][:, 0, :], bank[g][1][:], ACT.Exp).then_inc(sig("l_eq", g), 1)

            def f_y(half):
                def step(i, g):
                    act.wait_ge(counted["f_down"][g], nth(i, g, "f_down", 4 * half + 3))
                    act.activation(A03[g][:, 2 + half, :], bank[g][2 + half][:], ACT.Copy)\
                       .then_inc(sig(f"f_y_sb{half}", g), 1)
                return step

            def x_k(i, g):
                move(lambda g: A03[g][:, 1, :], 0, "x_k_sb", "x_k", col["xbk1"])(i, g)
                act.wait_ge(*at(i, g, "x_k_sb"))
                act.activation(PARTS[3][g], A03[g][:, 1, :], ACT.Copy).then_inc(sig("x_k_h", g), 1)

            def x_q(i, g):
                move(lambda g: A03[g][:, 0, :], 3, "x_q_sb", "x_q", wq_scaled_bias[:, 0:1], HD ** -0.5)(i, g)
                act.wait_ge(*at(i, g, "x_q_sb"))
                act.activation(PARTS[0][g], A03[g][:, 0, :], ACT.Copy).then_inc(sig("x_q_h", g), 1)

            def x_p(n):
                def step(i, g):
                    act.wait_ge(counted["x_b"][g], nth(i, g, "x_b", n))
                    if n >= 2:
                        act.wait_ge(counted["x_pv"][g], nth(i, g, "x_pv", n - 2))
                    act.activation(PTW[g][:, n % 2, :], bank[g][n % 2][:], ACT.Exp).then_inc(counted["x_p"][g], 1)
                return step

            def e_exp(i, g):
                act.wait_ge(*at(i, g, "e_sub"))
                act.activation(sm[5][g][:, 0:24], sm[4][g][:, 0:24], ACT.Exp).then_inc(sig("e_exp", g), 1)

            def e_gelu(n):
                e, f = n // FT1, n % FT1

                def step(i, g):
                    act.wait_ge(counted["e_up"][g], nth(i, g, "e_up", n))
                    if e >= 2:
                        act.wait_ge(counted["e_down"][g], nth(i, g, "e_down", e - 2))
                    act.activation(HFW[g][:, 2 * (e % 2) + f, :], bank[g][n % 2][:], ACT.Gelu,
                                   bias=col["b1"][:, n:n + 1]).then_inc(counted["e_act"][g], 1)
                return step

            def tile_of(n):
                return lambda g: A03[g][:, n, :] if n < 4 else A47[g][:, n - 4, :]

            t_of = lambda g: flat(T[g])
            gT_of = lambda g: gT[g]
            run(act, [
                (3.261, m_xt), (5.461, move(tile_of(0), 3, "m_b_sb", "m_b")),
                (7.12, move(tile_of(1), 0, "m_c_sb", "m_c")),
                (9.923, move(gT_of, 3, "m_dtt_sb", "m_dtt", col["dtb"], cols=P)), (13.373, m_tanh),
                (15.712, m_dt_exp), (16.51, m_dt_ln), (16.51, m_tz), (22.43, m_l(0)), (28.625, m_l(1)),
                (28.625, m_l(2)), (30.594, m_l(3)), (40.446, move(tile_of(0), 3, "c_kt_sb", "c_kt", col["xbk0"])),
                (43.663, move(t_of, 0, "c_xt_sb", "c_xt")),
                (47.384, move(tile_of(1), 1, "c_q_sb", "c_q", col["xbq0"])), (50.23, c_exp),
                (54.877, move(tile_of(4), 0, "c_ot_sb", "c_ot")), (62.178, move(t_of, 0, "f_xt_sb", "f_xt")),
                (62.28, move(gT_of, 1, "f_gt_sb", "f_gt", cols=P)), (64.733, f_gexp), (75.959, f_gathered),
                (79.298, f_gelu(0)), (82.298, f_gelu(1)), (82.298, f_gelu(2)), (82.298, f_gelu(3)),
                (82.298, f_gelu(4)), (83.68, f_y(0)), (83.68, f_gelu(5)), (83.68, f_gelu(6)), (83.68, f_gelu(7)),
                (87.247, f_y(1)), (96.937, move(lambda g: B16[g][:], 0, "f_add_sb", "f_add")),
                (104.602, move(t_of, 0, "l_xt_sb", "l_xt")), (105.682, l_kexp), (106.508, l_qexp),
                (113.832, move(tile_of(3), 2, "l_at_sb", "l_at")), (117.104, x_k),
                (125.994, move(t_of, 2, "x_xt_sb", "x_xt")), (125.994, x_q), (160.722, x_p(0)), (160.722, x_p(1)),
                (160.722, x_p(2)), (160.722, x_p(3)), (160.722, x_p(4)), (160.722, x_p(5)), (160.722, x_p(6)),
                (161.31, x_p(7)), (163.658, x_p(8)), (168.893, x_p(9)), (169.761, x_p(10)), (171.261, x_p(11)),
                (171.261, x_p(12)), (171.961, x_p(13)), (172.311, x_p(14)), (173.011, x_p(15)),
                (181.395, move(t_of, 0, "e_xt_sb", "e_xt")),
                (184.107, move(gT_of, 1, "e_gt_sb", "e_gt", col["bg"], cols=P)), (189.31, e_exp),
                (193.882, e_gelu(0)), (193.882, e_gelu(1)),
                (195.326, move(lambda g: cT[g], 2, "e_ct_sb", "e_ct", rows=NE1)), (197.369, e_gelu(2)),
                (198.149, e_gelu(3)), (198.79, e_gelu(4)), (198.79, e_gelu(5)), (199.472, e_gelu(6)),
                (199.539, e_gelu(7)), (207.35, e_gelu(8)), (207.35, e_gelu(9)), (211.713, e_gelu(10)),
                (211.713, e_gelu(11)),
            ])

        @block.gpsimd
        def _(pool):
            for g in range(1, LANES):
                set_stacks(pool, g)
            for g in range(LANES):
                pool.memset(spare[:, g:g + 1], 0.0).then_inc(lane_free[g], 16)

            pool.wait_ge(*loaded("mamba"))
            pool.wait_ge(constants, N_CONSTANTS)

            def rstd(name, produced):
                def step(i, g):
                    pool.wait_ge(*at(i, g, produced))
                    pool.tensor_tensor(sm[6][g][:, 0:GB], sm[7][g][:, 0:GB], neg_half[:], ALU.pow)\
                        .then_inc(sig(name, g), 1)
                return step

            def m_twice(i, g):
                pool.wait_ge(*at(i, g, "m_xt_sb"))
                apart(pool)
                pool.tensor_scalar(flat(R[g]), flat(A[4][g]), 2.0, 0.0, ALU.mult, ALU.add)\
                    .then_inc(sig("m_twice", g), 1)

            def m_rd(b):
                def step(i, g):
                    if b < 2:
                        pool.wait_ge(*at(i, g, "m_decay"))
                    else:
                        pool.wait_ge(counted["m_seg"][g], nth(i, g, "m_seg", b - 2))
                    apart(pool)
                    for h in range(HS):
                        last = pool.tensor_scalar(PT[b % 2][g][:, h, :], tri,
                                                  sm[5][g][:, b * HS + h:b * HS + h + 1], 0.0, ALU.mult, ALU.add)
                    last.then_inc(counted["m_rd"][g], 1)
                return step

            def resid(name, ready, bias):
                def step(i, g):
                    pool.wait_ge(*at(i, g, ready))
                    pool.tensor_tensor(R[g][:], X[g][:], spread(row[bias], 1, GB), ALU.add)\
                        .then_inc(sig(name, g), 1)
                return step

            def f_scat(i, g):
                pool.wait_ge(*at(i, g, "f_rows_sb"))
                apart(pool)
                for b in range(GB):
                    for h in range(2):
                        n = 2 * b + h
                        last = pool.tensor_scalar(HFW[g][:, h, b * P:(b + 1) * P], tok_row, sm[0][g][:, n:n + 1],
                                                  sm[0][g][:, 8 + n:9 + n], ALU.is_equal, ALU.mult)
                last.then_inc(sig("f_scat", g), 1)

            def x_zero(i, g):
                pool.wait_ge(*at(i, g, "l_qf"))
                apart(pool)
                pool.memset(A47[g][:].rearrange("p b n -> p (b n)"), 0.0).then_inc(sig("x_zero", g), 1)

            run(pool, [
                (-4.686, rstd("m_rstd", "m_ms")), (9.984, m_twice), (24.384, m_rd(0)), (24.384, m_rd(1)),
                (24.384, m_rd(2)), (36.226, m_rd(3)), (45.679, rstd("n0_rstd", "n0_eps")),
                (56.63, resid("c_resid", "n0_row3", "xbo0")), (63.916, rstd("n1_rstd", "n1_eps")), (81.401, f_scat),
                (88.598, rstd("n2_rstd", "n2_eps")), (96.826, resid("l_resid", "n2_row3", "lbo")),
                (100.804, x_zero), (104.767, rstd("n3_rstd", "n3_eps")),
                (118.641, resid("x_resid", "n3_row3", "xbo1")), (128.081, rstd("n4_rstd", "n4_eps")),
                (202.771, rstd("n5_rstd", "n5_eps")),
            ])



def kernel(**a):
    import concourse.bacc as bacc
    from concourse.bass_utils import run_bass_kernel_spmd

    f = {k: np.asarray(v) for k, v in a.items()}
    col = lambda v: v.reshape(-1, 1)
    rows = lambda v, n: v.reshape(n, P, -1).transpose(1, 0, 2)
    padded = lambda v: np.pad(v, ((0, 0), (0, 32 - v.shape[1])))
    gate_bias = lambda v: np.tile(padded(v.reshape(1, -1)), (GB, 1)).reshape(P, 1)
    order = np.array([HD * (4 * (pos % 4) + pos // 4) + d for d in range(HD) for pos in range(NH)])
    conv = rows(f["L0_attn_conv_w"], 2)
    columns = {
        "normw": col(f["L0_attn_norm_w"]), "D2": np.repeat(f["L0_attn_D"], PD).reshape(2, P).T,
        "convw0": conv[:, 0], "convw1": conv[:, 1], "convb": f["L0_attn_conv_b"].reshape(2, P).T,
        "dtb": gate_bias(f["L0_attn_dt_bias"]), "xbq0": col(f["L0_xattn_bq"]), "xbk0": col(f["L0_xattn_bk"]),
        "xbq1": col(f["L1_xattn_bq"][order]), "xbk1": col(f["L1_xattn_bk"][order]), "bg": gate_bias(f["L1_ffn_bg"]),
        "b1": f["L1_ffn_b1"].reshape(NE1 * FT1, P).T,
    }
    short_rows = {"A_log": f["L0_attn_A_log"], "xbo0": f["L0_xattn_bo"], "lbo": f["L1_attn_b_out"],
                  "xbv": f["L1_xattn_bv"], "xbo1": f["L1_xattn_bo"]}
    n, c = np.arange(P)[:, None], np.arange(P)[None, :]
    be, eb, bh = np.arange(P)[:, None], np.arange(32)[None, :], np.arange(2 * GB)[None, :]
    shapes = {
        "ident": n == c, "tri": n <= c, "strict": n > c, "head_mask": n // HD == c // HD,
        "head_cols": n // HD == c[:, :NH], "ones_of_head": (c % 32) // HD == c // 32 + 0 * n, "tok_id": n,
        "tok_row": c + 0 * n, "own_col": (be // NE0 == eb % GB) & (be % NE0 == eb // GB),
        "own_quarter": be % 4 == c[:, :4], "own_row": (be // NE0 == bh // 2) & (be % NE0 // 4 == bh % 2),
        "before": c[:, :NE1 * NE1] % NE1 < c[:, :NE1 * NE1] // NE1 + 0 * n,
    }
    w = {
        "shapes": np.concatenate([shapes[name].astype(np.float32) for name in SHAPES], 1),
        "columns": np.concatenate([columns[name] for name in COLUMNS], 1),
        "rows": np.concatenate([short_rows[name] for name in ROWS]),
        "inT": f["L0_attn_in_proj_w"].T[:, :6 * P], "dtT": padded(f["L0_attn_in_proj_w"].T[:, 6 * P:]),
        "outT": rows(f["L0_attn_out_proj_w"].T, 2),
        "wq0": f["L0_xattn_Wq"].T, "wk0": f["L0_xattn_Wk"].T, "wo0": f["L0_xattn_Wo"].T,
        "gate": padded(f["L0_ffn_gate_w"]), "w1": f["L0_ffn_w1"].transpose(1, 0, 2),
        "w2": f["L0_ffn_w2"].reshape(NE0, FT0, P, P).transpose(2, 0, 1, 3),
        "lqkv": f["L1_attn_W_qkv"], "lout": f["L1_attn_W_out"],
        "wq1": f["L1_xattn_Wq"][order].T, "wk1": f["L1_xattn_Wk"][order].T,
        "wv1": f["L1_xattn_Wv"].T, "wo1": f["L1_xattn_Wo"].T,
        "wg": padded(f["L1_ffn_Wg"]), "b2": f["L1_ffn_b2"], "we1": f["L1_ffn_W1"].transpose(1, 0, 2),
        "we2": f["L1_ffn_W2"].reshape(NE1, FT1, P, P).transpose(2, 0, 1, 3),
    }
    x, ctx = f["x"], f["ctx_1024"]
    nb = x.shape[0]
    arrays = {
        "in_x": x.transpose(1, 0, 2).reshape(P, nb * P), "in_ctx": ctx.transpose(1, 0, 2).reshape(P, nb * P),
        "in_ctxT": ctx.transpose(2, 0, 1).reshape(P, nb * P),
        "in_mask": f["mask_BxS2_bk0"].reshape(1, nb * P),
    }
    arrays.update({"in_w_" + k: v for k, v in w.items()})
    arrays = {k: np.ascontiguousarray(v) for k, v in arrays.items()}
    nc = bacc.Bacc("TRN2", target_bir_lowering=False, num_devices=1)
    t = {k: nc.dram_tensor(k, v.shape, mybir.dt.from_np(v.dtype), kind="ExternalInput").ap() for k, v in arrays.items()}
    out = nc.dram_tensor("out", (P, nb * P), F32, kind="ExternalOutput").ap()
    decoder(nc, t["in_x"], t["in_ctx"], t["in_ctxT"], t["in_mask"], {k: t["in_w_" + k] for k in w}, out)
    r = run_bass_kernel_spmd(nc, [arrays], core_ids=[0])
    y = r.results[0]["out"]
    return y.reshape(P, nb, P).transpose(1, 0, 2)
```
